# Optimizing a Trainium2 kernel written in Bass

```python
import numpy as np
import jax
import jax.numpy as jnp

def _softmax(x, axis=-1):
    return jax.nn.softmax(x, axis=axis)

def _gelu(x):
    return jax.nn.gelu(x, approximate=True)

def _silu(x):
    return jax.nn.silu(x)

def _sigmoid(x):
    return jax.nn.sigmoid(x)

def _layernorm(x, axis=-1, eps=1e-05):
    m = jnp.mean(x, axis=axis, keepdims=True)
    v = jnp.var(x, axis=axis, keepdims=True)
    return (x - m) / jnp.sqrt(v + eps)

def _scatter_add(tgt, idx, src, axis=0):
    return tgt.at[idx].add(src)

def _segment_sum(src, seg, n):
    return jax.ops.segment_sum(src, seg, n)
kernel_name = 'mk_gnn_preln_d4_gnn_r32_426ea2'

def setup_inputs(seed: int=0):
    np.random.seed(seed)
    _w = jnp.asarray

    def _rec_inputs():
        import jax
        import jax.numpy as jnp
        _gk = jax.random.key(seed)
        x = -0.000202 + 1 * jax.random.normal(jax.random.fold_in(_gk, 1), (3125, 128), jnp.float32)
        src = jax.random.randint(jax.random.fold_in(_gk, 2), (50000,), 0, 3125, jnp.int32)
        dst = jnp.minimum((3125 * jax.random.uniform(jax.random.fold_in(_gk, 3), (50000,)) ** 2.0).astype(jnp.int32), 99999)
        _o = jnp.argsort(dst, stable=True)
        src = src[_o]
        dst = dst[_o]
        edge_attr_64 = 0.000189758 + 1.00013 * jax.random.normal(jax.random.fold_in(_gk, 12), (50000, 64), jnp.float32)
        return (x, src, dst, edge_attr_64)
    x, src, dst, edge_attr_64 = _rec_inputs()

    def _L0_gnn_setup():
        import jax, jax.numpy as jnp
        import numpy as np
        N_NODES = 50000
        N_EDGES = 25000
        D = 128
        key = jax.random.key(seed)
        k1, k2, k3, k4 = jax.random.split(key, 4)
        features = jax.random.normal(k1, (N_NODES, D), dtype=jnp.float32)
        W = jax.random.normal(k2, (D, D), dtype=jnp.float32) * 0.05
        b = jnp.zeros((D,), dtype=jnp.float32)
        gamma = jnp.ones((D,), dtype=jnp.float32)
        beta = jnp.zeros((D,), dtype=jnp.float32)
        edge_src = jax.random.randint(k3, (N_EDGES,), 0, N_NODES, dtype=jnp.int32)
        edge_dst = jax.random.randint(k4, (N_EDGES,), 0, N_NODES, dtype=jnp.int32)
        return {'features': features, 'W': W, 'b': b, 'gamma': gamma, 'beta': beta, 'edge_src': edge_src, 'edge_dst': edge_dst}
    _L0_gnn_all = _L0_gnn_setup()
    _L0_gnn_in = {k: v for k, v in _L0_gnn_all.items() if k in ('W', 'b', 'gamma', 'beta')}
    del _L0_gnn_all

    def _L1_gnn_setup():
        import jax, jax.numpy as jnp
        import numpy as np
        N, E, D, H, ED = (50000, 25000, 128, 8, 64)
        C = D // H

        def _ln(x, g, b, eps=1e-05):
            m = jnp.mean(x, axis=-1, keepdims=True)
            v = jnp.var(x, axis=-1, keepdims=True)
            return (x - m) * jax.lax.rsqrt(v + eps) * g + b
        key = jax.random.key(seed)
        ks = jax.random.split(key, 16)
        p = lambda k, shape: jax.random.normal(k, shape, dtype=jnp.float32) * 0.05
        return {'x': jax.random.normal(ks[0], (N, D), dtype=jnp.float32), 'edge_index': jax.random.randint(ks[1], (2, E), 0, N, dtype=jnp.int64), 'edge_attr': jax.random.normal(ks[2], (E, ED), dtype=jnp.float32), 'Wq': p(ks[3], (D, D)), 'bq': jnp.zeros((D,), jnp.float32), 'Wk': p(ks[4], (D, D)), 'bk': jnp.zeros((D,), jnp.float32), 'Wv': p(ks[5], (D, D)), 'bv': jnp.zeros((D,), jnp.float32), 'We': p(ks[6], (ED, D)), 'Wskip': p(ks[7], (D, D)), 'bskip': jnp.zeros((D,), jnp.float32), 'g1': jnp.ones((D,), jnp.float32), 'b1': jnp.zeros((D,), jnp.float32), 'g2': jnp.ones((D,), jnp.float32), 'b2': jnp.zeros((D,), jnp.float32), 'Wf1': p(ks[8], (D, 4 * D)), 'bf1': jnp.zeros((4 * D,), jnp.float32), 'Wf2': p(ks[9], (4 * D, D)), 'bf2': jnp.zeros((D,), jnp.float32)}
    _L1_gnn_all = _L1_gnn_setup()
    _L1_gnn_in = {k: v for k, v in _L1_gnn_all.items() if k in ('Wq', 'bq', 'Wk', 'bk', 'Wv', 'bv', 'We', 'Wskip', 'bskip', 'g1', 'b1', 'g2', 'b2', 'Wf1', 'bf1', 'Wf2', 'bf2')}
    del _L1_gnn_all

    def _L2_gnn_setup():
        import jax, jax.numpy as jnp
        import numpy as np
        N, E, D, H1, H2 = (50000, 25000, 128, 3, 1)
        NEG_SLOPE = 0.2

        def gat_conv(h, src, dst, fc_w, attn_l, attn_r, res_w, bias, heads, out_dim):
            n = h.shape[0]
            feat = (h @ fc_w.T).reshape(n, heads, out_dim)
            el = jnp.einsum('nhd,hd->nh', feat, attn_l)
            er = jnp.einsum('nhd,hd->nh', feat, attn_r)
            e = el[src] + er[dst]
            e = jax.nn.leaky_relu(e, NEG_SLOPE)
            m = jax.ops.segment_max(e, dst, num_segments=n)
            ex = jnp.exp(e - m[dst])
            s = jax.ops.segment_sum(ex, dst, num_segments=n)
            alpha = ex / s[dst]
            msg = alpha[:, :, None] * feat[src]
            out = jax.ops.segment_sum(msg, dst, num_segments=n)
            out = out + (h @ res_w.T).reshape(n, heads, out_dim)
            out = out + bias[None, :, :]
            return out
        key = jax.random.key(seed)
        ks = jax.random.split(key, 16)
        inp = {'node_feats': jax.random.normal(ks[0], (N, D), dtype=jnp.float32), 'src': jax.random.randint(ks[1], (E,), 0, N, dtype=jnp.int64), 'dst': jax.random.randint(ks[2], (E,), 0, N, dtype=jnp.int64), 'fc1_w': jax.random.normal(ks[3], (H1 * D, D), dtype=jnp.float32) * 0.05, 'attn_l1': jax.random.normal(ks[4], (H1, D), dtype=jnp.float32) * 0.05, 'attn_r1': jax.random.normal(ks[5], (H1, D), dtype=jnp.float32) * 0.05, 'res1_w': jax.random.normal(ks[6], (H1 * D, D), dtype=jnp.float32) * 0.05, 'bias1': jnp.zeros((H1, D), dtype=jnp.float32), 'fc2_w': jax.random.normal(ks[7], (H2 * D, H1 * D), dtype=jnp.float32) * 0.05, 'attn_l2': jax.random.normal(ks[8], (H2, D), dtype=jnp.float32) * 0.05, 'attn_r2': jax.random.normal(ks[9], (H2, D), dtype=jnp.float32) * 0.05, 'res2_w': jax.random.normal(ks[10], (H2 * D, H1 * D), dtype=jnp.float32) * 0.05, 'bias2': jnp.zeros((H2, D), dtype=jnp.float32)}
        return inp
    _L2_gnn_all = _L2_gnn_setup()
    _L2_gnn_in = {k: v for k, v in _L2_gnn_all.items() if k in ('fc1_w', 'attn_l1', 'attn_r1', 'res1_w', 'bias1', 'fc2_w', 'attn_l2', 'attn_r2', 'res2_w', 'bias2')}
    del _L2_gnn_all

    def _L3_gnn_setup():
        import jax, jax.numpy as jnp
        import numpy as np
        N, E, D = (50000, 25000, 128)
        BN_EPS = 1e-05

        def _sage_conv(x, src, dst, Wl, Wr, b):
            n = x.shape[0]
            msg = x[src]
            agg = jax.ops.segment_sum(msg, dst, num_segments=n)
            cnt = jax.ops.segment_sum(jnp.ones((src.shape[0],), x.dtype), dst, num_segments=n)
            agg = agg / jnp.maximum(cnt, 1.0)[:, None]
            return agg @ Wl.T + x @ Wr.T + b

        def _bn_eval(x, gamma, beta, rmean, rvar):
            return (x - rmean) * (gamma / jnp.sqrt(rvar + BN_EPS)) + beta
        key = jax.random.key(seed)
        ks = jax.random.split(key, 12)
        s = 1.0 / np.sqrt(D)
        inp = {'x': jax.random.normal(ks[0], (N, D), jnp.float32), 'edge_index': jax.random.randint(ks[1], (2, E), 0, N, jnp.int32), 'Wl0': jax.random.normal(ks[2], (D, D), jnp.float32) * s, 'Wr0': jax.random.normal(ks[3], (D, D), jnp.float32) * s, 'b0': jnp.zeros((D,), jnp.float32), 'g0': jnp.ones((D,), jnp.float32), 'be0': jnp.zeros((D,), jnp.float32), 'rm0': jax.random.normal(ks[4], (D,), jnp.float32) * 0.1, 'rv0': jax.random.uniform(ks[5], (D,), jnp.float32, 0.5, 1.5), 'Wl1': jax.random.normal(ks[6], (D, D), jnp.float32) * s, 'Wr1': jax.random.normal(ks[7], (D, D), jnp.float32) * s, 'b1': jnp.zeros((D,), jnp.float32), 'g1': jnp.ones((D,), jnp.float32), 'be1': jnp.zeros((D,), jnp.float32), 'rm1': jax.random.normal(ks[8], (D,), jnp.float32) * 0.1, 'rv1': jax.random.uniform(ks[9], (D,), jnp.float32, 0.5, 1.5)}
        return inp
    _L3_gnn_all = _L3_gnn_setup()
    _L3_gnn_in = {k: v for k, v in _L3_gnn_all.items() if k in ('Wl0', 'Wr0', 'b0', 'g0', 'be0', 'rm0', 'rv0', 'Wl1', 'Wr1', 'b1', 'g1', 'be1', 'rm1', 'rv1')}
    del _L3_gnn_all
    return {'x': x, 'src': src, 'dst': dst, 'edge_attr_64': edge_attr_64, 'L0_gnn_W': _L0_gnn_in['W'], 'L0_gnn_b': _L0_gnn_in['b'], 'L0_gnn_gamma': _L0_gnn_in['gamma'], 'L0_gnn_beta': _L0_gnn_in['beta'], 'L1_gnn_Wq': _L1_gnn_in['Wq'], 'L1_gnn_bq': _L1_gnn_in['bq'], 'L1_gnn_Wk': _L1_gnn_in['Wk'], 'L1_gnn_bk': _L1_gnn_in['bk'], 'L1_gnn_Wv': _L1_gnn_in['Wv'], 'L1_gnn_bv': _L1_gnn_in['bv'], 'L1_gnn_We': _L1_gnn_in['We'], 'L1_gnn_Wskip': _L1_gnn_in['Wskip'], 'L1_gnn_bskip': _L1_gnn_in['bskip'], 'L1_gnn_g1': _L1_gnn_in['g1'], 'L1_gnn_b1': _L1_gnn_in['b1'], 'L1_gnn_g2': _L1_gnn_in['g2'], 'L1_gnn_b2': _L1_gnn_in['b2'], 'L1_gnn_Wf1': _L1_gnn_in['Wf1'], 'L1_gnn_bf1': _L1_gnn_in['bf1'], 'L1_gnn_Wf2': _L1_gnn_in['Wf2'], 'L1_gnn_bf2': _L1_gnn_in['bf2'], 'L2_gnn_fc1_w': _L2_gnn_in['fc1_w'], 'L2_gnn_attn_l1': _L2_gnn_in['attn_l1'], 'L2_gnn_attn_r1': _L2_gnn_in['attn_r1'], 'L2_gnn_res1_w': _L2_gnn_in['res1_w'], 'L2_gnn_bias1': _L2_gnn_in['bias1'], 'L2_gnn_fc2_w': _L2_gnn_in['fc2_w'], 'L2_gnn_attn_l2': _L2_gnn_in['attn_l2'], 'L2_gnn_attn_r2': _L2_gnn_in['attn_r2'], 'L2_gnn_res2_w': _L2_gnn_in['res2_w'], 'L2_gnn_bias2': _L2_gnn_in['bias2'], 'L3_gnn_Wl0': _L3_gnn_in['Wl0'], 'L3_gnn_Wr0': _L3_gnn_in['Wr0'], 'L3_gnn_b0': _L3_gnn_in['b0'], 'L3_gnn_g0': _L3_gnn_in['g0'], 'L3_gnn_be0': _L3_gnn_in['be0'], 'L3_gnn_rm0': _L3_gnn_in['rm0'], 'L3_gnn_rv0': _L3_gnn_in['rv0'], 'L3_gnn_Wl1': _L3_gnn_in['Wl1'], 'L3_gnn_Wr1': _L3_gnn_in['Wr1'], 'L3_gnn_b1': _L3_gnn_in['b1'], 'L3_gnn_g1': _L3_gnn_in['g1'], 'L3_gnn_be1': _L3_gnn_in['be1'], 'L3_gnn_rm1': _L3_gnn_in['rm1'], 'L3_gnn_rv1': _L3_gnn_in['rv1']}

def reference(x, src, dst, edge_attr_64, L0_gnn_W, L0_gnn_b, L0_gnn_gamma, L0_gnn_beta, L1_gnn_Wq, L1_gnn_bq, L1_gnn_Wk, L1_gnn_bk, L1_gnn_Wv, L1_gnn_bv, L1_gnn_We, L1_gnn_Wskip, L1_gnn_bskip, L1_gnn_g1, L1_gnn_b1, L1_gnn_g2, L1_gnn_b2, L1_gnn_Wf1, L1_gnn_bf1, L1_gnn_Wf2, L1_gnn_bf2, L2_gnn_fc1_w, L2_gnn_attn_l1, L2_gnn_attn_r1, L2_gnn_res1_w, L2_gnn_bias1, L2_gnn_fc2_w, L2_gnn_attn_l2, L2_gnn_attn_r2, L2_gnn_res2_w, L2_gnn_bias2, L3_gnn_Wl0, L3_gnn_Wr0, L3_gnn_b0, L3_gnn_g0, L3_gnn_be0, L3_gnn_rm0, L3_gnn_rv0, L3_gnn_Wl1, L3_gnn_Wr1, L3_gnn_b1, L3_gnn_g1, L3_gnn_be1, L3_gnn_rm1, L3_gnn_rv1):
    import jax
    import jax.numpy as jnp

    def _L0_gnn_ref(features, W, b, gamma, beta, edge_src, edge_dst):
        import jax, jax.numpy as jnp
        import numpy as np
        N_NODES = 50000
        N_EDGES = 25000
        D = 128
        N = features.shape[0]
        ones_e = jnp.ones(edge_src.shape[0], dtype=features.dtype)
        deg_out = jax.ops.segment_sum(ones_e, edge_src, num_segments=N)
        deg_in = jax.ops.segment_sum(ones_e, edge_dst, num_segments=N)
        norm_out = jax.lax.rsqrt(jnp.maximum(deg_out, 1.0))
        norm_in = jax.lax.rsqrt(jnp.maximum(deg_in, 1.0))
        h = features * norm_out[:, None]
        h = h @ W
        agg = jax.ops.segment_sum(h[edge_src], edge_dst, num_segments=N)
        gcn_out = agg * norm_in[:, None] + b
        mu = jnp.mean(gcn_out, axis=-1, keepdims=True)
        var = jnp.mean(jnp.square(gcn_out - mu), axis=-1, keepdims=True)
        normed = (gcn_out - mu) * jax.lax.rsqrt(var + 1e-05) * gamma + beta
        out = jax.nn.relu(normed)
        return out + features

    def _L1_gnn_ref(x, edge_index, edge_attr, Wq, bq, Wk, bk, Wv, bv, We, Wskip, bskip, g1, b1, g2, b2, Wf1, bf1, Wf2, bf2):
        import jax, jax.numpy as jnp
        import numpy as np
        N, E, D, H, ED = (50000, 25000, 128, 8, 64)
        C = D // H

        def _ln(x, g, b, eps=1e-05):
            m = jnp.mean(x, axis=-1, keepdims=True)
            v = jnp.var(x, axis=-1, keepdims=True)
            return (x - m) * jax.lax.rsqrt(v + eps) * g + b
        n = x.shape[0]
        src, dst = (edge_index[0], edge_index[1])
        q = (x @ Wq + bq).reshape(n, H, C)
        k = (x @ Wk + bk).reshape(n, H, C)
        v = (x @ Wv + bv).reshape(n, H, C)
        e = (edge_attr @ We).reshape(-1, H, C)
        k_j = k[src] + e
        v_j = v[src] + e
        logits = jnp.sum(q[dst] * k_j, axis=-1) / np.sqrt(C)
        m = jax.ops.segment_max(logits, dst, num_segments=n)
        ex = jnp.exp(logits - m[dst])
        denom = jax.ops.segment_sum(ex, dst, num_segments=n)
        alpha = ex / denom[dst]
        agg = jax.ops.segment_sum(alpha[..., None] * v_j, dst, num_segments=n)
        conv = agg.reshape(n, D) + x @ Wskip + bskip
        h = _ln(conv + x, g1, b1)
        ffn = jax.nn.gelu(h @ Wf1 + bf1, approximate=False) @ Wf2 + bf2
        return _ln(ffn + h, g2, b2)

    def _L2_gnn_ref(node_feats, src, dst, fc1_w, attn_l1, attn_r1, res1_w, bias1, fc2_w, attn_l2, attn_r2, res2_w, bias2):
        import jax, jax.numpy as jnp
        import numpy as np
        N, E, D, H1, H2 = (50000, 25000, 128, 3, 1)
        NEG_SLOPE = 0.2

        def gat_conv(h, src, dst, fc_w, attn_l, attn_r, res_w, bias, heads, out_dim):
            n = h.shape[0]
            feat = (h @ fc_w.T).reshape(n, heads, out_dim)
            el = jnp.einsum('nhd,hd->nh', feat, attn_l)
            er = jnp.einsum('nhd,hd->nh', feat, attn_r)
            e = el[src] + er[dst]
            e = jax.nn.leaky_relu(e, NEG_SLOPE)
            m = jax.ops.segment_max(e, dst, num_segments=n)
            ex = jnp.exp(e - m[dst])
            s = jax.ops.segment_sum(ex, dst, num_segments=n)
            alpha = ex / s[dst]
            msg = alpha[:, :, None] * feat[src]
            out = jax.ops.segment_sum(msg, dst, num_segments=n)
            out = out + (h @ res_w.T).reshape(n, heads, out_dim)
            out = out + bias[None, :, :]
            return out
        x = gat_conv(node_feats, src, dst, fc1_w, attn_l1, attn_r1, res1_w, bias1, H1, D)
        x = jax.nn.elu(x).reshape(x.shape[0], -1)
        x = gat_conv(x, src, dst, fc2_w, attn_l2, attn_r2, res2_w, bias2, H2, D)
        return x.reshape(x.shape[0], -1)

    def _L3_gnn_ref(x, edge_index, Wl0, Wr0, b0, g0, be0, rm0, rv0, Wl1, Wr1, b1, g1, be1, rm1, rv1):
        import jax, jax.numpy as jnp
        import numpy as np
        N, E, D = (50000, 25000, 128)
        BN_EPS = 1e-05

        def _sage_conv(x, src, dst, Wl, Wr, b):
            n = x.shape[0]
            msg = x[src]
            agg = jax.ops.segment_sum(msg, dst, num_segments=n)
            cnt = jax.ops.segment_sum(jnp.ones((src.shape[0],), x.dtype), dst, num_segments=n)
            agg = agg / jnp.maximum(cnt, 1.0)[:, None]
            return agg @ Wl.T + x @ Wr.T + b

        def _bn_eval(x, gamma, beta, rmean, rvar):
            return (x - rmean) * (gamma / jnp.sqrt(rvar + BN_EPS)) + beta
        src, dst = (edge_index[0], edge_index[1])
        h = _sage_conv(x, src, dst, Wl0, Wr0, b0)
        h = jax.nn.relu(_bn_eval(h, g0, be0, rm0, rv0))
        h = _sage_conv(h, src, dst, Wl1, Wr1, b1)
        return _bn_eval(h, g1, be1, rm1, rv1)
    edge_index = jnp.stack([src, dst])
    h = jnp.maximum(_layernorm(x, axis=-1), 0.0)
    x = x + _L0_gnn_ref(h, L0_gnn_W, L0_gnn_b, L0_gnn_gamma, L0_gnn_beta, src, dst)
    h = jnp.maximum(_layernorm(x, axis=-1), 0.0)
    x = x + _L1_gnn_ref(h, edge_index, edge_attr_64, L1_gnn_Wq, L1_gnn_bq, L1_gnn_Wk, L1_gnn_bk, L1_gnn_Wv, L1_gnn_bv, L1_gnn_We, L1_gnn_Wskip, L1_gnn_bskip, L1_gnn_g1, L1_gnn_b1, L1_gnn_g2, L1_gnn_b2, L1_gnn_Wf1, L1_gnn_bf1, L1_gnn_Wf2, L1_gnn_bf2)
    h = jnp.maximum(_layernorm(x, axis=-1), 0.0)
    x = x + _L2_gnn_ref(h, src, dst, L2_gnn_fc1_w, L2_gnn_attn_l1, L2_gnn_attn_r1, L2_gnn_res1_w, L2_gnn_bias1, L2_gnn_fc2_w, L2_gnn_attn_l2, L2_gnn_attn_r2, L2_gnn_res2_w, L2_gnn_bias2)
    h = jnp.maximum(_layernorm(x, axis=-1), 0.0)
    x = x + _L3_gnn_ref(h, edge_index, L3_gnn_Wl0, L3_gnn_Wr0, L3_gnn_b0, L3_gnn_g0, L3_gnn_be0, L3_gnn_rm0, L3_gnn_rv0, L3_gnn_Wl1, L3_gnn_Wr1, L3_gnn_b1, L3_gnn_g1, L3_gnn_be1, L3_gnn_rm1, L3_gnn_rv1)
    return x

_drawn_inputs = setup_inputs


def setup_inputs(seed=0):
    import zlib

    import numpy as np

    out = dict(_drawn_inputs(seed))
    spreads = {'L0_gnn_b': (0.0, 0.1),
     'L0_gnn_gamma': (1.0, 0.2),
     'L0_gnn_beta': (0.0, 0.1),
     'L1_gnn_bq': (0.0, 0.8),
     'L1_gnn_bk': (0.0, 2.0),
     'L1_gnn_bv': (0.0, 0.1),
     'L1_gnn_bskip': (0.0, 0.1),
     'L1_gnn_g1': (1.0, 0.2),
     'L1_gnn_b1': (0.0, 0.1),
     'L1_gnn_g2': (1.0, 0.2),
     'L1_gnn_b2': (0.0, 0.1),
     'L1_gnn_bf1': (0.0, 0.341),
     'L1_gnn_bf2': (0.0, 0.1),
     'L2_gnn_bias1': (0.0, 0.1),
     'L2_gnn_bias2': (0.0, 0.1),
     'L3_gnn_b0': (0.0, 0.1),
     'L3_gnn_g0': (1.0, 0.2),
     'L3_gnn_be0': (0.0, 0.1),
     'L3_gnn_b1': (0.0, 0.1),
     'L3_gnn_g1': (1.0, 0.2),
     'L3_gnn_be1': (0.0, 0.1)}
    factors = {'L1_gnn_Wq': 3.011,
     'L1_gnn_Wk': 5.108,
     'L2_gnn_attn_l1': 8.0,
     'L2_gnn_attn_r1': 25.953,
     'L2_gnn_attn_l2': 8.0,
     'L2_gnn_attn_r2': 25.305}
    for name, (base, spread) in spreads.items():
        noise = np.random.default_rng([zlib.crc32(name.encode()), seed]).standard_normal(out[name].shape)
        drawn = base * np.exp(spread * noise) if base else spread * noise
        out[name] = jnp.asarray(drawn.astype(out[name].dtype))
    for name, factor in factors.items():
        out[name] = (out[name] * factor).astype(out[name].dtype)
    return out
```

```python
from contextlib import ExitStack

import concourse.bass as bass
import numpy as np
from concourse import mybir

F32 = mybir.dt.float32
BF16 = mybir.dt.bfloat16
I32 = mybir.dt.int32
ALU = mybir.AluOpType
ACT = mybir.ActivationFunctionType
AX_X = mybir.AxisListType.X

P = 128
N, E, D, ED = 3125, 50000, 128, 64
NT = -(-N // P)
NP = NT * P
JT = 5
NJ = NT // JT
GC = 4
NG = -(-E // (P * GC))
CH = NG * GC
EP = CH * P
QA = 4
CQ = CH // QA
H1, C1 = 8, 16
H2 = 3
FF = 4 * D
BIG = 1.0e30
EPS = 1e-5
BANK = 512
UNROLL = 4
PASSES = ("gcn", "attn", "gat1", "gat2", "sage1", "sage2")
WEIGHTED = {"attn": (H1, C1, 0.25), "gat1": (H2, D, 1.0), "gat2": (1, D, 1.0)}
assert NT % JT == 0 and NG % 2 == 0 and CH % QA == 0 and CQ <= P


def width(name):
    return WEIGHTED[name][0] * (WEIGHTED[name][1] + 1) if name in WEIGHTED else D


class GroupSignal:

    def __init__(self, sem, passes):
        self.sem = sem
        self.base = {p: NG * i for i, p in enumerate(passes)}

    def at(self, p, q, r, back=0):
        return self.base[p] + 4 * q + (r - back + 1)


class RingSignal:

    def __init__(self, sems, passes, dmas=1):
        self.sems, self.ring, self.each = sems, len(sems), 16 * dmas
        self.base, self.total = {}, [0] * len(sems)
        for p in passes:
            self.base[p] = list(self.total)
            for g in range(NG):
                self.total[g % self.ring] += self.each

    def of(self, r):
        return self.sems[r % self.ring]

    def at(self, p, q, r, before=0):
        use = q * (UNROLL // self.ring) + (r // self.ring + 1 - before)
        return use * self.each + self.base[p][r % self.ring]


def past(q, r, n):
    return not isinstance(q, int) or 4 * q + r >= n


class Steps:

    def __init__(self, names, base, turns=1):
        assert len(set(names)) == len(names), names
        self.base, self.n = base, len(names)
        self.index = {name: i for i, name in enumerate(names)}
        self.end = base + turns * self.n

    def at(self, name, turn=0):
        return self.base + self.index[name] + turn * self.n


def over_groups(eng, stages):
    last = max(lag for lag, _ in stages)

    def peeled(n):
        for lag, what in stages:
            if 0 <= n - lag < NG:
                what((n - lag) // UNROLL, (n - lag) % UNROLL)

    for n in range(2 * UNROLL):
        peeled(n)
    with eng.Fori(2, NG // UNROLL) as i:
        for r in range(UNROLL):
            for lag, what in stages:
                what(i + (r - lag) // UNROLL, (r - lag) % UNROLL)
    for n in range(NG // UNROLL * UNROLL, NG + last):
        peeled(n)


LN = ("mean", "neg", "cent", "sq", "var", "vare", "sd", "rs")


def ln(pre):
    return [pre + s for s in LN]


def gnn_stack_kernel(nc, out, x, src, dst, edge_attr_64, **w):
    ctx = ExitStack()
    with ctx:
        def sb(name, shape, dt=F32):
            return ctx.enter_context(nc.sbuf_tensor(name, shape, dt))

        def sem(name):
            return ctx.enter_context(nc.semaphore(name))

        def hbm(name, shape, dt=F32):
            return nc.dram_tensor(name, shape, dt, kind="Internal").ap()

        esrc = hbm("esrc", [EP], I32)
        edst = hbm("edst", [P + EP], I32)
        eattr = hbm("eattr", [EP, ED])
        breaks = hbm("breaks", [EP + P])
        same_hbm = hbm("same_hbm", [NG, P, GC * P], BF16)
        q_tab = hbm("q_tab", [NP, D])
        row_tab = {"gcn": hbm("t_gcn", [NP, 3 * D], BF16), "attn": hbm("t_attn", [NP, 2 * D]),
                   "gat1": hbm("t_gat1", [NP, D + H2]), "gat2": hbm("t_gat2", [NP, D + 1]),
                   "sage1": hbm("t_sage1", [NP, 3 * D], BF16), "sage2": hbm("t_sage2", [NP, 3 * D], BF16)}
        er_tab = {"gat1": hbm("er_gat1", [NP, H2]), "gat2": hbm("er_gat2", [NP, 2])}
        ends = {p: hbm(f"ends_{p}", [EP + P, width(p)]) for p in PASSES}
        carry = {p: hbm(f"carry_{p}", [CH + P, width(p)]) for p in PASSES}

        ident = sb("ident", [P, P])
        flip = sb("flip", [P, P])
        ones = sb("ones", [P, P])
        upper = sb("upper", [P, P])
        iota_row = sb("iota_row", [P, P])
        iota_i = sb("iota_i", [P, P], I32)
        dst_f = sb("dst_f", [P, CH])
        src_i = sb("src_i", [P, CH], I32)
        dst_i = sb("dst_i", [P, CH], I32)
        last_dst = sb("last_dst", [CQ, QA])
        carries = sb("carries", [CQ, QA, CH])
        spread = sb("spread", [H1, H1, CQ])
        deg = sb("deg", [P, 2, NT])
        norm = sb("norm", [P, 2, NT])
        cnt_r = sb("cnt_r", [P, NT])
        tot = sb("tot", [P, NT])
        tot_x = sb("tot_x", [P, NT])
        cum = sb("cum", [P, NT])
        ntmp = sb("ntmp", [P, 6, NT])
        ntmp_i = sb("ntmp_i", [P, 3, NT], I32)
        end_i = sb("end_i", [P, NT], I32)
        carry_i = sb("carry_i", [P, NT], I32)
        zrow = sb("zrow", [P, 390])
        pad_i = sb("pad_i", [P, 4], I32)

        def row_of(key, n=D):
            return sb("r_" + key, [P, n])
        rows = {k: row_of(k) for k in ("L0_gnn_b", "L0_gnn_gamma", "L0_gnn_beta", "L1_gnn_bskip", "L1_gnn_g1",
                                       "L1_gnn_b1", "L1_gnn_g2", "L1_gnn_b2", "L1_gnn_bf2", "L2_gnn_bias2",
                                       "L3_gnn_b0", "L3_gnn_g0", "L3_gnn_be0", "L3_gnn_rm0", "L3_gnn_rv0",
                                       "L3_gnn_b1", "L3_gnn_g1", "L3_gnn_be1", "L3_gnn_rm1", "L3_gnn_rv1")}
        b_qkv = row_of("b_qkv", 3 * D)
        bias1 = row_of("bias1", H2 * D)
        w0 = sb("w0", [P, D])
        w_qkv = sb("w_qkv", [P, 3 * D])
        w_skip = sb("w_skip", [P, D])
        w_e = sb("w_e", [ED, D])
        w_f1 = sb("w_f1", [P, FF])
        b_f1 = sb("b_f1", [P, FF // P])
        w_f2 = sb("w_f2", [P, FF // P, D])
        a1 = sb("a1", [P, 2, H2])
        a2 = sb("a2", [P, 2])
        fc1_t = sb("fc1_t", [P, H2, D])
        res1_t = sb("res1_t", [P, H2, D])
        u1 = sb("u1", [P, 2, H2])
        w2 = sb("w2", [P, H2, 2 * D + 2])
        sage_t = sb("sage_t", [P, 4, D])
        bn_a = sb("bn_a", [P, 2, D])
        bn_b = sb("bn_b", [P, 2, D])

        x_sb = sb("x_sb", [P, NT, D])
        h_sb = sb("h_sb", [P, NT, D])
        y = sb("y", [P, JT, D])
        sq = sb("sq", [P, JT, D])
        hs = sb("hs", [P, JT, D])
        st = sb("st", [P, 5, JT])
        rec = sb("rec", [P, 2, JT * H1])
        er_n = sb("er_n", [P, JT, H2])
        er_2 = sb("er_2", [P, JT, 2])

        src_ix = sb("src_ix", [P, UNROLL, GC], I32)
        dst_ix = sb("dst_ix", [P, UNROLL, GC], I32)
        def carve(t, items, start=0):
            at, got = start, {}
            for k, (parts, dims, dt) in items.items():
                n = int(np.prod(dims)) * (2 if dt == BF16 else 4) // 4
                v = t[0:parts, at:at + n]
                v = v if dt == F32 else v.bitcast(dt)
                letters = "abcd"[:len(dims)]
                got[k] = v.rearrange(f"p ({' '.join(letters)}) -> p {' '.join(letters)}", **dict(zip(letters, dims)))
                at += n
            return got

        agg = sb("agg", [P, GC * D * (2 * UNROLL + UNROLL + 2) + 2 * GC * H2 * (D + 1)])
        early = carve(agg, {"row_b": (P, (UNROLL, GC, 2 * D), F32), "q_b": (P, (UNROLL, GC, D), F32),
                            "msg": (P, (2, GC * H2 * (D + 1)), F32), "diag": (P, (2, GC, P), F32)})
        row_b, q_b, msg, diag = (early[k] for k in ("row_b", "q_b", "msg", "diag"))
        row_s = carve(agg, {"row_s": (P, (UNROLL, GC * 4 * D), BF16)})["row_s"]
        prep = carve(agg, {k: (CQ, (QA, P), dt) for k, dt in (("src_r", I32), ("dst_r", I32), ("prev_r", I32),
                                                              ("src_rf", F32), ("dst_rf", F32), ("brk_r", F32))}
                     | {"after": (CQ, (CH,), F32), "after_i": (CQ, (CH,), I32), "part_i": (P, (CH,), I32),
                        "lo_f": (P, (2, CH), F32), "hi_f": (P, (2, CH), F32), "raw": (P, (16, D), F32),
                        "hot_lo": (P, (2, UNROLL, P), BF16), "hot_hi": (P, (2, UNROLL, NT), BF16)})
        src_r, dst_r, prev_r, src_rf, dst_rf, brk_r = (prep[k] for k in ("src_r", "dst_r", "prev_r", "src_rf", "dst_rf", "brk_r"))
        after, after_i, part_i, lo_f, hi_f = (prep[k] for k in ("after", "after_i", "part_i", "lo_f", "hi_f"))
        raw, hot_lo, hot_hi = (prep[k] for k in ("raw", "hot_lo", "hot_hi"))
        at_b = sb("at_b", [P, UNROLL, GC, ED])
        brk_b = sb("brk_b", [H1, UNROLL, GC * P + 1])
        same_b = sb("same_b", [P, UNROLL, GC, P], BF16)
        prod = sb("prod", [P, GC, D])
        z_b = sb("z_b", [P, GC, H2])
        logit = sb("logit", [P, 2, GC * H1])
        fwd = sb("fwd", [H1, 2, GC * P])
        mx = sb("mx", [H1, 2, GC * P])
        dif = sb("dif", [P, 2, GC * H1])
        wgt = sb("wgt", [P, 2, GC * H1])
        first_m = sb("first_m", [H1, CH])
        last_m = sb("last_m", [H1, CH])
        last_c = sb("last_c", [CQ, QA, H1])

        scratch = sb("scratch", [P, JT * (2 * H2 * D + P + 3 * D) + FF * JT + JT * 3 * D // 2])
        node = carve(scratch, {
            "a_n": (P, (JT, H2 * D), F32), "a_t": (P, (JT * H2 * P,), F32), "h_t": (P, (JT * P,), F32),
            "hid": (P, (FF // P, JT * P), F32), "tab": (P, (JT, 3 * D), F32), "tab_b": (P, (JT, 3, D), BF16)})
        a_n, a_t, h_t, hid, tab, tab_b = (node[k] for k in ("a_n", "a_t", "h_t", "hid", "tab", "tab_b"))
        sb_at = [0]

        def edge_part(parts, *dims):
            n = int(np.prod(dims))
            v = scratch[0:parts, sb_at[0]:sb_at[0] + n]
            sb_at[0] += n
            letters = "abcd"[:len(dims)]
            return v.rearrange(f"p ({' '.join(letters)}) -> p {' '.join(letters)}", **dict(zip(letters, dims)))

        o_b = edge_part(P, 2, GC * H2 * (D + 1))
        same_f = edge_part(P, 2, GC, P)
        at_t = edge_part(ED, 2, GC * P)
        gw = edge_part(CQ, QA, CH)
        z_rows = edge_part(CQ, QA, H2 * (D + 1))
        r_rows = edge_part(CQ, QA, H2 * (D + 1))

        ps = ctx.enter_context(nc.psum_tensor("ps", [P, 8 * BANK], F32))

        def bank(b, n=1):
            return ps[:, b * BANK:(b + n) * BANK]

        s_setup = sem("s_setup")
        s_load = sem("s_load")
        s_store = sem("s_store")
        s_steps = sem("s_steps")
        s_hot = sem("s_hot")
        s_hist = sem("s_hist")
        wp = tuple(WEIGHTED)
        rows_in = RingSignal([sem(f"rows_in{i}") for i in range(4)], PASSES, GC)
        dst_rows_in = RingSignal([sem(f"dst_rows_in{i}") for i in range(4)], wp, GC)
        attr_in = RingSignal([sem(f"attr_in{i}") for i in range(4)], ("attn",))
        brk_in = RingSignal([sem(f"brk_in{i}") for i in range(4)], wp)
        same_in = RingSignal([sem(f"same_in{i}") for i in range(4)], PASSES[1:])
        same_out = RingSignal([sem(f"same_out{i}") for i in range(4)], ("gcn",))
        ends_out = RingSignal([sem(f"ends_out{i}") for i in range(2)], PASSES)
        ix_done = GroupSignal(sem("ix_done"), PASSES)
        diag_done = GroupSignal(sem("diag_done"), ("gcn",))
        bcast_done = GroupSignal(sem("bcast_done"), ("gcn",))
        same_done = GroupSignal(sem("same_done"), ("gcn",))
        attr_t_done = GroupSignal(sem("attr_t_done"), ("attn",))
        attr_sb_done = GroupSignal(sem("attr_sb_done"), ("attn",))
        e_done = GroupSignal(sem("e_done"), ("attn",))
        kve_done = GroupSignal(sem("kve_done"), ("attn",))
        prod_done = GroupSignal(sem("prod_done"), wp)
        logit_done = GroupSignal(sem("logit_done"), wp)
        logit_t_done = GroupSignal(sem("logit_t_done"), wp)
        fwd_done = GroupSignal(sem("fwd_done"), wp)
        max_done = GroupSignal(sem("max_done"), wp)
        max_t_done = GroupSignal(sem("max_t_done"), wp)
        kept_done = GroupSignal(sem("kept_done"), wp)
        dif_done = GroupSignal(sem("dif_done"), wp)
        exp_done = GroupSignal(sem("exp_done"), wp)
        msg_done = GroupSignal(sem("msg_done"), wp)
        same_f_done = GroupSignal(sem("same_f_done"), wp)
        sum_done = GroupSignal(sem("sum_done"), PASSES)
        evac_done = GroupSignal(sem("evac_done"), PASSES)
        s_seed = sem("s_seed")
        s_gather = sem("s_gather")
        s_agg = sem("s_agg")

        chains = {}
        total = [0]

        def chain(key, names, turns=1):
            chains[key] = Steps(names, total[0], turns)
            total[0] = chains[key].end

        wt = [f"wt{i}" for i in range(16)]
        chain("prep", ["consts", "pads", "pads_out", "flip", "edges_in", "cast", "brk", "brk2", "brk_out",
                       "cols", "cols_i", "bits", "bits_f"])
        chain("hist", ["hist_start", "hist_read", "deg_max", "deg_sqrt", "deg_norm", "cnt_r", "cum_ps", "tot_sb", "tot_scan",
                       "tot_ex", "cum", "nz", "end", "end_ii", "end_xor", "end_f", "end_m", "end_i",
                       "blk_i", "blk_f", "start", "inner", "blk_m", "blk_n", "carry_i",
                       "bnd_ps", "last_sb", "after_f", "carries", "carries2", "spread",
                       "wt_ps", "wt_sb", "bn_var", "bn_sd", "bn_rs", "bn_a", "bn_b1", "bn_b2", "bn_b3"])
        chain("n0", ["xl"] + ln("a") + ["hs", "hkeep", "hn", "hi", "r1", "mid", "r2", "lo", "store"], NJ)
        for p in PASSES:
            heads = [[f"{s}{h}" for s in ("fb", "d")] + [f"{s}{h}_{t}" for s in ("e", "g") for t in range(QA)] + [f"r{h}"]
                     for h in range(WEIGHTED[p][0])] if p in WEIGHTED else [["r"]]
            pre = ["lc_ps", "lc_sb"] if p in WEIGHTED else []
            chain("x_" + p, ["z_in"] + pre + sum(heads, []) + ["r_sb", "r_out", "agg_ok"])
            chain("n_" + p, {
                "gcn": ["an", "T", "Ts", "lin", "y"] + ln("a") + ["an2", "ag", "ab", "ar", "ax", "xk"] + ln("b")
                       + ["hs", "hkeep", "T2", "T2s", "qkv", "tab", "store"],
                "attn": ["den", "rec", "an", "hl", "T", "Ts", "lin", "y", "y2", "y3"] + ln("a") + ["an2", "ag", "ab", "T2", "T2s",
                        "ffn1"] + [f"gelu{o}" for o in range(4)] + ["ffn2", "z", "z2"] + ln("b") + ["bn2", "bg", "bb", "bx", "xk"]
                        + ln("c") + ["hs", "hkeep", "T3", "T3s", "el", "tab", "el_s", "er_s", "store"],
                "gat1": ["den", "rec", "an", "hl", "T", "Ts", "T1s", "lin", "z", "min", "exp", "elu", "elu2", "T2", "T2s",
                         "feat", "tab", "er_s", "res", "store"],
                "gat2": ["den", "rec", "an", "y", "y2", "yx", "xk"] + ln("a") + ["hs", "hkeep", "hi", "r1", "mid", "r2", "lo", "store"],
                "sage1": ["an", "hl", "T", "Ts", "T1s", "lin", "ya", "yb", "hs", "hkeep", "hi", "r1", "mid", "r2", "lo", "store"],
                "sage2": ["an", "hl", "T", "Ts", "T1s", "lin", "ya", "yb", "yx"],
            }[p], NJ)

        s_apart_act, s_apart_dve, s_apart_pool, s_apart_sp = (sem(f"s_apart_{e}") for e in ("act", "dve", "pool", "sp"))

        def apart(eng, own):
            eng.sem_inc(own, 1)

        block = ctx.enter_context(nc.Block())

        def bc(ap, shape):
            return ap.to_broadcast(shape)

        def tiles(ap, j):
            return ap[:, bass.ds(j * JT, JT), :] if not isinstance(j, int) else ap[:, j * JT:(j + 1) * JT, :]

        def chunk_rows(ap, q, r):
            v = ap.rearrange("(q r k p) c -> q r k p c", r=2, k=GC, p=P)
            return v

        def agg_of(p):
            return agg[:, 0:NT * width(p)].rearrange("p (t c) -> p t c", t=NT)

        def grp(ap, q, r):
            g = q * UNROLL + r
            return ap[bass.ds(g, 1)] if not isinstance(g, int) else ap[g:g + 1]

        @block.sync
        def _(sp):
            loads = [0]

            def load(dst_ap, src_ap):
                sp.dma_start(dst_ap, src_ap).then_inc(s_load, 16)
                loads[0] += 16

            def landed():
                sp.wait_ge(s_load, loads[0])

            c = chains["prep"]
            for k, t in rows.items():
                if k != "L2_gnn_bias2":
                    load(t[:, :], w[k].rearrange("(a n) -> a n", a=1).to_broadcast([P, D]))
            for i, k in enumerate(("bq", "bk", "bv")):
                load(b_qkv[:, i * D:(i + 1) * D], w[f"L1_gnn_{k}"].rearrange("(a n) -> a n", a=1).to_broadcast([P, D]))
            load(bias1[:, :], w["L2_gnn_bias1"].rearrange("(a h) n -> a (h n)", a=1).to_broadcast([P, H2 * D]))
            load(rows["L2_gnn_bias2"][:, :], w["L2_gnn_bias2"].to_broadcast([P, D]))
            load(w0[:, :], w["L0_gnn_W"])
            for i, k in enumerate(("Wq", "Wk", "Wv")):
                load(w_qkv[:, i * D:(i + 1) * D], w[f"L1_gnn_{k}"])
            load(w_skip[:, :], w["L1_gnn_Wskip"])
            load(w_e[:, :], w["L1_gnn_We"])
            load(w_f1[:, :], w["L1_gnn_Wf1"])
            with nc.allow_non_contiguous_dma(reason="bias as columns"):
                load(b_f1[:, :], w["L1_gnn_bf1"].rearrange("(o p) -> p o", p=P))
            load(w_f2[:, :, :], w["L1_gnn_Wf2"].rearrange("(o p) n -> p o n", p=P))
            load(raw[:, 0:3, :], w["L2_gnn_fc1_w"].rearrange("(h p) n -> p h n", p=P))
            load(raw[:, 3:6, :], w["L2_gnn_res1_w"].rearrange("(h p) n -> p h n", p=P))
            load(raw[:, 6:9, :], w["L2_gnn_fc2_w"].rearrange("p (h n) -> p h n", h=H2))
            load(raw[:, 9:12, :], w["L2_gnn_res2_w"].rearrange("p (h n) -> p h n", h=H2))
            for i, k in enumerate(("Wl0", "Wr0", "Wl1", "Wr1")):
                load(raw[:, 12 + i, :], w[f"L3_gnn_{k}"])
            with nc.allow_non_contiguous_dma(reason="attention vectors as columns"):
                for i, k in enumerate(("attn_l", "attn_r")):
                    load(a1[:, i, :], w[f"L2_gnn_{k}1"].rearrange("h p -> p h"))
                    load(a2[:, i:i + 1], w[f"L2_gnn_{k}2"].rearrange("h p -> p h"))
            full = N // P * P
            load(x_sb[:, 0:NT - 1, :], x[0:full, :].rearrange("(t p) n -> p t n", p=P))
            sp.wait_ge(s_setup, 1)
            load(x_sb[0:N - full, NT - 1, :], x[full:N, :])
            load(esrc[0:E].rearrange("(a n) -> a n", a=16), src.rearrange("(a n) -> a n", a=16))
            load(edst[P:P + E].rearrange("(a n) -> a n", a=16), dst.rearrange("(a n) -> a n", a=16))
            load(eattr[0:E, :], edge_attr_64)
            sp.wait_ge(s_steps, c.at("pads_out"))
            load(edst[0:P].rearrange("(p a) -> p a", a=1), pad_i[:, 0:1])
            npad = EP - E
            for d_ap, o in ((esrc, 0), (edst, P)):
                load(d_ap[o + E:o + E + P].rearrange("(p a) -> p a", a=1), pad_i[:, 1:2])
                load(d_ap[o + E + P:o + EP].rearrange("(p a) -> p a", a=1), pad_i[0:npad - P, 1:2])
            load(eattr[E:E + P, :], zrow[:, 0:ED])
            load(eattr[E + P:EP, :], zrow[0:npad - P, 0:ED])
            for p in PASSES:
                load(ends[p][EP:EP + P, :], zrow[:, 0:width(p)])
                load(carry[p][CH:CH + P, :], zrow[:, 0:width(p)])
            landed()
            sp.sem_inc(s_steps, 1)
            sp.wait_ge(s_steps, c.at("edges_in"))
            load(src_r[:, :, :], esrc.rearrange("(a t e) -> t a e", a=QA, e=P))
            load(dst_r[:, :, :], edst[P:P + EP].rearrange("(a t e) -> t a e", a=QA, e=P))
            load(prev_r[:, :, :], edst[P - 1:P - 1 + EP].rearrange("(a t e) -> t a e", a=QA, e=P))
            landed()
            sp.sem_inc(s_steps, 1)
            sp.wait_ge(s_steps, c.at("brk_out"))
            load(breaks[0:EP].rearrange("(a t e) -> t a e", a=QA, e=P), brk_r[:, :, :])
            load(breaks[EP:EP + P].rearrange("(p a) -> p a", a=1), ntmp[:, 5, 0:1])
            landed()
            sp.sem_inc(s_steps, 1)

            stored = [0]

            def stores(cc, j, pairs):
                sp.wait_ge(s_steps, cc.at("store", j))
                for d_ap, s_ap in pairs:
                    sp.dma_start(d_ap, s_ap).then_inc(s_store, 16)
                sp.wait_ge(s_store, stored[0] + 16 * len(pairs) + j * (16 * len(pairs)))
                sp.sem_inc(s_steps, 1)

            def node_rows(t, j):
                v = t.rearrange("(j k p) c -> j p k c", k=JT, p=P)
                return v[bass.ds(j, 1)].rearrange("j p k c -> (j p) k c")

            def table_loop(key, pairs):
                with sp.Fori(0, NJ) as j:
                    stores(chains[key], j, pairs(j))
                stored[0] += 16 * NJ * len(pairs(0))

            split = tab_b[:, :, :, :].rearrange("p k s c -> p k (s c)")
            table_loop("n0", lambda j: [(node_rows(row_tab["gcn"], j), split)])

            def edge_pass(p):
                c = chains["x_" + p]
                W = width(p)
                v_out = ends[p][0:EP, :].rearrange("(g k p) c -> g p k c", k=GC, p=P)
                v_attr = eattr.rearrange("(g k p) c -> g p k c", k=GC, p=P)

                def load_group(q, r):
                    if p in WEIGHTED:
                        if past(q, r, 4):
                            sp.wait_ge(max_done.sem, max_done.at(p, q, r, 4))
                        g = q * UNROLL + r
                        v = breaks[bass.ds(g * (GC * P), GC * P + 1)]
                        sp.dma_start(brk_b[0:WEIGHTED[p][0], r, :],
                                     v.rearrange("(a n) -> a n", a=1).to_broadcast([WEIGHTED[p][0], GC * P + 1]))\
                          .then_inc(brk_in.of(r), 16)
                        if past(q, r, 4):
                            sp.wait_ge(same_f_done.sem, same_f_done.at(p, q, r, 4))
                    elif p != "gcn":
                        if past(q, r, 4):
                            sp.wait_ge(sum_done.sem, sum_done.at(p, q, r, 4))
                    if p == "attn":
                        if past(q, r, 4):
                            sp.wait_ge(attr_t_done.sem, attr_t_done.at(p, q, r, 4))
                        sp.dma_start(at_b[:, r, :, :], grp(v_attr, q, r).rearrange("g p k c -> (g p) k c"))\
                          .then_inc(attr_in.of(r), 16)
                    if p != "gcn":
                        sp.dma_start(same_b[:, r, :, :],
                                     grp(same_hbm, q, r).rearrange("g p (k c) -> (g p) k c", k=GC))\
                          .then_inc(same_in.of(r), 16)

                def store_same(q, r):
                    sp.wait_ge(same_done.sem, same_done.at(p, q, r))
                    apart(sp, s_apart_sp)
                    sp.dma_start(grp(same_hbm, q, r).rearrange("g p (k c) -> (g p) k c", k=GC), same_b[:, r, :, :])\
                      .then_inc(same_out.of(r), 16)

                def store_ends(q, r):
                    sp.wait_ge(evac_done.sem, evac_done.at(p, q, r))
                    apart(sp, s_apart_sp)
                    sp.dma_start(grp(v_out, q, r).rearrange("g p k c -> (g p) k c"),
                                 o_b[:, r % 2, 0:GC * W].rearrange("p (k c) -> p k c", k=GC))\
                      .then_inc(ends_out.of(r), 16)

                if p == "gcn":
                    over_groups(sp, [(2, store_same), (3, store_ends)])
                    for r in range(4):
                        sp.wait_ge(same_out.sems[r], same_out.total[r])
                else:
                    over_groups(sp, [(0, load_group), (5, store_ends)])
                for r in range(2):
                    sp.wait_ge(ends_out.of((NG - 1 - r) % 4), ends_out.at(p, (NG - 1 - r) // 4, (NG - 1 - r) % 4))
                sp.wait_ge(s_steps, c.at("z_in"))
                v = ends[p][0:EP, :].rearrange("(a t e) c -> t a e c", a=QA, e=P)
                load(z_rows[:, :, 0:W], v[:, :, 0, :])
                landed()
                sp.sem_inc(s_steps, 1)
                sp.wait_ge(s_steps, c.at("r_out"))
                load(carry[p][0:CH, :].rearrange("(a t) c -> t a c", a=QA), r_rows[:, :, 0:W])
                landed()
                sp.sem_inc(s_steps, 1)

            edge_pass("gcn")
            table_loop("n_gcn", lambda j: [(node_rows(q_tab, j), tab[:, :, 0:D]),
                                           (node_rows(row_tab["attn"], j), tab[:, :, D:3 * D])])
            edge_pass("attn")
            table_loop("n_attn", lambda j: [(node_rows(row_tab["gat1"], j), tab[:, :, 0:D + H2]),
                                            (node_rows(er_tab["gat1"], j), er_n[:, :, :])])
            edge_pass("gat1")
            table_loop("n_gat1", lambda j: [(node_rows(row_tab["gat2"], j), tab[:, :, 0:D + 1]),
                                            (node_rows(er_tab["gat2"], j), er_2[:, :, :])])
            edge_pass("gat2")
            table_loop("n_gat2", lambda j: [(node_rows(row_tab["sage1"], j), split)])
            edge_pass("sage1")
            table_loop("n_sage1", lambda j: [(node_rows(row_tab["sage2"], j), split)])
            edge_pass("sage2")
            sp.wait_ge(s_steps, chains["n_sage2"].end)
            load(out[0:full, :].rearrange("(t p) n -> p t n", p=P), x_sb[:, 0:NT - 1, :])
            load(out[full:N, :], x_sb[0:N - full, NT - 1, :])
            landed()

        @block.gpsimd
        def _(pool):
            c = chains["prep"]
            g = nc.gpsimd
            g.memset(x_sb[:, NT - 1, :], 0.0).then_inc(s_setup, 1)
            g.memset(ident[:, :], 0.0)
            g.memset(flip[:, :], 0.0)
            g.memset(ones[:, :], 1.0)
            g.memset(zrow[:, :], 0.0)
            g.memset(ntmp[:, 5, :], -BIG)
            g.memset(upper[:, :], 1.0)
            g.memset(fwd[:, 1, :], -BIG)
            g.memset(pad_i[:, 0:1], -1)
            g.memset(pad_i[:, 1:2], NP - 1)
            g.iota(iota_i[:, :], pattern=[[1, P]], base=0, channel_multiplier=0)
            g.iota(after_i[:, :], pattern=[[1, CH]], base=0, channel_multiplier=-1).then_inc(s_steps, 1)
            pool.wait_ge(s_steps, c.at("pads"))
            g.affine_select(out=ident[:, :], in_=ident[:, :], compare_op=ALU.not_equal, fill=1.0, base=0,
                            pattern=[[-1, P]], channel_multiplier=1)
            g.affine_select(out=upper[:, :], in_=upper[:, :], compare_op=ALU.is_ge, fill=0.0, base=0,
                            pattern=[[1, P]], channel_multiplier=-1)
            g.affine_select(out=flip[:, :], in_=flip[:, :], compare_op=ALU.not_equal, fill=1.0, base=1 - P,
                            pattern=[[1, P]], channel_multiplier=1).then_inc(s_steps, 1)
            gathered = [0]
            grouped = [0]

            def edge_pass(p):
                W = width(p)
                weighted = p in WEIGHTED
                dst_tab = q_tab if p == "attn" else er_tab.get(p)

                def indices(q, r):
                    if past(q, r, 4):
                        pool.wait_ge(rows_in.of(r), rows_in.at(p, q, r, 1))
                    if weighted:
                        if past(q, r, 4):
                            pool.wait_ge(dst_rows_in.of(r), dst_rows_in.at(p, q, r, 1))
                    apart(pool, s_apart_pool)
                    gg = q * UNROLL + r
                    s = bass.ds(gg * GC, GC)
                    i = g.tensor_copy(src_ix[:, r, :], src_i[:, s])
                    if weighted:
                        i = g.tensor_copy(dst_ix[:, r, :], dst_i[:, s])
                    i.then_inc(ix_done.sem, 1)

                def gather(q, r):
                    pool.wait_ge(ix_done.sem, ix_done.at(p, q, r))
                    if weighted:
                        if past(q, r, 4):
                            pool.wait_ge(msg_done.sem, msg_done.at(p, q, r, 4))
                    else:
                        if past(q, r, 4):
                            pool.wait_ge(sum_done.sem, sum_done.at(p, q, r, 4))
                    if weighted:
                        if past(q, r, 4):
                            pool.wait_ge(prod_done.sem, prod_done.at(p, q, r, 4))
                    apart(pool, s_apart_pool)
                    for k in range(GC):
                        if weighted:
                            c2 = dst_tab.shape[1]
                            g.indirect_dma_start(
                                out=q_b[:, r, k, 0:c2], out_offset=None, in_=dst_tab,
                                in_offset=bass.IndirectOffsetOnAxis(ap=dst_ix[:, r, k:k + 1], axis=0))\
                             .then_inc(dst_rows_in.of(r), 16)
                        if weighted:
                            o = row_b[:, r, k, 0:row_tab[p].shape[1]]
                        else:
                            o = row_s[:, r, k * 3 * D:(k + 1) * 3 * D]
                        g.indirect_dma_start(out=o, out_offset=None, in_=row_tab[p],
                                             in_offset=bass.IndirectOffsetOnAxis(ap=src_ix[:, r, k:k + 1], axis=0))\
                         .then_inc(rows_in.of(r), 16)

                before = chains["n0"].end if p == "gcn" else chains["n_" + PASSES[PASSES.index(p) - 1]].end
                pool.wait_ge(s_steps, before)
                over_groups(pool, [(0, indices), (1, gather)])
                c = chains["x_" + p]
                pool.wait_ge(s_steps, c.base + 1)
                av = agg_of(p)
                for t in range(NT):
                    g.indirect_dma_start(out=av[:, t, :], out_offset=None, in_=ends[p],
                                         in_offset=bass.IndirectOffsetOnAxis(ap=end_i[:, t:t + 1], axis=0))\
                     .then_inc(s_gather, 16)
                gathered[0] += 16 * NT
                pool.wait_ge(s_steps, c.at("agg_ok"))
                pool.wait_ge(s_gather, gathered[0])
                for t in range(NT):
                    g.indirect_dma_start(out=av[:, t, :], out_offset=None, in_=carry[p],
                                         in_offset=bass.IndirectOffsetOnAxis(ap=carry_i[:, t:t + 1], axis=0),
                                         compute_op=ALU.add).then_inc(s_gather, 16)
                gathered[0] += 16 * NT
                pool.wait_ge(s_gather, gathered[0])
                pool.sem_inc(s_steps, 1)

            for p in PASSES:
                edge_pass(p)

        @block.scalar
        def _(act):
            a = nc.scalar

            def copy(o, i):
                return a.activation(o, i, ACT.Copy)

            c = chains["hist"]
            act.wait_ge(s_steps, c.at("deg_sqrt"))
            a.activation(norm[:, :, :], norm[:, :, :], ACT.Sqrt).then_inc(s_steps, 1)
            def wt_copy():
                copy(fc1_t[:, :, :], ps[:, 0:384].rearrange("p (h n) -> p h n", h=3))
                copy(res1_t[:, :, :], bank(1)[:, 0:384].rearrange("p (h n) -> p h n", h=3))
                copy(w2[:, :, 0:D], bank(2)[:, 0:384].rearrange("p (h n) -> p h n", h=3))
                copy(w2[:, :, D + 2:2 * D + 2], bank(3)[:, 0:384].rearrange("p (h n) -> p h n", h=3))
                copy(sage_t[:, :, :], bank(4)[:, :].rearrange("p (h n) -> p h n", h=4))
                copy(u1[:, :, :], bank(5)[:, 0:6].rearrange("p (l h) -> p l h", l=2))
                return copy(w2[:, :, D:D + 2], bank(6)[:, 0:6].rearrange("p (h l) -> p h l", l=2))

            act.wait_ge(s_steps, c.at("wt_sb"))
            wt_copy().then_inc(s_steps, 1)
            act.wait_ge(s_steps, c.at("bn_sd"))
            a.activation(bn_a[:, :, :], bn_a[:, :, :], ACT.Sqrt).then_inc(s_steps, 1)

            def ln_act(c, j, pre):
                act.wait_ge(s_steps, c.at(pre + "sq", j))
                a.activation(sq[:, :, :], y[:, :, :], ACT.Square).then_inc(s_steps, 1)
                act.wait_ge(s_steps, c.at(pre + "sd", j))
                a.activation(st[:, 2, :], st[:, 1, :], ACT.Sqrt).then_inc(s_steps, 1)

            def keep_h(c, j):
                act.wait_ge(s_steps, c.at("hkeep", j))
                apart(act, s_apart_act)
                copy(tiles(h_sb, j), hs[:, :, :]).then_inc(s_steps, 1)

            def load_h(c, j):
                act.wait_ge(s_steps, c.at("hl", j))
                apart(act, s_apart_act)
                copy(hs[:, :, :], tiles(h_sb, j)).then_inc(s_steps, 1)

            def split_act(c, j):
                act.wait_ge(s_steps, c.at("hi", j))
                copy(tab_b[:, :, 0, :], hs[:, :, :]).then_inc(s_steps, 1)
                act.wait_ge(s_steps, c.at("mid", j))
                copy(tab_b[:, :, 1, :], sq[:, :, :]).then_inc(s_steps, 1)

            c = chains["n0"]
            with act.Fori(0, NJ) as j:
                ln_act(c, j, "a")
                keep_h(c, j)
                split_act(c, j)

            def edge_pass(p):
                W = width(p)
                weighted = p in WEIGHTED

                def attr_sb(q, r):
                    act.wait_ge(attr_t_done.sem, attr_t_done.at(p, q, r))
                    if past(q, r, 2):
                        act.wait_ge(e_done.sem, e_done.at(p, q, r, 2))
                    copy(at_t[:, r % 2, :], bank(0)[0:ED, :]).then_inc(attr_sb_done.sem, 1)

                def keep_max(q, r):
                    heads = WEIGHTED[p][0]
                    act.wait_ge(max_done.sem, max_done.at(p, q, r))
                    apart(act, s_apart_act)
                    g0 = q * (UNROLL * GC) + r * GC
                    v = mx[0:heads, r % 2, :].rearrange("h (k e) -> h k e", k=GC)[:, ::-1, :]
                    copy(first_m[0:heads, bass.ds(g0, GC)], v[:, :, P - 1])
                    copy(last_m[0:heads, bass.ds(g0, GC)], v[:, :, 0]).then_inc(kept_done.sem, 1)

                def exps(q, r):
                    heads, _, scale = WEIGHTED[p]
                    act.wait_ge(dif_done.sem, dif_done.at(p, q, r))
                    if past(q, r, 2):
                        act.wait_ge(msg_done.sem, msg_done.at(p, q, r, 2))
                    a.activation(wgt[:, r % 2, 0:GC * heads], dif[:, r % 2, 0:GC * heads], ACT.Exp, scale=scale)\
                     .then_inc(exp_done.sem, 1)

                def same_f32(q, r):
                    act.wait_ge(same_in.of(r), same_in.at(p, q, r))
                    if past(q, r, 2):
                        act.wait_ge(sum_done.sem, sum_done.at(p, q, r, 2))
                    copy(same_f[:, r % 2, :, :], same_b[:, r, :, :]).then_inc(same_f_done.sem, 1)

                def evac(q, r):
                    act.wait_ge(sum_done.sem, sum_done.at(p, q, r))
                    if past(q, r, 2):
                        act.wait_ge(ends_out.of(r), ends_out.at(p, q, r, 1))
                    o = o_b[:, r % 2, 0:GC * W].rearrange("p (k c) -> p k c", k=GC)
                    if p == "gat1":
                        s = bank(4, 4).rearrange("p (k c) -> p k c", k=GC)[:, :, 0:W]
                    elif weighted:
                        s = bank(4 + 2 * (r % 2), 2).rearrange("p (k c) -> p k c", k=GC)[:, :, 0:W]
                    else:
                        s = bank(4 + r % 2).rearrange("p (k c) -> p k c", k=GC)
                    copy(o, s).then_inc(evac_done.sem, 1)

                if p == "attn":
                    over_groups(act, [(1, attr_sb), (3, keep_max), (4, same_f32), (3, exps), (4, evac)])
                elif weighted:
                    over_groups(act, [(3, keep_max), (4, same_f32), (3, exps), (4, evac)])
                else:
                    over_groups(act, [(2, evac)])

                c = chains["x_" + p]
                r_v = ps[0:CQ, 4 * BANK:8 * BANK].rearrange("p (a c) -> p a c", a=QA)[:, :, 0:W]
                if weighted:
                    heads, _, scale = WEIGHTED[p]
                    act.wait_ge(s_steps, c.at("lc_sb"))
                    copy(last_c[:, :, 0:heads],
                                                        ps[0:CQ, 0:QA * heads].rearrange("p (a h) -> p a h", a=QA)).then_inc(s_steps, 1)
                    for h in range(heads):
                        for t in range(QA):
                            act.wait_ge(s_steps, c.at(f"e{h}_{t}"))
                            a.activation(gw[:, t, :], gw[:, t, :], ACT.Exp, scale=-scale).then_inc(s_steps, 1)
                act.wait_ge(s_steps, c.at("r_sb"))
                copy(r_rows[:, :, 0:W], r_v).then_inc(s_steps, 1)

            def t_copy(c, j, name, o, s):
                act.wait_ge(s_steps, c.at(name, j))
                copy(o, s).then_inc(s_steps, 1)

            edge_pass("gcn")
            c = chains["n_gcn"]
            with act.Fori(0, NJ) as j:
                t_copy(c, j, "Ts", a_t[:, 0:JT * P], ps[:, 0:JT * P])
                ln_act(c, j, "a")
                ln_act(c, j, "b")
                keep_h(c, j)
                t_copy(c, j, "T2s", h_t[:, :], ps[:, 0:JT * P])
            edge_pass("attn")
            c = chains["n_attn"]
            with act.Fori(0, NJ) as j:
                load_h(c, j)
                t_copy(c, j, "Ts", h_t[:, :], ps[:, 0:JT * P])
                ln_act(c, j, "a")
                t_copy(c, j, "T2s", a_t[:, 0:JT * P], ps[:, 0:JT * P])
                for o in range(4):
                    act.wait_ge(s_steps, c.at(f"gelu{o}", j))
                    a.activation(
                        hid[:, o, :].rearrange("p (s n) -> p s n", s=2),
                        bank(2 * o, 2).rearrange("p (s n) -> p s n", s=2)[:, :, 0:JT * P // 2],
                        ACT.Gelu, bias=b_f1[:, o:o + 1]).then_inc(s_steps, 1)
                ln_act(c, j, "b")
                ln_act(c, j, "c")
                keep_h(c, j)
                t_copy(c, j, "T3s", h_t[:, :], ps[:, 0:JT * P])
                t_copy(c, j, "tab", tab[:, :, 0:D], hs[:, :, :])
            edge_pass("gat1")
            c = chains["n_gat1"]
            with act.Fori(0, NJ) as j:
                load_h(c, j)
                t_copy(c, j, "Ts", a_t[:, :], ps[:, 0:JT * H2 * P])
                t_copy(c, j, "T1s", h_t[:, :], ps[:, 4 * BANK:4 * BANK + JT * P])
                act.wait_ge(s_steps, c.at("exp", j))
                a.activation(a_n[:, :, :], a_n[:, :, :], ACT.Exp).then_inc(s_steps, 1)
                t_copy(c, j, "T2s", a_t[:, :], ps[:, 0:JT * H2 * P])
                f_v = ps[:, 0:JT * BANK].rearrange("p (k c) -> p k c", k=JT)
                t_copy(c, j, "er_s", er_2[:, :, :], f_v[:, :, D:D + 2])
                act.wait_ge(s_steps, c.at("res", j))
                apart(act, s_apart_act)
                copy(tiles(h_sb, j), f_v[:, :, D + 2:2 * D + 2]).then_inc(s_steps, 1)
            edge_pass("gat2")
            c = chains["n_gat2"]
            with act.Fori(0, NJ) as j:
                ln_act(c, j, "a")
                keep_h(c, j)
                split_act(c, j)
            for p in ("sage1", "sage2"):
                edge_pass(p)
                c = chains["n_" + p]
                with act.Fori(0, NJ) as j:
                    load_h(c, j)
                    t_copy(c, j, "Ts", a_t[:, 0:JT * P], ps[:, 0:JT * P])
                    t_copy(c, j, "T1s", h_t[:, :], ps[:, 2 * BANK:2 * BANK + JT * P])
                    if p == "sage1":
                        keep_h(c, j)
                        split_act(c, j)

        @block.tensor
        def _(pe):
            mm = nc.tensor.matmul

            c = chains["prep"]
            pe.wait_ge(s_steps, c.at("cols"))
            for a in range(QA):
                mm(ps[:, a * CQ:(a + 1) * CQ], src_rf[:, a, :], ident[0:CQ, 0:CQ], start=True, stop=True)
                i = mm(ps[:, BANK + a * CQ:BANK + (a + 1) * CQ], dst_rf[:, a, :], ident[0:CQ, 0:CQ], start=True, stop=True)
            i.then_inc(s_steps, 1)

            def hist(first, last, turn):
                pe.wait_ge(s_hot, turn * 2 + 2)
                for s in range(2):
                    for k in range(UNROLL):
                        i = mm(ps[:, s * BANK:s * BANK + NT], hot_lo[:, s, k, :], hot_hi[:, s, k, :],
                               start=first and k == 0, stop=last and k == UNROLL - 1, skip_group_check=True)
                i.then_inc(s_hist, 1)

            hist(True, False, 0)
            with pe.Fori(1, NG - 1) as t:
                hist(False, False, t)
            hist(False, True, NG - 1)
            c = chains["hist"]
            pe.wait_ge(s_hist, NG)
            pe.wait_ge(s_steps, c.at("hist_start"))
            pe.sem_inc(s_steps, 1)
            pe.wait_ge(s_steps, c.at("cum_ps"))
            mm(ps[:, 0:NT], upper[:, :], deg[:, 1, :], start=True, stop=True)
            mm(ps[:, BANK:BANK + NT], ones[:, :], deg[:, 1, :], start=True, stop=True).then_inc(s_steps, 1)
            pe.wait_ge(s_steps, c.at("bnd_ps"))
            for a in range(QA):
                mm(ps[0:CQ, a:a + 1], dst_f[:, a * CQ:(a + 1) * CQ], ident[:, 0:1], start=True, stop=True)
            mm(ps[0:CQ, BANK:BANK + CH], bc(ident[:, P - 1:P], [P, CQ]), dst_f[:, :], start=True, stop=True)\
                .then_inc(s_steps, 1)
            pe.wait_ge(s_steps, c.at("wt_ps"))
            for i in range(16):
                mm(ps[:, (i // 3) * BANK + (i % 3) * D if i < 12 else 4 * BANK + (i - 12) * D:][:, 0:D],
                   raw[:, i, :], ident[:, :], start=True, stop=True)
            for h in range(H2):
                for l in range(2):
                    mm(ps[:, 5 * BANK + l * H2 + h:5 * BANK + l * H2 + h + 1], raw[:, h, :], a1[:, l, h:h + 1],
                       start=True, stop=True)
                i = mm(ps[:, 6 * BANK + 2 * h:6 * BANK + 2 * h + 2], raw[:, 6 + h, :], a2[:, :], start=True, stop=True)
            i.then_inc(s_steps, 1)

            def edge_pass(p):
                W = width(p)
                weighted = p in WEIGHTED
                if weighted:
                    heads, cols, _ = WEIGHTED[p]

                def bcast_dst(q, r):
                    pe.wait_ge(diag_done.sem, diag_done.at(p, q, r))
                    if past(q, r, 1):
                        pe.wait_ge(same_done.sem, same_done.at(p, q, r, 1))
                    mm(bank(0), ones[:, :], diag[:, r % 2, :, :].rearrange("p k c -> p (k c)"), start=True, stop=True)\
                        .then_inc(bcast_done.sem, 1)

                def attr_t(q, r):
                    pe.wait_ge(attr_in.of(r), attr_in.at(p, q, r))
                    if past(q, r, 1):
                        pe.wait_ge(attr_sb_done.sem, attr_sb_done.at(p, q, r, 1))
                    for k in range(GC):
                        i = mm(bank(0)[0:ED, k * P:(k + 1) * P], at_b[:, r, k, :], flip[:, :], start=True, stop=True)
                    i.then_inc(attr_t_done.sem, 1)

                def edge_terms(q, r):
                    pe.wait_ge(attr_sb_done.sem, attr_sb_done.at(p, q, r))
                    if past(q, r, 1):
                        pe.wait_ge(kve_done.sem, kve_done.at(p, q, r, 1))
                    for k in range(GC):
                        i = mm(bank(1)[:, k * D:(k + 1) * D], at_t[:, r % 2, k * P:(k + 1) * P], w_e[:, :],
                               start=True, stop=True)
                    i.then_inc(e_done.sem, 1)

                def logit_t(q, r):
                    pe.wait_ge(logit_done.sem, logit_done.at(p, q, r))
                    if past(q, r, 1):
                        pe.wait_ge(fwd_done.sem, fwd_done.at(p, q, r, 1))
                    for k in range(GC):
                        i = mm(bank(2)[0:heads, k * P:(k + 1) * P], logit[:, r % 2, k * heads:(k + 1) * heads],
                               flip[:, :], start=True, stop=True)
                    i.then_inc(logit_t_done.sem, 1)

                def max_t(q, r):
                    pe.wait_ge(max_done.sem, max_done.at(p, q, r))
                    if past(q, r, 1):
                        pe.wait_ge(dif_done.sem, dif_done.at(p, q, r, 1))
                    for k in range(GC):
                        i = mm(bank(3)[:, k * heads:(k + 1) * heads],
                               mx[0:heads, r % 2, (GC - 1 - k) * P:(GC - k) * P], ident[0:heads, 0:heads],
                               start=True, stop=True)
                    i.then_inc(max_t_done.sem, 1)

                def sums(q, r):
                    if weighted:
                        pe.wait_ge(msg_done.sem, msg_done.at(p, q, r))
                        pe.wait_ge(same_f_done.sem, same_f_done.at(p, q, r))
                        if past(q, r, 1 if p == "gat1" else 2):
                            pe.wait_ge(evac_done.sem, evac_done.at(p, q, r, 1 if p == "gat1" else 2))
                        for k in range(GC):
                            if p == "gat1":
                                o = bank(4 + k)[:, 0:W]
                            else:
                                o = bank(4 + 2 * (r % 2) + k // 2)[:, (k % 2) * 256:(k % 2) * 256 + W]
                            i = mm(o, same_f[:, r % 2, k, :], msg[:, r % 2, k * W:(k + 1) * W], start=True, stop=True)
                    else:
                        pe.wait_ge(rows_in.of(r), rows_in.at(p, q, r))
                        if p == "gcn":
                            pe.wait_ge(same_done.sem, same_done.at(p, q, r))
                        else:
                            pe.wait_ge(same_in.of(r), same_in.at(p, q, r))
                        if past(q, r, 2):
                            pe.wait_ge(evac_done.sem, evac_done.at(p, q, r, 2))
                        for k in range(GC):
                            for s in range(3):
                                o = (k * 3 + s) * D
                                i = mm(bank(4 + r % 2)[:, k * D:(k + 1) * D], same_b[:, r, k, :],
                                       row_s[:, r, o:o + D], start=s == 0, stop=s == 2)
                    i.then_inc(sum_done.sem, 1)

                if p == "gcn":
                    over_groups(pe, [(1, bcast_dst), (2, sums)])
                elif p == "attn":
                    over_groups(pe, [(2, edge_terms), (1, attr_t), (3, max_t), (2, logit_t), (4, sums)])
                elif weighted:
                    over_groups(pe, [(3, max_t), (2, logit_t), (4, sums)])
                else:
                    over_groups(pe, [(2, sums)])

                c = chains["x_" + p]

                def carried(h, c0, c1, mat):
                    for b in range(QA):
                        for t in range(b + 1):
                            i = mm(ps[0:CQ, (4 + b) * BANK + c0:(4 + b) * BANK + c1], mat[:, t, b * CQ:(b + 1) * CQ],
                                   z_rows[:, t, c0:c1], start=t == 0, stop=t == b)
                    return i

                if weighted:
                    pe.wait_ge(s_steps, c.at("lc_ps"))
                    for a in range(QA):
                        i = mm(ps[0:CQ, a * heads:(a + 1) * heads], last_m[0:heads, a * CQ:(a + 1) * CQ],
                               ident[0:heads, 0:heads], start=True, stop=True)
                    i.then_inc(s_steps, 1)
                    for h in range(heads):
                        pe.wait_ge(s_steps, c.at(f"fb{h}"))
                        mm(ps[0:CQ, BANK:BANK + CH], spread[0:heads, h, :],
                                                          first_m[0:heads, :], start=True, stop=True).then_inc(s_steps, 1)
                        pe.wait_ge(s_steps, c.at(f"r{h}"))
                        carried(h, h * (cols + 1), (h + 1) * (cols + 1), gw).then_inc(s_steps, 1)
                else:
                    pe.wait_ge(s_steps, c.at("r"))
                    carried(0, 0, D, carries).then_inc(s_steps, 1)

            def transposes(c, j, name, srcs, b0=0):
                pe.wait_ge(s_steps, c.at(name, j))
                for i, s in enumerate(srcs):
                    last = mm(ps[:, b0 * BANK + i * P:b0 * BANK + (i + 1) * P], s, ident[:, :], start=True, stop=True)
                last.then_inc(s_steps, 1)

            def linear(c, j, name, out_of, terms):
                pe.wait_ge(s_steps, c.at(name, j))
                for k in range(JT):
                    for i, (lhs, rhs) in enumerate(terms):
                        last = mm(out_of(k), lhs(k), rhs, start=i == 0, stop=i == len(terms) - 1)
                last.then_inc(s_steps, 1)

            def part(t, k, n=P):
                return t[:, k * n:(k + 1) * n]

            edge_pass("gcn")
            c = chains["n_gcn"]
            with pe.Fori(0, NJ) as j:
                transposes(c, j, "T", [a_n[:, k, 0:D] for k in range(JT)])
                linear(c, j, "lin", lambda k: part(ps, 8 + k), [(lambda k: part(a_t, k), w0[:, :])])
                transposes(c, j, "T2", [hs[:, k, :] for k in range(JT)])
                linear(c, j, "qkv", lambda k: bank(2 + k)[:, 0:3 * D], [(lambda k: part(h_t, k), w_qkv[:, :])])
            edge_pass("attn")
            c = chains["n_attn"]
            with pe.Fori(0, NJ) as j:
                transposes(c, j, "T", [hs[:, k, :] for k in range(JT)])
                linear(c, j, "lin", lambda k: part(ps, 8 + k), [(lambda k: part(h_t, k), w_skip[:, :])])
                transposes(c, j, "T2", [y[:, k, :] for k in range(JT)])
                pe.wait_ge(s_steps, c.at("ffn1", j))
                half = JT * P // 2
                for o in range(4):
                    for s in range(2):
                        i = mm(bank(2 * o + s)[:, 0:half], w_f1[:, o * P:(o + 1) * P], a_t[:, s * half:(s + 1) * half],
                               start=True, stop=True)
                i.then_inc(s_steps, 1)
                linear(c, j, "ffn2", lambda k: part(ps, k),
                       [((lambda k, o=o: hid[:, o, k * P:(k + 1) * P]), w_f2[:, o, :]) for o in range(4)])
                transposes(c, j, "T3", [hs[:, k, :] for k in range(JT)])
                linear(c, j, "el", lambda k: bank(2)[:, k * 6:(k + 1) * 6],
                       [(lambda k: part(h_t, k), u1[:, :, :].rearrange("p l h -> p (l h)"))])
            edge_pass("gat1")
            c = chains["n_gat1"]
            with pe.Fori(0, NJ) as j:
                pe.wait_ge(s_steps, c.at("T", j))
                for k in range(JT):
                    for h in range(H2):
                        mm(part(ps, k * H2 + h), a_n[:, k, h * D:(h + 1) * D], ident[:, :], start=True, stop=True)
                    last = mm(ps[:, 4 * BANK + k * P:4 * BANK + (k + 1) * P], hs[:, k, :], ident[:, :],
                              start=True, stop=True)
                last.then_inc(s_steps, 1)
                pe.wait_ge(s_steps, c.at("lin", j))
                for k in range(JT):
                    for h in range(H2):
                        o = bank(k)[:, h * D:(h + 1) * D]
                        mm(o, part(a_t, k * H2 + h), fc1_t[:, h, :], start=True, stop=False)
                        i = mm(o, part(h_t, k), res1_t[:, h, :], start=False, stop=True)
                i.then_inc(s_steps, 1)
                transposes(c, j, "T2", [a_n[:, k, h * D:(h + 1) * D] for k in range(JT) for h in range(H2)])
                linear(c, j, "feat", lambda k: bank(k)[:, 0:2 * D + 2],
                       [((lambda k, h=h: part(a_t, k * H2 + h)), w2[:, h, :]) for h in range(H2)])
            edge_pass("gat2")
            for i, p in enumerate(("sage1", "sage2")):
                edge_pass(p)
                c = chains["n_" + p]
                with pe.Fori(0, NJ) as j:
                    pe.wait_ge(s_steps, c.at("T", j))
                    for k in range(JT):
                        mm(part(ps, k), a_n[:, k, 0:D], ident[:, :], start=True, stop=True)
                        last = mm(part(ps, 8 + k), hs[:, k, :], ident[:, :], start=True, stop=True)
                    last.then_inc(s_steps, 1)
                    linear(c, j, "lin", lambda k: bank(4 + k // 4)[:, (k % 4) * P:(k % 4 + 1) * P],
                           [(lambda k: part(a_t, k), sage_t[:, 2 * i, :]), (lambda k: part(h_t, k), sage_t[:, 2 * i + 1, :])])

        @block.vector
        def _(dve):
            v = nc.vector
            tt, ts, stt = v.tensor_tensor, v.tensor_scalar, v.scalar_tensor_tensor

            c = chains["prep"]
            dve.wait_ge(s_steps, c.at("flip"))
            v.tensor_copy(iota_row[:, :], iota_i[:, :]).then_inc(s_steps, 1)
            dve.wait_ge(s_steps, c.at("cast"))
            v.tensor_copy(src_rf[:, :, ::-1], src_r[:, :, :])
            v.tensor_copy(dst_rf[:, :, ::-1], dst_r[:, :, :]).then_inc(s_steps, 1)
            dve.wait_ge(s_steps, c.at("brk"))
            tt(brk_r[:, :, :], dst_r[:, :, :], prev_r[:, :, :], ALU.not_equal).then_inc(s_steps, 1)
            dve.wait_ge(s_steps, c.at("brk2"))
            ts(brk_r[:, :, :], brk_r[:, :, :], -BIG, None, ALU.mult).then_inc(s_steps, 1)
            dve.wait_ge(s_steps, c.at("cols_i"))
            v.tensor_copy(src_i[:, :], ps[:, 0:CH])
            v.tensor_copy(dst_f[:, :], ps[:, BANK:BANK + CH])
            v.tensor_copy(dst_i[:, :], ps[:, BANK:BANK + CH]).then_inc(s_steps, 1)
            dve.wait_ge(s_steps, c.at("bits"))
            for i, t in enumerate((src_i, dst_i)):
                ts(part_i[:, :], t[:, :], P - 1, None, ALU.bitwise_and).then_inc(s_seed, 1)
                dve.wait_ge(s_seed, 4 * i + 1)
                v.tensor_copy(lo_f[:, i, :], part_i[:, :]).then_inc(s_seed, 1)
                dve.wait_ge(s_seed, 4 * i + 2)
                ts(part_i[:, :], t[:, :], 7, None, ALU.logical_shift_right).then_inc(s_seed, 1)
                dve.wait_ge(s_seed, 4 * i + 3)
                v.tensor_copy(hi_f[:, i, :], part_i[:, :]).then_inc(s_seed, 1)
                dve.wait_ge(s_seed, 4 * i + 4)
            dve.sem_inc(s_steps, 1)
            dve.wait_ge(s_steps, c.at("bits_f"))
            dve.sem_inc(s_steps, 1)

            def hot(turn, wait):
                for s in range(2):
                    if wait:
                        dve.wait_ge(s_hist, turn)
                    cols = bass.ds(turn * UNROLL, UNROLL)
                    tt(hot_lo[:, s, :, :], bc(iota_row[:, :].rearrange("p (a c) -> p a c", a=1), [P, UNROLL, P]),
                       bc(lo_f[:, s, cols].rearrange("p (a c) -> p a c", c=1), [P, UNROLL, P]), ALU.is_equal)
                    tt(hot_hi[:, s, :, :], bc(iota_row[:, 0:NT].rearrange("p (a c) -> p a c", a=1), [P, UNROLL, NT]),
                       bc(hi_f[:, s, cols].rearrange("p (a c) -> p a c", c=1), [P, UNROLL, NT]), ALU.is_equal)\
                        .then_inc(s_hot, 1)

            dve.wait_ge(s_steps, chains["prep"].end)
            hot(0, False)
            with dve.Fori(1, NG) as t:
                hot(t, True)

            c = chains["hist"]
            dve.wait_ge(s_steps, c.at("hist_read"))
            v.tensor_copy(deg[:, 0, :], ps[:, 0:NT])
            v.tensor_copy(deg[:, 1, :], ps[:, BANK:BANK + NT]).then_inc(s_steps, 1)
            n = lambda i: ntmp[:, i, :]
            ni = lambda i: ntmp_i[:, i, :]
            dve.wait_ge(s_steps, c.at("deg_max"))
            ts(norm[:, :, :], deg[:, :, :], 1.0, None, ALU.max).then_inc(s_steps, 1)
            dve.wait_ge(s_steps, c.at("deg_norm"))
            v.reciprocal(norm[:, :, :], norm[:, :, :]).then_inc(s_steps, 1)
            dve.wait_ge(s_steps, c.at("cnt_r"))
            ts(n(0), deg[:, 1, :], 1.0, None, ALU.max).then_inc(s_seed, 1)
            dve.wait_ge(s_seed, 9)
            v.reciprocal(cnt_r[:, :], n(0)).then_inc(s_steps, 1)
            dve.wait_ge(s_steps, c.at("tot_sb"))
            v.tensor_copy(tot[:, :], ps[:, BANK:BANK + NT]).then_inc(s_steps, 1)
            dve.wait_ge(s_steps, c.at("tot_scan"))
            v.tensor_tensor_scan(tot_x[:, :], ones[:, 0:NT], tot[:, :], 0.0, ALU.mult, ALU.add).then_inc(s_steps, 1)
            dve.wait_ge(s_steps, c.at("tot_ex"))
            tt(tot_x[:, :], tot_x[:, :], tot[:, :], ALU.subtract).then_inc(s_steps, 1)
            dve.wait_ge(s_steps, c.at("cum"))
            tt(cum[:, :], tot_x[:, :], ps[:, 0:NT], ALU.add).then_inc(s_steps, 1)
            dve.wait_ge(s_steps, c.at("nz"))
            ts(n(0), deg[:, 1, :], 0.0, None, ALU.is_gt).then_inc(s_steps, 1)
            dve.wait_ge(s_steps, c.at("end"))
            stt(n(1), cum[:, :], -1.0, n(0), ALU.add, ALU.mult).then_inc(s_steps, 1)
            dve.wait_ge(s_steps, c.at("end_ii"))
            v.tensor_copy(ni(0), n(1)).then_inc(s_steps, 1)
            dve.wait_ge(s_steps, c.at("end_xor"))
            ts(ni(1), ni(0), P - 1, None, ALU.bitwise_xor).then_inc(s_steps, 1)
            dve.wait_ge(s_steps, c.at("end_f"))
            v.tensor_copy(n(2), ni(1)).then_inc(s_steps, 1)
            dve.wait_ge(s_steps, c.at("end_m"))
            stt(n(2), n(2), float(-EP), n(0), ALU.add, ALU.mult).then_inc(s_steps, 1)
            dve.wait_ge(s_steps, c.at("end_i"))
            ts(end_i[:, :], n(2), float(EP), None, ALU.add).then_inc(s_steps, 1)
            dve.wait_ge(s_steps, c.at("blk_i"))
            ts(ni(2), ni(0), 7, None, ALU.logical_shift_right).then_inc(s_steps, 1)
            dve.wait_ge(s_steps, c.at("blk_f"))
            v.tensor_copy(n(3), ni(2)).then_inc(s_steps, 1)
            dve.wait_ge(s_steps, c.at("start"))
            tt(n(4), cum[:, :], deg[:, 1, :], ALU.subtract).then_inc(s_steps, 1)
            dve.wait_ge(s_steps, c.at("inner"))
            stt(n(4), n(3), float(P), n(4), ALU.mult, ALU.is_ge).then_inc(s_steps, 1)
            dve.wait_ge(s_steps, c.at("blk_m"))
            tt(n(4), n(4), n(0), ALU.mult).then_inc(s_steps, 1)
            dve.wait_ge(s_steps, c.at("blk_n"))
            stt(n(3), n(3), float(-CH), n(4), ALU.add, ALU.mult).then_inc(s_steps, 1)
            dve.wait_ge(s_steps, c.at("carry_i"))
            ts(carry_i[:, :], n(3), float(CH), None, ALU.add).then_inc(s_steps, 1)
            dve.wait_ge(s_steps, c.at("last_sb"))
            v.tensor_copy(last_dst[:, :], ps[0:CQ, 0:QA]).then_inc(s_steps, 1)
            dve.wait_ge(s_steps, c.at("after_f"))
            v.tensor_copy(after[:, :], after_i[0:CQ, :]).then_inc(s_steps, 1)
            dve.wait_ge(s_steps, c.at("carries"))
            for a in range(QA):
                i = ts(carries[:, a, :], after[:, :], float(a * CQ), None, ALU.is_gt)
            i.then_inc(s_steps, 1)
            dve.wait_ge(s_steps, c.at("carries2"))
            for a in range(QA):
                i = stt(carries[:, a, :], ps[0:CQ, BANK:BANK + CH], last_dst[:, a:a + 1], carries[:, a, :],
                        ALU.is_equal, ALU.mult)
            i.then_inc(s_steps, 1)
            dve.wait_ge(s_steps, c.at("spread"))
            v.tensor_copy(
                spread[:, :, :], bc(ident[0:H1, 0:H1].rearrange("h (g c) -> h g c", c=1), [H1, H1, CQ])).then_inc(s_steps, 1)
            dve.wait_ge(s_steps, c.at("bn_var"))
            for i in range(2):
                last = ts(bn_a[:, i, :], rows[f"L3_gnn_rv{i}"][:, :], EPS, None, ALU.add)
            last.then_inc(s_steps, 1)
            dve.wait_ge(s_steps, c.at("bn_rs"))
            v.reciprocal(bn_a[:, :, :], bn_a[:, :, :]).then_inc(s_steps, 1)
            for name, o, x0, y0, op in (("bn_a", bn_a, bn_a, "g", ALU.mult), ("bn_b1", bn_b, "b", "rm", ALU.subtract),
                                        ("bn_b2", bn_b, bn_b, bn_a, ALU.mult), ("bn_b3", bn_b, bn_b, "be", ALU.add)):
                dve.wait_ge(s_steps, c.at(name))
                pick = lambda s, i: rows[f"L3_gnn_{s}{i}"][:, :] if isinstance(s, str) else s[:, i, :]
                for i in range(2):
                    last = tt(o[:, i, :], pick(x0, i), pick(y0, i), op)
                last.then_inc(s_steps, 1)

            def nb(ap, n=D):
                return bc(ap.rearrange("p (k a) -> p k a", a=1), [P, JT, n])

            def fb(ap, n=D):
                return bc(ap.rearrange("p (a c) -> p a c", a=1), [P, JT, n])

            Y = y[:, :, :]

            def norm_steps(c, j, pre):
                dve.wait_ge(s_steps, c.at(pre + "mean", j))
                v.reduce_sum(st[:, 0, :], Y, axis=AX_X).then_inc(s_steps, 1)
                dve.wait_ge(s_steps, c.at(pre + "neg", j))
                ts(st[:, 4, :], st[:, 0, :], 1.0 / D, None, ALU.mult).then_inc(s_steps, 1)
                dve.wait_ge(s_steps, c.at(pre + "cent", j))
                tt(Y, Y, nb(st[:, 4, :]), ALU.subtract).then_inc(s_steps, 1)
                dve.wait_ge(s_steps, c.at(pre + "var", j))
                v.reduce_sum(st[:, 0, :], sq[:, :, :], axis=AX_X).then_inc(s_steps, 1)
                dve.wait_ge(s_steps, c.at(pre + "vare", j))
                ts(st[:, 1, :], st[:, 0, :], 1.0 / D, EPS, ALU.mult, ALU.add).then_inc(s_steps, 1)
                dve.wait_ge(s_steps, c.at(pre + "rs", j))
                v.reciprocal(st[:, 3, :], st[:, 2, :]).then_inc(s_steps, 1)

            def add_to_x(c, j, name):
                dve.wait_ge(s_steps, c.at(name, j))
                tt(Y, Y, tiles(x_sb, j), ALU.add).then_inc(s_steps, 1)
                dve.wait_ge(s_steps, c.at("xk", j))
                apart(dve, s_apart_dve)
                v.tensor_copy(tiles(x_sb, j), Y).then_inc(s_steps, 1)

            def relu_norm(c, j):
                dve.wait_ge(s_steps, c.at("hs", j))
                stt(hs[:, :, :], Y, 0.0, nb(st[:, 3, :]), ALU.max, ALU.mult).then_inc(s_steps, 1)

            def split_dve(c, j):
                dve.wait_ge(s_steps, c.at("r1", j))
                tt(sq[:, :, :], hs[:, :, :], tab_b[:, :, 0, :], ALU.subtract).then_inc(s_steps, 1)
                dve.wait_ge(s_steps, c.at("r2", j))
                tt(sq[:, :, :], sq[:, :, :], tab_b[:, :, 1, :], ALU.subtract).then_inc(s_steps, 1)
                dve.wait_ge(s_steps, c.at("lo", j))
                v.tensor_copy(tab_b[:, :, 2, :], sq[:, :, :]).then_inc(s_steps, 1)

            def cols(ap, j):
                return ap[:, bass.ds(j * JT, JT)]

            c = chains["n0"]
            with dve.Fori(0, NJ) as j:
                dve.wait_ge(s_steps, c.at("xl", j))
                v.tensor_copy(Y, tiles(x_sb, j)).then_inc(s_steps, 1)
                norm_steps(c, j, "a")
                relu_norm(c, j)
                dve.wait_ge(s_steps, c.at("hn", j))
                tt(hs[:, :, :], hs[:, :, :], nb(cols(norm[:, 0, :], j)), ALU.mult).then_inc(s_steps, 1)
                split_dve(c, j)

            def edge_pass(p):
                W = width(p)
                weighted = p in WEIGHTED
                if weighted:
                    heads, nc_, _ = WEIGHTED[p]

                def diags(q, r):
                    if past(q, r, 2):
                        dve.wait_ge(bcast_done.sem, bcast_done.at(p, q, r, 2))
                    g0 = bass.ds(q * (UNROLL * GC) + r * GC, GC)
                    tt(diag[:, r % 2, :, :], bc(ident[:, :].rearrange("p (a c) -> p a c", a=1), [P, GC, P]),
                       bc(dst_f[:, g0].rearrange("p (k c) -> p k c", c=1), [P, GC, P]), ALU.mult)\
                        .then_inc(diag_done.sem, 1)

                def same(q, r):
                    dve.wait_ge(bcast_done.sem, bcast_done.at(p, q, r))
                    if past(q, r, 4):
                        dve.wait_ge(sum_done.sem, sum_done.at(p, q, r, 4))
                    if past(q, r, 4):
                        dve.wait_ge(same_out.of(r), same_out.at(p, q, r, 1))
                    g0 = bass.ds(q * (UNROLL * GC) + r * GC, GC)
                    tt(same_b[:, r, :, :], bank(0).rearrange("p (k c) -> p k c", k=GC),
                       bc(dst_f[:, g0].rearrange("p (k c) -> p k c", c=1), [P, GC, P]), ALU.is_equal)\
                        .then_inc(same_done.sem, 1)

                def logits(q, r):
                    dve.wait_ge(rows_in.of(r), rows_in.at(p, q, r))
                    dve.wait_ge(dst_rows_in.of(r), dst_rows_in.at(p, q, r))
                    l = logit[:, r % 2, 0:GC * heads]
                    if p == "attn":
                        dve.wait_ge(e_done.sem, e_done.at(p, q, r))
                        kv = row_b[:, r, :, :].rearrange("p k (s c) -> p k s c", s=2)
                        tt(kv, kv, bc(bank(1).rearrange("p (k s c) -> p k s c", k=GC, s=1), [P, GC, 2, D]), ALU.add)\
                            .then_inc(kve_done.sem, 1)
                        dve.wait_ge(kve_done.sem, kve_done.at(p, q, r))
                        if past(q, r, 1):
                            dve.wait_ge(logit_done.sem, logit_done.at(p, q, r, 1))
                        tt(prod[:, :, :], row_b[:, r, :, 0:D], q_b[:, r, :, :], ALU.mult).then_inc(prod_done.sem, 1)
                        dve.wait_ge(prod_done.sem, prod_done.at(p, q, r))
                        if past(q, r, 2):
                            dve.wait_ge(logit_t_done.sem, logit_t_done.at(p, q, r, 2))
                        if past(q, r, 2):
                            dve.wait_ge(dif_done.sem, dif_done.at(p, q, r, 2))
                        v.reduce_sum(l, prod[:, :, :].rearrange("p k (h c) -> p (k h) c", h=heads), axis=AX_X)\
                            .then_inc(logit_done.sem, 1)
                    else:
                        z = z_b[:, :, 0:heads]
                        if past(q, r, 1):
                            dve.wait_ge(logit_done.sem, logit_done.at(p, q, r, 1))
                        er0 = 0 if p == "gat1" else 1
                        tt(z, row_b[:, r, :, D:D + heads], q_b[:, r, :, er0:er0 + heads], ALU.add).then_inc(prod_done.sem, 1)
                        dve.wait_ge(prod_done.sem, prod_done.at(p, q, r))
                        if past(q, r, 2):
                            dve.wait_ge(logit_t_done.sem, logit_t_done.at(p, q, r, 2))
                        if past(q, r, 2):
                            dve.wait_ge(dif_done.sem, dif_done.at(p, q, r, 2))
                        stt(l.rearrange("p (k h) -> p k h", k=GC), z, 0.2, z, ALU.mult, ALU.max)\
                            .then_inc(logit_done.sem, 1)

                def maxima(q, r):
                    s = r % 2
                    dve.wait_ge(logit_t_done.sem, logit_t_done.at(p, q, r))
                    dve.wait_ge(brk_in.of(r), brk_in.at(p, q, r))
                    if past(q, r, 1):
                        dve.wait_ge(fwd_done.sem, fwd_done.at(p, q, r, 1))
                    if past(q, r, 1):
                        dve.wait_ge(max_done.sem, max_done.at(p, q, r, 1))
                    b = brk_b[0:heads, r, :]
                    v.tensor_tensor_scan(fwd[0:heads, s, :], b[:, 0:GC * P], bank(2)[0:heads, :],
                                         fwd[0:heads, 1 - s, GC * P - 1:GC * P], ALU.add, ALU.max)\
                        .then_inc(fwd_done.sem, 1)
                    dve.wait_ge(fwd_done.sem, fwd_done.at(p, q, r))
                    if past(q, r, 2):
                        dve.wait_ge(max_t_done.sem, max_t_done.at(p, q, r, 2))
                    if past(q, r, 2):
                        dve.wait_ge(kept_done.sem, kept_done.at(p, q, r, 2))
                    v.tensor_tensor_scan(mx[0:heads, s, :], b[:, GC * P:0:-1], fwd[0:heads, s, ::-1],
                                         -BIG, ALU.add, ALU.max).then_inc(max_done.sem, 1)

                def difs(q, r):
                    dve.wait_ge(max_t_done.sem, max_t_done.at(p, q, r))
                    if past(q, r, 2):
                        dve.wait_ge(exp_done.sem, exp_done.at(p, q, r, 2))
                    n = GC * heads
                    tt(dif[:, r % 2, 0:n], logit[:, r % 2, 0:n], bank(3)[:, 0:n], ALU.subtract).then_inc(dif_done.sem, 1)

                def messages(q, r):
                    dve.wait_ge(exp_done.sem, exp_done.at(p, q, r))
                    if past(q, r, 2):
                        dve.wait_ge(sum_done.sem, sum_done.at(p, q, r, 2))
                    s = r % 2
                    m = msg[:, s, 0:GC * W].rearrange("p (k h c) -> p k h c", k=GC, h=heads)
                    e = wgt[:, s, 0:GC * heads].rearrange("p (k h c) -> p k h c", k=GC, h=heads)
                    v.tensor_copy(m[:, :, :, nc_:nc_ + 1], e)
                    if p == "attn":
                        i = tt(m[:, :, :, 0:nc_], row_b[:, r, :, D:2 * D].rearrange("p k (h c) -> p k h c", h=heads),
                               bc(e, [P, GC, heads, nc_]), ALU.mult)
                    else:
                        i = tt(m[:, :, :, 0:nc_],
                               bc(row_b[:, r, :, 0:D].rearrange("p k (h c) -> p k h c", h=1), [P, GC, heads, D]),
                               bc(e, [P, GC, heads, nc_]), ALU.mult)
                    i.then_inc(msg_done.sem, 1)

                if p == "gcn":
                    over_groups(dve, [(0, diags), (1, same)])
                elif weighted:
                    over_groups(dve, [(4, messages), (3, maxima), (2, logits), (3, difs)])

                c = chains["x_" + p]
                if weighted:
                    for h in range(heads):
                        dve.wait_ge(s_steps, c.at(f"d{h}"))
                        for t in range(QA):
                            i = ts(gw[:, t, :], ps[0:CQ, BANK:BANK + CH], last_c[:, t, h:h + 1], 0.0,
                                   ALU.subtract, ALU.max)
                        i.then_inc(s_steps, 1)
                        for t in range(QA):
                            dve.wait_ge(s_steps, c.at(f"g{h}_{t}"))
                            tt(gw[:, t, :], gw[:, t, :], carries[:, t, :], ALU.mult).then_inc(s_steps, 1)

            edge_pass("gcn")
            c = chains["n_gcn"]
            av = agg_of("gcn")
            with dve.Fori(0, NJ) as j:
                dve.wait_ge(s_steps, c.at("an", j))
                tt(a_n[:, :, 0:D], tiles(av, j), nb(cols(norm[:, 1, :], j)), ALU.mult).then_inc(s_steps, 1)
                lin = ps[:, 8 * P:13 * P].rearrange("p (k c) -> p k c", k=JT)
                dve.wait_ge(s_steps, c.at("y", j))
                tt(Y, lin, fb(rows["L0_gnn_b"][:, :]), ALU.add).then_inc(s_steps, 1)
                norm_steps(c, j, "a")
                dve.wait_ge(s_steps, c.at("an2", j))
                tt(Y, Y, nb(st[:, 3, :]), ALU.mult).then_inc(s_steps, 1)
                dve.wait_ge(s_steps, c.at("ag", j))
                tt(Y, Y, fb(rows["L0_gnn_gamma"][:, :]), ALU.mult).then_inc(s_steps, 1)
                dve.wait_ge(s_steps, c.at("ab", j))
                tt(Y, Y, fb(rows["L0_gnn_beta"][:, :]), ALU.add).then_inc(s_steps, 1)
                dve.wait_ge(s_steps, c.at("ar", j))
                stt(Y, Y, 0.0, tiles(h_sb, j), ALU.max, ALU.add).then_inc(s_steps, 1)
                add_to_x(c, j, "ax")
                norm_steps(c, j, "b")
                relu_norm(c, j)
                q_v = ps[:, 2 * BANK:(2 + JT) * BANK].rearrange("p (k c) -> p k c", k=JT)[:, :, 0:3 * D]
                dve.wait_ge(s_steps, c.at("tab", j))
                tt(tab[:, :, :], q_v, fb(b_qkv[:, :], 3 * D), ALU.add).then_inc(s_steps, 1)

            def weights_of(c, j, p):
                heads, nc_, _ = WEIGHTED[p]
                av = agg_of(p).rearrange("p t (h c) -> p t h c", h=heads)
                a = av[:, bass.ds(j * JT, JT), :, :]
                r0 = rec[:, 0, 0:JT * heads].rearrange("p (k h c) -> p k h c", k=JT, h=heads)
                r1 = rec[:, 1, 0:JT * heads].rearrange("p (k h c) -> p k h c", k=JT, h=heads)
                dve.wait_ge(s_steps, c.at("den", j))
                ts(r0, a[:, :, :, nc_:nc_ + 1], 0.5, None, ALU.max).then_inc(s_steps, 1)
                dve.wait_ge(s_steps, c.at("rec", j))
                v.reciprocal(rec[:, 1, 0:JT * heads], rec[:, 0, 0:JT * heads]).then_inc(s_steps, 1)
                o = a_n[:, :, 0:heads * nc_].rearrange("p k (h c) -> p k h c", h=heads)
                dve.wait_ge(s_steps, c.at("an", j))
                tt(o, a[:, :, :, 0:nc_], bc(r1, [P, JT, heads, nc_]), ALU.mult).then_inc(s_steps, 1)

            def affine(c, j, pre, gamma, beta):
                dve.wait_ge(s_steps, c.at(pre + "n2", j))
                tt(Y, Y, nb(st[:, 3, :]), ALU.mult).then_inc(s_steps, 1)
                dve.wait_ge(s_steps, c.at(pre + "g", j))
                tt(Y, Y, fb(rows[gamma][:, :]), ALU.mult).then_inc(s_steps, 1)
                dve.wait_ge(s_steps, c.at(pre + "b", j))
                tt(Y, Y, fb(rows[beta][:, :]), ALU.add).then_inc(s_steps, 1)

            edge_pass("attn")
            c = chains["n_attn"]
            with dve.Fori(0, NJ) as j:
                weights_of(c, j, "attn")
                dve.wait_ge(s_steps, c.at("y", j))
                tt(Y, lin, a_n[:, :, 0:D], ALU.add).then_inc(s_steps, 1)
                dve.wait_ge(s_steps, c.at("y2", j))
                tt(Y, Y, fb(rows["L1_gnn_bskip"][:, :]), ALU.add).then_inc(s_steps, 1)
                dve.wait_ge(s_steps, c.at("y3", j))
                tt(Y, Y, hs[:, :, :], ALU.add).then_inc(s_steps, 1)
                norm_steps(c, j, "a")
                affine(c, j, "a", "L1_gnn_g1", "L1_gnn_b1")
                ffn = ps[:, 0:JT * P].rearrange("p (k c) -> p k c", k=JT)
                dve.wait_ge(s_steps, c.at("z", j))
                tt(Y, Y, ffn, ALU.add).then_inc(s_steps, 1)
                dve.wait_ge(s_steps, c.at("z2", j))
                tt(Y, Y, fb(rows["L1_gnn_bf2"][:, :]), ALU.add).then_inc(s_steps, 1)
                norm_steps(c, j, "b")
                affine(c, j, "b", "L1_gnn_g2", "L1_gnn_b2")
                add_to_x(c, j, "bx")
                norm_steps(c, j, "c")
                relu_norm(c, j)
                el_v = bank(2)[:, 0:JT * 2 * H2].rearrange("p (k l h) -> p k l h", k=JT, l=2)
                dve.wait_ge(s_steps, c.at("el_s", j))
                v.tensor_copy(tab[:, :, D:D + H2], el_v[:, :, 0, :]).then_inc(s_steps, 1)
                dve.wait_ge(s_steps, c.at("er_s", j))
                v.tensor_copy(er_n[:, :, :], el_v[:, :, 1, :]).then_inc(s_steps, 1)

            edge_pass("gat1")
            c = chains["n_gat1"]
            wide = ps[:, 0:JT * BANK].rearrange("p (k c) -> p k c", k=JT)
            with dve.Fori(0, NJ) as j:
                weights_of(c, j, "gat1")
                W3 = H2 * D
                dve.wait_ge(s_steps, c.at("z", j))
                tt(tab[:, :, 0:W3], wide[:, :, 0:W3], fb(bias1[:, :], W3), ALU.add).then_inc(s_steps, 1)
                dve.wait_ge(s_steps, c.at("min", j))
                ts(a_n[:, :, :], tab[:, :, 0:W3], 0.0, None, ALU.min).then_inc(s_steps, 1)
                dve.wait_ge(s_steps, c.at("elu", j))
                stt(a_n[:, :, :], tab[:, :, 0:W3], 0.0, a_n[:, :, :], ALU.max, ALU.add).then_inc(s_steps, 1)
                dve.wait_ge(s_steps, c.at("elu2", j))
                ts(a_n[:, :, :], a_n[:, :, :], -1.0, None, ALU.add).then_inc(s_steps, 1)
                dve.wait_ge(s_steps, c.at("tab", j))
                v.tensor_copy(tab[:, :, 0:D + 1], wide[:, :, 0:D + 1]).then_inc(s_steps, 1)

            edge_pass("gat2")
            c = chains["n_gat2"]
            with dve.Fori(0, NJ) as j:
                weights_of(c, j, "gat2")
                dve.wait_ge(s_steps, c.at("y", j))
                tt(Y, a_n[:, :, 0:D], tiles(h_sb, j), ALU.add).then_inc(s_steps, 1)
                dve.wait_ge(s_steps, c.at("y2", j))
                tt(Y, Y, fb(rows["L2_gnn_bias2"][:, :]), ALU.add).then_inc(s_steps, 1)
                add_to_x(c, j, "yx")
                norm_steps(c, j, "a")
                relu_norm(c, j)
                split_dve(c, j)

            for i, p in enumerate(("sage1", "sage2")):
                edge_pass(p)
                c = chains["n_" + p]
                av = agg_of(p)
                sage = ps[:, 4 * BANK:4 * BANK + JT * P].rearrange("p (k c) -> p k c", k=JT)
                with dve.Fori(0, NJ) as j:
                    dve.wait_ge(s_steps, c.at("an", j))
                    tt(a_n[:, :, 0:D], tiles(av, j), nb(cols(cnt_r[:, :], j)), ALU.mult).then_inc(s_steps, 1)
                    dve.wait_ge(s_steps, c.at("ya", j))
                    tt(Y, sage, fb(bn_a[:, i, :]), ALU.mult).then_inc(s_steps, 1)
                    dve.wait_ge(s_steps, c.at("yb", j))
                    tt(Y, Y, fb(bn_b[:, i, :]), ALU.add).then_inc(s_steps, 1)
                    if p == "sage1":
                        dve.wait_ge(s_steps, c.at("hs", j))
                        ts(hs[:, :, :], Y, 0.0, None, ALU.max).then_inc(s_steps, 1)
                        split_dve(c, j)
                    else:
                        dve.wait_ge(s_steps, c.at("yx", j))
                        tt(tiles(x_sb, j), Y, tiles(x_sb, j), ALU.add).then_inc(s_steps, 1)


_INS = ["x", "src", "dst", "edge_attr_64", "L0_gnn_W", "L0_gnn_b", "L0_gnn_gamma", "L0_gnn_beta", "L1_gnn_Wq",
        "L1_gnn_bq", "L1_gnn_Wk", "L1_gnn_bk", "L1_gnn_Wv", "L1_gnn_bv", "L1_gnn_We", "L1_gnn_Wskip",
        "L1_gnn_bskip", "L1_gnn_g1", "L1_gnn_b1", "L1_gnn_g2", "L1_gnn_b2", "L1_gnn_Wf1", "L1_gnn_bf1",
        "L1_gnn_Wf2", "L1_gnn_bf2", "L2_gnn_fc1_w", "L2_gnn_attn_l1", "L2_gnn_attn_r1", "L2_gnn_res1_w",
        "L2_gnn_bias1", "L2_gnn_fc2_w", "L2_gnn_attn_l2", "L2_gnn_attn_r2", "L2_gnn_res2_w", "L2_gnn_bias2",
        "L3_gnn_Wl0", "L3_gnn_Wr0", "L3_gnn_b0", "L3_gnn_g0", "L3_gnn_be0", "L3_gnn_rm0", "L3_gnn_rv0",
        "L3_gnn_Wl1", "L3_gnn_Wr1", "L3_gnn_b1", "L3_gnn_g1", "L3_gnn_be1", "L3_gnn_rm1", "L3_gnn_rv1"]


def kernel(**inputs):
    import numpy as _np
    import concourse.bacc as _bacc
    from concourse.bass_utils import run_bass_kernel_spmd as _run

    nc = _bacc.Bacc("TRN2", target_bir_lowering=False, num_devices=1)
    arrays, args = {}, {}
    for name in _INS:
        a = _np.ascontiguousarray(inputs[name])
        arrays[f"in_{name}"] = a
        args[name] = nc.dram_tensor(f"in_{name}", a.shape, mybir.dt.from_np(a.dtype), kind="ExternalInput").ap()
    out = nc.dram_tensor("out_x", (N, D), F32, kind="ExternalOutput").ap()
    gnn_stack_kernel(nc, out, **args)
    return _run(nc, [arrays], core_ids=[0]).results[0]["out_x"]
```

```python
from contextlib import ExitStack

import concourse.bass as bass
import numpy as np
from concourse import mybir

F32 = mybir.dt.float32
BF16 = mybir.dt.bfloat16
I32 = mybir.dt.int32
ALU = mybir.AluOpType
ACT = mybir.ActivationFunctionType
AX_X = mybir.AxisListType.X

P = 128
N, E, D, ED = 3125, 50000, 128, 64
NT = -(-N // P)
NP = NT * P
JT = 5
NJ = NT // JT
GC = 4
NG = -(-E // (P * GC))
CH = NG * GC
EP = CH * P
QA = 4
CQ = CH // QA
H1, C1 = 8, 16
H2 = 3
FF = 4 * D
BIG = 1.0e30
EPS = 1e-5
BANK = 512
UNROLL = 4
PASSES = ("gcn", "attn", "gat1", "gat2", "sage1", "sage2")
WEIGHTED = {"attn": (H1, C1, 0.25), "gat1": (H2, D, 1.0), "gat2": (1, D, 1.0)}
assert NT % JT == 0 and NG % 2 == 0 and CH % QA == 0 and CQ <= P


def width(name):
    return WEIGHTED[name][0] * (WEIGHTED[name][1] + 1) if name in WEIGHTED else D


class GroupSignal:

    def __init__(self, sem, passes):
        self.sem = sem
        self.base = {p: NG * i for i, p in enumerate(passes)}

    def at(self, p, q, r, back=0):
        return self.base[p] + 4 * q + (r - back + 1)


class RingSignal:

    def __init__(self, sems, passes, dmas=1):
        self.sems, self.ring, self.each = sems, len(sems), 16 * dmas
        self.base, self.total = {}, [0] * len(sems)
        for p in passes:
            self.base[p] = list(self.total)
            for g in range(NG):
                self.total[g % self.ring] += self.each

    def of(self, r):
        return self.sems[r % self.ring]

    def at(self, p, q, r, before=0):
        use = q * (UNROLL // self.ring) + (r // self.ring + 1 - before)
        return use * self.each + self.base[p][r % self.ring]


def past(q, r, n):
    return not isinstance(q, int) or 4 * q + r >= n


class Steps:

    def __init__(self, names, base, turns=1):
        assert len(set(names)) == len(names), names
        self.base, self.n = base, len(names)
        self.index = {name: i for i, name in enumerate(names)}
        self.end = base + turns * self.n

    def at(self, name, turn=0):
        return self.base + self.index[name] + turn * self.n


def over_groups(eng, stages):
    last = max(lag for lag, _ in stages)

    def peeled(n):
        for lag, what in stages:
            if 0 <= n - lag < NG:
                what((n - lag) // UNROLL, (n - lag) % UNROLL)

    for n in range(2 * UNROLL):
        peeled(n)
    with eng.Fori(2, NG // UNROLL) as i:
        for r in range(UNROLL):
            for lag, what in stages:
                what(i + (r - lag) // UNROLL, (r - lag) % UNROLL)
    for n in range(NG // UNROLL * UNROLL, NG + last):
        peeled(n)


LN = ("mean", "neg", "cent", "sq", "var", "vare", "sd", "rs")


def ln(pre):
    return [pre + s for s in LN]


def gnn_stack_kernel(nc, out, x, src, dst, edge_attr_64, **w):
    ctx = ExitStack()
    with ctx:
        def sb(name, shape, dt=F32):
            return ctx.enter_context(nc.sbuf_tensor(name, shape, dt))

        def sem(name):
            return ctx.enter_context(nc.semaphore(name))

        def hbm(name, shape, dt=F32):
            return nc.dram_tensor(name, shape, dt, kind="Internal").ap()

        esrc = hbm("esrc", [EP], I32)
        edst = hbm("edst", [P + EP], I32)
        attr_given = hbm("attr_given", [EP, ED])
        eattr = hbm("eattr", [EP, ED])
        breaks = hbm("breaks", [EP + P])
        same_hbm = hbm("same_hbm", [NG, P, GC * P], BF16)
        q_tab = hbm("q_tab", [NP, D])
        row_tab = {"gcn": hbm("t_gcn", [NP, 3 * D], BF16), "attn": hbm("t_attn", [NP, 2 * D]),
                   "gat1": hbm("t_gat1", [NP, D + H2]), "gat2": hbm("t_gat2", [NP, D + 1]),
                   "sage1": hbm("t_sage1", [NP, 3 * D], BF16), "sage2": hbm("t_sage2", [NP, 3 * D], BF16)}
        starts = {"attn": hbm("starts_q", [EP + NP, D]), "gat1": hbm("starts_er1", [EP + NP, H2]),
                  "gat2": hbm("starts_er2", [EP + NP, 2])}
        er_tab = {"gat1": hbm("er_gat1", [NP, H2]), "gat2": hbm("er_gat2", [NP, 2])}
        ends = {p: hbm(f"ends_{p}", [EP + P, width(p)]) for p in PASSES}
        carry = {p: hbm(f"carry_{p}", [CH + P, width(p)]) for p in PASSES}

        ident = sb("ident", [P, P])
        ones = sb("ones", [P, P])
        upper = sb("upper", [P, P])
        iota_row = sb("iota_row", [P, P])
        iota_i = sb("iota_i", [P, P], I32)
        dst_f = sb("dst_f", [P, CH])
        src_i = sb("src_i", [P, CH], I32)
        dst_i = sb("dst_i", [P, CH], I32)
        start_i = sb("start_i", [P, NT], I32)
        node_i = sb("node_i", [P, NT], I32)
        first_i = sb("first_i", [CQ, QA], I32)
        last_dst = sb("last_dst", [CQ, QA])
        carries = sb("carries", [CQ, QA, CH])
        spread = sb("spread", [H1, H1, CQ])
        deg = sb("deg", [P, 2, NT])
        norm = sb("norm", [P, 2, NT])
        cnt_r = sb("cnt_r", [P, NT])
        tot = sb("tot", [P, NT])
        tot_x = sb("tot_x", [P, NT])
        cum = sb("cum", [P, NT])
        ntmp = sb("ntmp", [P, 9, NT])
        ntmp_i = sb("ntmp_i", [P, 5, NT], I32)
        end_i = sb("end_i", [P, NT], I32)
        carry_i = sb("carry_i", [P, NT], I32)
        zrow = sb("zrow", [P, 390])
        pad_i = sb("pad_i", [P, 4], I32)

        def row_of(key, n=D):
            return sb("r_" + key, [P, n])
        rows = {k: row_of(k) for k in ("L0_gnn_b", "L0_gnn_gamma", "L0_gnn_beta", "L1_gnn_bskip", "L1_gnn_g1",
                                       "L1_gnn_b1", "L1_gnn_g2", "L1_gnn_b2", "L1_gnn_bf2", "L2_gnn_bias2",
                                       "L3_gnn_b0", "L3_gnn_g0", "L3_gnn_be0", "L3_gnn_rm0", "L3_gnn_rv0",
                                       "L3_gnn_b1", "L3_gnn_g1", "L3_gnn_be1", "L3_gnn_rm1", "L3_gnn_rv1")}
        b_qkv = row_of("b_qkv", 3 * D)
        bias1 = row_of("bias1", H2 * D)
        w0 = sb("w0", [P, D])
        w_qkv = sb("w_qkv", [P, 3 * D])
        w_skip = sb("w_skip", [P, D])
        w_e = sb("w_e", [ED, D])
        w_f1 = sb("w_f1", [P, FF])
        b_f1 = sb("b_f1", [P, FF // P])
        w_f2 = sb("w_f2", [P, FF // P, D])
        a1 = sb("a1", [P, 2, H2])
        a2 = sb("a2", [P, 2])
        fc1_t = sb("fc1_t", [P, H2, D])
        res1_t = sb("res1_t", [P, H2, D])
        u1 = sb("u1", [P, 2, H2])
        w2 = sb("w2", [P, H2, 2 * D + 2])
        sage_t = sb("sage_t", [P, 4, D])
        bn_a = sb("bn_a", [P, 2, D])
        bn_b = sb("bn_b", [P, 2, D])

        x_sb = sb("x_sb", [P, NT, D])
        h_sb = sb("h_sb", [P, NT, D])
        y = sb("y", [P, JT, D])
        sq = sb("sq", [P, JT, D])
        hs = sb("hs", [P, JT, D])
        st = sb("st", [P, 5, JT])
        falls = sb("falls", [CQ, 1])
        unsorted_i = sb("unsorted_i", [1, 1], I32)
        rec = sb("rec", [P, 2, JT * H1])
        er_all = {"gat1": sb("er_all1", [P, NT, H2]), "gat2": sb("er_all2", [P, NT, 2])}
        er_c = sb("er_c", [P, CH, H2])

        src_ix = sb("src_ix", [P, UNROLL, GC], I32)
        def carve(t, items, start=0):
            at, got = start, {}
            for k, (parts, dims, dt) in items.items():
                n = int(np.prod(dims)) * (2 if dt == BF16 else 4) // 4
                v = t[0:parts, at:at + n]
                v = v if dt == F32 else v.bitcast(dt)
                letters = "abcd"[:len(dims)]
                got[k] = v.rearrange(f"p ({' '.join(letters)}) -> p {' '.join(letters)}", **dict(zip(letters, dims)))
                at += n
            return got

        agg = sb("agg", [P, GC * D * (2 * UNROLL + UNROLL + 2) + 2 * GC * H2 * (D + 1)])
        early = carve(agg, {"row_b": (P, (UNROLL, GC, 2 * D), F32), "q_b": (P, (UNROLL, GC, D), F32),
                            "msg": (P, (2, GC * H2 * (D + 1)), F32), "diag": (P, (2, GC, P), F32)})
        row_b, q_b, msg, diag = (early[k] for k in ("row_b", "q_b", "msg", "diag"))
        row_s = carve(agg, {"row_s": (P, (UNROLL, GC * 4 * D), BF16)})["row_s"]
        first_rows = carve(agg, {"first": (CQ, (QA, D), F32)})["first"]
        q_all = carve(agg, {"q_all": (P, (NT, D), F32)}, 2 * NT * D)["q_all"]
        er_r = carve(agg, {"er_r": (CQ, (QA, P * H2), F32)}, UNROLL * GC * 3 * D)["er_r"]
        prep = carve(agg, {k: (CQ, (QA, P), dt) for k, dt in (("src_r", I32), ("dst_r", I32), ("prev_r", I32),
                                                              ("src_rf", F32), ("dst_rf", F32), ("brk_r", F32))}
                     | {"after": (CQ, (CH,), F32), "after_i": (CQ, (CH,), I32), "part_i": (P, (CH,), I32),
                        "lo_f": (P, (2, CH), F32), "hi_f": (P, (2, CH), F32), "raw": (P, (16, D), F32),
                        "hot_hi": (P, (4, UNROLL, NT), BF16)})
        src_r, dst_r, prev_r, src_rf, dst_rf, brk_r = (prep[k] for k in ("src_r", "dst_r", "prev_r", "src_rf", "dst_rf", "brk_r"))
        after, after_i, part_i, lo_f, hi_f = (prep[k] for k in ("after", "after_i", "part_i", "lo_f", "hi_f"))
        raw, hot_hi = (prep[k] for k in ("raw", "hot_hi"))
        at_b = sb("at_b", [P, UNROLL, GC, ED])
        hot_lo = carve(at_b[:, :, :, :].rearrange("p r k c -> p (r k c)"), {"hot_lo": (P, (4, UNROLL, P), BF16)})["hot_lo"]
        brk_b = sb("brk_b", [H1, UNROLL, GC * P + 1])
        same_b = sb("same_b", [P, UNROLL, GC, P], BF16)
        prod = sb("prod", [P, GC, D])
        z_b = sb("z_b", [P, GC, H2])
        logit = sb("logit", [P, 2, GC * H1])
        fwd = sb("fwd", [H1, 2, GC * P])
        mx = sb("mx", [H1, 2, GC * P])
        dif = sb("dif", [P, 2, GC * H1])
        wgt = sb("wgt", [P, 2, GC * H1])
        first_m = sb("first_m", [H1, CH])
        last_m = sb("last_m", [H1, CH])
        last_c = sb("last_c", [CQ, QA, H1])

        scratch = sb("scratch", [P, 2 * GC * H2 * (D + 1) + (UNROLL + 2) * GC * P + QA * CH + 2 * QA * H2 * (D + 1)])
        node = carve(scratch, {
            "a_n": (P, (JT, H2 * D), F32), "a_t": (P, (JT * H2 * P,), F32), "h_t": (P, (JT * P,), F32),
            "hid": (P, (FF // P, JT * P), F32), "tab": (P, (JT, 3 * D), F32), "tab_b": (P, (JT, 3, D), BF16)})
        a_n, a_t, h_t, hid, tab, tab_b = (node[k] for k in ("a_n", "a_t", "h_t", "hid", "tab", "tab_b"))
        sb_at = [0]

        def edge_part(parts, *dims):
            n = int(np.prod(dims))
            v = scratch[0:parts, sb_at[0]:sb_at[0] + n]
            sb_at[0] += n
            letters = "abcd"[:len(dims)]
            return v.rearrange(f"p ({' '.join(letters)}) -> p {' '.join(letters)}", **dict(zip(letters, dims)))

        o_b = edge_part(P, 2, GC * H2 * (D + 1))
        same_f = edge_part(P, UNROLL, GC, P)
        at_t = edge_part(ED, 2, GC * P)
        gw = edge_part(CQ, QA, CH)
        z_rows = edge_part(CQ, QA, H2 * (D + 1))
        r_rows = edge_part(CQ, QA, H2 * (D + 1))

        by_block = carve(h_sb[:, :, :].rearrange("p t c -> p (t c)"), {
            "src_k": (P, (CH,), I32), "dst_k": (P, (CH,), I32), "dst_kf": (P, (CH,), F32), "rank": (P, (CH,), F32),
            "rank_i": (P, (3, CH), I32), "pay": (P, (5, GC), I32), "attr_k": (P, (GC, ED), F32)})
        src_k, dst_k, dst_kf, rank = (by_block[k] for k in ("src_k", "dst_k", "dst_kf", "rank"))
        rank_i, pay, attr_k = (by_block[k] for k in ("rank_i", "pay", "attr_k"))
        by_node = carve(scratch, {k: (P, (NP,), F32) for k in ("nodes", "held", "run")})
        nodes, held, run = (by_node[k] for k in ("nodes", "held", "run"))

        ps = ctx.enter_context(nc.psum_tensor("ps", [P, 8 * BANK], F32))

        def bank(b, n=1):
            return ps[:, b * BANK:(b + n) * BANK]

        def max_ps(p):
            return bank(1 if p == "gat1" else 6)[:, 0:GC * H1]

        s_setup = sem("s_setup")
        s_load = sem("s_load")
        s_store = sem("s_store")
        s_steps = sem("s_steps")
        s_hot = sem("s_hot")
        s_hist = sem("s_hist")
        wp = tuple(WEIGHTED)
        rows_in = RingSignal([sem(f"rows_in{i}") for i in range(4)], PASSES, GC)
        starts_in = RingSignal([sem(f"starts_in{i}") for i in range(4)], ("attn",))
        attr_in = RingSignal([sem(f"attr_in{i}") for i in range(4)], ("attn",))
        brk_in = RingSignal([sem(f"brk_in{i}") for i in range(4)], wp)
        same_in = RingSignal([sem(f"same_in{i}") for i in range(4)], PASSES[1:])
        same_out = RingSignal([sem(f"same_out{i}") for i in range(4)], ("gcn",))
        ends_out = RingSignal([sem(f"ends_out{i}") for i in range(2)], PASSES)
        ix_done = GroupSignal(sem("ix_done"), PASSES)
        diag_done = GroupSignal(sem("diag_done"), ("gcn",))
        bcast_done = GroupSignal(sem("bcast_done"), ("gcn",))
        same_done = GroupSignal(sem("same_done"), ("gcn",))
        attr_t_done = GroupSignal(sem("attr_t_done"), ("attn",))
        attr_sb_done = GroupSignal(sem("attr_sb_done"), ("attn",))
        e_done = GroupSignal(sem("e_done"), ("attn",))
        kve_done = GroupSignal(sem("kve_done"), ("attn",))
        prod_done = GroupSignal(sem("prod_done"), wp)
        logit_done = GroupSignal(sem("logit_done"), wp)
        logit_t_done = GroupSignal(sem("logit_t_done"), wp)
        fwd_done = GroupSignal(sem("fwd_done"), wp)
        max_done = GroupSignal(sem("max_done"), wp)
        max_t_done = GroupSignal(sem("max_t_done"), wp)
        kept_done = GroupSignal(sem("kept_done"), wp)
        dif_done = GroupSignal(sem("dif_done"), wp)
        exp_done = GroupSignal(sem("exp_done"), wp)
        msg_done = GroupSignal(sem("msg_done"), wp)
        same_f_done = GroupSignal(sem("same_f_done"), wp)
        sum_done = GroupSignal(sem("sum_done"), PASSES)
        evac_done = GroupSignal(sem("evac_done"), PASSES)
        dst_done = GroupSignal(sem("dst_done"), wp)
        s_fill = sem("s_fill")
        FILLS = 16 * (7 + 1 + 1 + 2)
        s_sort_dve, s_sort_pool, s_sort_dma = sem("s_sort_dve"), sem("s_sort_pool"), sem("s_sort_dma")
        s_seed = sem("s_seed")
        s_gather = sem("s_gather")
        s_agg = sem("s_agg")

        chains = {}
        total = [0]

        def chain(key, names, turns=1):
            chains[key] = Steps(names, total[0], turns)
            total[0] = chains[key].end

        wt = [f"wt{i}" for i in range(16)]
        chain("prep", ["consts", "pads", "pads_out", "edges_in", "look_lt", "look_sum", "look_ps", "look_i",
                       "sort_in", "sort_hist", "sort_pre", "sort_pre_sb", "sort_tot", "sort_rank", "sort_move", "iota_f", "cast", "brk", "brk2",
                       "cols", "cols_i", "bits", "bits_f"])
        chain("hist", ["hist_start", "hist_read", "deg_max", "deg_sqrt", "deg_norm", "cnt_r", "cum_ps", "tot_sb", "tot_scan",
                       "tot_ex", "cum", "nz", "end", "end_ii", "end_xor", "end_f", "end_m", "end_i",
                       "blk_i", "blk_f", "start", "inner", "blk_m", "blk_n", "carry_i",
                       "st_i", "st_x", "st_f", "id_f", "st_d", "st_m", "st_n", "start_i",
                       "bnd_ps", "last_sb", "after_f", "carries", "carries2", "spread",
                       "wt_ps", "wt_sb", "bn_var", "bn_sd", "bn_rs", "bn_a", "bn_b1", "bn_b2", "bn_b3", "brk_out"])
        chain("n0", ["xl"] + ln("a") + ["hs", "hkeep", "hn", "hi", "r1", "mid", "r2", "lo", "store"], NJ)
        for p in PASSES:
            heads = [[f"{s}{h}" for s in ("fb", "d")] + [f"e{h}", f"g{h}", f"r{h}"]
                     for h in range(WEIGHTED[p][0])] if p in WEIGHTED else [["r"]]
            pre = ["lc_ps", "lc_sb"] if p in WEIGHTED else []
            if p in WEIGHTED:
                chain("s_" + p, ["starts", "firsts"] + (["er_in", "er_ps", "er_sb"] if p != "attn" else []))
            chain("x_" + p, ["z_in"] + pre + sum(heads, []) + ["r_sb", "r_out", "agg_ok"])
            chain("n_" + p, {
                "gcn": ["an", "T", "Ts", "lin", "y"] + ln("a") + ["an2", "ag", "ab", "ar", "ax", "xk"] + ln("b")
                       + ["hs", "hkeep", "T2", "T2s", "qkv", "tab", "qk", "store"],
                "attn": ["den", "rec", "an", "hl", "T", "Ts", "lin", "y", "y2", "y3"] + ln("a") + ["an2", "ag", "ab", "T2", "T2s",
                        "ffn1"] + [f"gelu{o}" for o in range(4)] + ["ffn2", "z", "z2"] + ln("b") + ["bn2", "bg", "bb", "bx", "xk"]
                        + ln("c") + ["hs", "hkeep", "T3", "T3s", "el", "tab", "el_s", "er_s", "store"],
                "gat1": ["den", "rec", "an", "hl", "T", "Ts", "T1s", "lin", "z", "min", "exp", "elu", "elu2", "T2", "T2s",
                         "feat", "tab", "er_s", "res", "store"],
                "gat2": ["den", "rec", "an", "y", "y2", "yx", "xk"] + ln("a") + ["hs", "hkeep", "hi", "r1", "mid", "r2", "lo", "store"],
                "sage1": ["an", "hl", "T", "Ts", "T1s", "lin", "ya", "yb", "hs", "hkeep", "hi", "r1", "mid", "r2", "lo", "store"],
                "sage2": ["an", "hl", "T", "Ts", "T1s", "lin", "ya", "yb", "yx"],
            }[p], NJ)

        s_apart_act, s_apart_dve, s_apart_pool, s_apart_sp, s_apart_pe = (
            sem(f"s_apart_{e}") for e in ("act", "dve", "pool", "sp", "pe"))

        def apart(eng, own):
            eng.sem_inc(own, 1)

        block = ctx.enter_context(nc.Block())

        def bc(ap, shape):
            return ap.to_broadcast(shape)

        def tiles(ap, j):
            return ap[:, bass.ds(j * JT, JT), :] if not isinstance(j, int) else ap[:, j * JT:(j + 1) * JT, :]

        def chunk_rows(ap, q, r):
            v = ap.rearrange("(q r k p) c -> q r k p c", r=2, k=GC, p=P)
            return v

        def agg_of(p):
            return agg[:, 0:NT * width(p)].rearrange("p (t c) -> p t c", t=NT)

        def grp(ap, q, r):
            g = q * UNROLL + r
            return ap[bass.ds(g, 1)] if not isinstance(g, int) else ap[g:g + 1]

        @block.sync
        def _(sp):
            loads = [0]

            def load(dst_ap, src_ap):
                sp.dma_start(dst_ap, src_ap).then_inc(s_load, 16)
                loads[0] += 16

            def landed():
                sp.wait_ge(s_load, loads[0])

            c = chains["prep"]
            for k, t in rows.items():
                if k != "L2_gnn_bias2":
                    load(t[:, :], w[k].rearrange("(a n) -> a n", a=1).to_broadcast([P, D]))
            for i, k in enumerate(("bq", "bk", "bv")):
                load(b_qkv[:, i * D:(i + 1) * D], w[f"L1_gnn_{k}"].rearrange("(a n) -> a n", a=1).to_broadcast([P, D]))
            load(bias1[:, :], w["L2_gnn_bias1"].rearrange("(a h) n -> a (h n)", a=1).to_broadcast([P, H2 * D]))
            load(rows["L2_gnn_bias2"][:, :], w["L2_gnn_bias2"].to_broadcast([P, D]))
            load(w0[:, :], w["L0_gnn_W"])
            for i, k in enumerate(("Wq", "Wk", "Wv")):
                load(w_qkv[:, i * D:(i + 1) * D], w[f"L1_gnn_{k}"])
            load(w_skip[:, :], w["L1_gnn_Wskip"])
            load(w_e[:, :], w["L1_gnn_We"])
            load(w_f1[:, :], w["L1_gnn_Wf1"])
            with nc.allow_non_contiguous_dma(reason="bias as columns"):
                load(b_f1[:, :], w["L1_gnn_bf1"].rearrange("(o p) -> p o", p=P))
            load(w_f2[:, :, :], w["L1_gnn_Wf2"].rearrange("(o p) n -> p o n", p=P))
            load(raw[:, 0:3, :], w["L2_gnn_fc1_w"].rearrange("(h p) n -> p h n", p=P))
            load(raw[:, 3:6, :], w["L2_gnn_res1_w"].rearrange("(h p) n -> p h n", p=P))
            load(raw[:, 6:9, :], w["L2_gnn_fc2_w"].rearrange("p (h n) -> p h n", h=H2))
            load(raw[:, 9:12, :], w["L2_gnn_res2_w"].rearrange("p (h n) -> p h n", h=H2))
            for i, k in enumerate(("Wl0", "Wr0", "Wl1", "Wr1")):
                load(raw[:, 12 + i, :], w[f"L3_gnn_{k}"])
            with nc.allow_non_contiguous_dma(reason="attention vectors as columns"):
                for i, k in enumerate(("attn_l", "attn_r")):
                    load(a1[:, i, :], w[f"L2_gnn_{k}1"].rearrange("h p -> p h"))
                    load(a2[:, i:i + 1], w[f"L2_gnn_{k}2"].rearrange("h p -> p h"))
            full = N // P * P
            load(x_sb[:, 0:NT - 1, :], x[0:full, :].rearrange("(t p) n -> p t n", p=P))
            sp.wait_ge(s_setup, 1)
            load(x_sb[0:N - full, NT - 1, :], x[full:N, :])
            load(esrc[0:E].rearrange("(a n) -> a n", a=16), src.rearrange("(a n) -> a n", a=16))
            load(edst[P:P + E].rearrange("(a n) -> a n", a=16), dst.rearrange("(a n) -> a n", a=16))
            sp.wait_ge(s_steps, c.at("pads_out"))
            load(edst[0:P].rearrange("(p a) -> p a", a=1), pad_i[:, 0:1])
            npad = EP - E
            for d_ap, o in ((esrc, 0), (edst, P)):
                load(d_ap[o + E:o + E + P].rearrange("(p a) -> p a", a=1), pad_i[:, 1:2])
                load(d_ap[o + E + P:o + EP].rearrange("(p a) -> p a", a=1), pad_i[0:npad - P, 1:2])
            tail = E % P
            load(eattr[E - tail:E - tail + P - tail, :], zrow[0:P - tail, 0:ED])
            load(eattr[EP - P:EP, :], zrow[:, 0:ED])
            for p in PASSES:
                load(ends[p][EP:EP + P, :], zrow[:, 0:width(p)])
                load(carry[p][CH:CH + P, :], zrow[:, 0:width(p)])
            landed()
            sp.sem_inc(s_steps, 1)
            sp.wait_ge(s_steps, c.at("edges_in"))
            load(src_r[:, :, :], esrc.rearrange("(a t e) -> t a e", a=QA, e=P))
            load(dst_r[:, :, :], edst[P:P + EP].rearrange("(a t e) -> t a e", a=QA, e=P))
            load(prev_r[:, :, :], edst[P - 1:P - 1 + EP].rearrange("(a t e) -> t a e", a=QA, e=P))
            landed()
            sp.sem_inc(s_steps, 1)
            sp.wait_ge(s_steps, chains["hist"].at("brk_out"))
            load(breaks[0:EP].rearrange("(a t e) -> t a e", a=QA, e=P), brk_r[:, :, :])
            load(breaks[EP:EP + P].rearrange("(p a) -> p a", a=1), ntmp[:, 8, 0:1])
            landed()
            sp.sem_inc(s_steps, 1)

            stored = [0]

            def stores(cc, j, pairs):
                sp.wait_ge(s_steps, cc.at("store", j))
                for d_ap, s_ap in pairs:
                    sp.dma_start(d_ap, s_ap).then_inc(s_store, 16)
                sp.wait_ge(s_store, stored[0] + 16 * len(pairs) + j * (16 * len(pairs)))
                sp.sem_inc(s_steps, 1)

            def node_rows(t, j):
                v = t.rearrange("(j k p) c -> j p k c", k=JT, p=P)
                return v[bass.ds(j, 1)].rearrange("j p k c -> (j p) k c")

            def table_loop(key, pairs):
                with sp.Fori(0, NJ) as j:
                    stores(chains[key], j, pairs(j))
                stored[0] += 16 * NJ * len(pairs(0))

            split = tab_b[:, :, :, :].rearrange("p k s c -> p k (s c)")
            table_loop("n0", lambda j: [(node_rows(row_tab["gcn"], j), split)])

            def edge_pass(p):
                c = chains["x_" + p]
                W = width(p)
                v_out = ends[p][0:EP, :].rearrange("(g k p) c -> g p k c", k=GC, p=P)
                v_attr = eattr.rearrange("(g k p) c -> g p k c", k=GC, p=P)

                if p in WEIGHTED:
                    cs = chains["s_" + p]
                    sp.wait_ge(s_steps, cs.at("firsts"))
                    load(starts[p][0:EP, :].rearrange("(a t e) c -> t a e c", a=QA, e=P)[:, :, P - 1, :],
                         first_rows[:, :, 0:starts[p].shape[1]])
                    landed()
                    sp.sem_inc(s_steps, 1)
                    if p != "attn":
                        sp.wait_ge(s_steps, cs.at("er_in"))
                        load(er_r[:, :, 0:P * starts[p].shape[1]],
                             starts[p][0:EP, :].rearrange("(a t e) c -> t a (e c)", a=QA, e=P))
                        landed()
                        sp.sem_inc(s_steps, 1)
                v_st = starts["attn"][0:EP, :].rearrange("(g k p) c -> g p k c", k=GC, p=P)

                def load_group(q, r):
                    if p in WEIGHTED:
                        if past(q, r, 4):
                            sp.wait_ge(max_done.sem, max_done.at(p, q, r, 4))
                        g = q * UNROLL + r
                        v = breaks[bass.ds(g * (GC * P), GC * P + 1)]
                        sp.dma_start(brk_b[0:WEIGHTED[p][0], r, :],
                                     v.rearrange("(a n) -> a n", a=1).to_broadcast([WEIGHTED[p][0], GC * P + 1]))\
                          .then_inc(brk_in.of(r), 16)
                        if past(q, r, 4):
                            sp.wait_ge(same_f_done.sem, same_f_done.at(p, q, r, 4))
                    elif p != "gcn":
                        if past(q, r, 4):
                            sp.wait_ge(sum_done.sem, sum_done.at(p, q, r, 4))
                    if p == "attn":
                        if past(q, r, 4):
                            sp.wait_ge(attr_t_done.sem, attr_t_done.at(p, q, r, 4))
                        if past(q, r, 4):
                            sp.wait_ge(dst_done.sem, dst_done.at(p, q, r, 4))
                        sp.dma_start(q_b[:, r, :, :], grp(v_st, q, r).rearrange("g p k c -> (g p) k c"))\
                          .then_inc(starts_in.of(r), 16)
                        sp.dma_start(at_b[:, r, :, :], grp(v_attr, q, r).rearrange("g p k c -> (g p) k c"))\
                          .then_inc(attr_in.of(r), 16)
                    if p != "gcn":
                        sp.dma_start(same_b[:, r, :, :],
                                     grp(same_hbm, q, r).rearrange("g p (k c) -> (g p) k c", k=GC))\
                          .then_inc(same_in.of(r), 16)

                def store_same(q, r):
                    sp.wait_ge(same_done.sem, same_done.at(p, q, r))
                    apart(sp, s_apart_sp)
                    sp.dma_start(grp(same_hbm, q, r).rearrange("g p (k c) -> (g p) k c", k=GC), same_b[:, r, :, :])\
                      .then_inc(same_out.of(r), 16)

                def store_ends(q, r):
                    sp.wait_ge(evac_done.sem, evac_done.at(p, q, r))
                    apart(sp, s_apart_sp)
                    sp.dma_start(grp(v_out, q, r).rearrange("g p k c -> (g p) k c"),
                                 o_b[:, r % 2, 0:GC * W].rearrange("p (k c) -> p k c", k=GC))\
                      .then_inc(ends_out.of(r), 16)

                if p == "gcn":
                    over_groups(sp, [(2, store_same), (3, store_ends)])
                    for r in range(4):
                        sp.wait_ge(same_out.sems[r], same_out.total[r])
                else:
                    over_groups(sp, [(0, load_group), (4 if p == "attn" else 5, store_ends)])
                for r in range(2):
                    sp.wait_ge(ends_out.of((NG - 1 - r) % 4), ends_out.at(p, (NG - 1 - r) // 4, (NG - 1 - r) % 4))
                sp.wait_ge(s_steps, c.at("z_in"))
                v = ends[p][0:EP, :].rearrange("(a t e) c -> t a e c", a=QA, e=P)
                load(z_rows[:, :, 0:W], v[:, :, 0, :])
                landed()
                sp.sem_inc(s_steps, 1)
                sp.wait_ge(s_steps, c.at("r_out"))
                load(carry[p][0:CH, :].rearrange("(a t) c -> t a c", a=QA), r_rows[:, :, 0:W])
                landed()
                sp.sem_inc(s_steps, 1)

            edge_pass("gcn")
            table_loop("n_gcn", lambda j: [(node_rows(q_tab, j), tab[:, :, 0:D]),
                                           (node_rows(row_tab["attn"], j), tab[:, :, D:3 * D])])
            edge_pass("attn")
            table_loop("n_attn", lambda j: [(node_rows(row_tab["gat1"], j), tab[:, :, 0:D + H2]),
                                            (node_rows(er_tab["gat1"], j), tiles(er_all["gat1"], j))])
            edge_pass("gat1")
            table_loop("n_gat1", lambda j: [(node_rows(row_tab["gat2"], j), tab[:, :, 0:D + 1]),
                                            (node_rows(er_tab["gat2"], j), tiles(er_all["gat2"], j))])
            edge_pass("gat2")
            table_loop("n_gat2", lambda j: [(node_rows(row_tab["sage1"], j), split)])
            edge_pass("sage1")
            table_loop("n_sage1", lambda j: [(node_rows(row_tab["sage2"], j), split)])
            edge_pass("sage2")
            sp.wait_ge(s_steps, chains["n_sage2"].end)
            load(out[0:full, :].rearrange("(t p) n -> p t n", p=P), x_sb[:, 0:NT - 1, :])
            load(out[full:N, :], x_sb[0:N - full, NT - 1, :])
            landed()

        @block.gpsimd
        def _(pool):
            c = chains["prep"]
            g = nc.gpsimd
            g.memset(x_sb[:, NT - 1, :], 0.0).then_inc(s_setup, 1)
            g.memset(ident[:, :], 0.0)
            g.memset(ones[:, :], 1.0)
            g.memset(zrow[:, :], 0.0)
            g.memset(ntmp[:, 8, :], -BIG)
            g.memset(upper[:, :], 1.0)
            g.memset(fwd[:, 1, :], -BIG)
            g.memset(pad_i[:, 0:1], -1)
            g.memset(pad_i[:, 1:2], NP - 1)
            g.memset(scratch[:, :], 0.0).then_inc(s_setup, 1)
            g.iota(node_i[:, :], pattern=[[P, NT]], base=0, channel_multiplier=1)
            g.iota(iota_i[:, :], pattern=[[1, P]], base=0, channel_multiplier=0)
            g.iota(after_i[:, :], pattern=[[1, CH]], base=0, channel_multiplier=-1).then_inc(s_steps, 1)
            pool.wait_ge(s_steps, c.at("pads"))
            g.affine_select(out=ident[:, :], in_=ident[:, :], compare_op=ALU.not_equal, fill=1.0, base=0,
                            pattern=[[-1, P]], channel_multiplier=1)
            g.affine_select(out=upper[:, :], in_=upper[:, :], compare_op=ALU.is_ge, fill=0.0, base=0,
                            pattern=[[1, P]], channel_multiplier=-1).then_inc(s_steps, 1)
            pool.wait_ge(s_steps, c.at("sort_in"))
            unsorted_pool = pool.value_load(unsorted_i[0:1, 0:1], min_val=0, max_val=EP)
            with pool.If(unsorted_pool > 0):
                pool.wait_ge(s_fill, FILLS)
                full = E // P * P
                pool.dma_start(attr_given[0:E, :], edge_attr_64).then_inc(s_sort_dma, 16)
                pool.dma_start(attr_given[E:E + P, :], zrow[:, 0:ED]).then_inc(s_sort_dma, 16)
                pool.dma_start(attr_given[E + P:EP, :], zrow[0:EP - E - P, 0:ED]).then_inc(s_sort_dma, 16)
                pool.dma_start(src_k[:, :], esrc.rearrange("(p i) -> p i", p=P)).then_inc(s_sort_dma, 16)
                pool.dma_start(dst_k[:, :], edst[P:P + EP].rearrange("(p i) -> p i", p=P)).then_inc(s_sort_dma, 16)
                g.iota(run[:, :].bitcast(I32), pattern=[[1, NP]], base=0, channel_multiplier=0).then_inc(s_sort_pool, 1)
                pool.wait_ge(s_sort_pool, 1)
                pool.wait_ge(s_sort_dma, 5 * 16)
            pool.sem_inc(s_steps, 1)
            pool.wait_ge(s_steps, c.at("sort_move"))
            with pool.If(unsorted_pool > 0):
                v_given = attr_given.rearrange("(p i g) c -> i p g c", p=P, g=GC)
                with pool.Fori(0, NG) as i:
                    edges = bass.ds(i * GC, GC)
                    g.tensor_copy(pay[:, 0, :], src_k[:, edges])
                    g.tensor_copy(pay[:, 1, :], dst_k[:, edges])
                    g.tensor_copy(pay[:, 2:5, :], rank_i[:, :, edges]).then_inc(s_sort_pool, 1)
                    pool.dma_start(attr_k[:, :, :], v_given[bass.ds(i, 1)].rearrange("i p g c -> (i p) g c"))\
                        .then_inc(s_sort_dma, 16)
                    pool.wait_ge(s_sort_pool, i + 2)
                    pool.wait_ge(s_sort_dma, i * (16 * (3 * GC + 1)) + 6 * 16)
                    apart(pool, s_apart_pool)
                    for k in range(GC):
                        for to, which, what in ((esrc.rearrange("(e a) -> e a", a=1), 2, pay[:, 0, k:k + 1]),
                                                (edst.rearrange("(e a) -> e a", a=1), 3, pay[:, 1, k:k + 1]),
                                                (eattr, 4, attr_k[:, k, :])):
                            g.indirect_dma_start(out=to, in_=what, in_offset=None, out_offset=bass.IndirectOffsetOnAxis(
                                ap=pay[:, which, k:k + 1], axis=0)).then_inc(s_sort_dma, 16)
                    pool.wait_ge(s_sort_dma, i * (16 * (3 * GC + 1)) + 16 * (6 + 3 * GC))
                    apart(pool, s_apart_pool)
                pool.dma_start(src_r[:, :, :], esrc.rearrange("(a t e) -> t a e", a=QA, e=P)).then_inc(s_sort_dma, 16)
                pool.dma_start(dst_r[:, :, :], edst[P:P + EP].rearrange("(a t e) -> t a e", a=QA, e=P))\
                    .then_inc(s_sort_dma, 16)
                pool.dma_start(prev_r[:, :, :], edst[P - 1:P - 1 + EP].rearrange("(a t e) -> t a e", a=QA, e=P))\
                    .then_inc(s_sort_dma, 16)
                pool.wait_ge(s_sort_dma, 16 * (5 + NG * (3 * GC + 1) + 3))
            pool.sem_inc(s_steps, 1)
            gathered = [0]

            def edge_pass(p):
                W = width(p)
                weighted = p in WEIGHTED
                dst_tab = q_tab if p == "attn" else er_tab.get(p)
                dst_all = q_all if p == "attn" else er_all.get(p)

                def indices(q, r):
                    if past(q, r, 4):
                        pool.wait_ge(rows_in.of(r), rows_in.at(p, q, r, 1))
                    apart(pool, s_apart_pool)
                    gg = q * UNROLL + r
                    s = bass.ds(gg * GC, GC)
                    g.tensor_copy(src_ix[:, r, :], src_i[:, s]).then_inc(ix_done.sem, 1)

                def gather(q, r):
                    pool.wait_ge(ix_done.sem, ix_done.at(p, q, r))
                    if weighted:
                        if past(q, r, 4):
                            pool.wait_ge(msg_done.sem, msg_done.at(p, q, r, 4))
                    else:
                        if past(q, r, 4):
                            pool.wait_ge(sum_done.sem, sum_done.at(p, q, r, 4))
                    apart(pool, s_apart_pool)
                    for k in range(GC):
                        if weighted:
                            o = row_b[:, r, k, 0:row_tab[p].shape[1]]
                        else:
                            o = row_s[:, r, k * 3 * D:(k + 1) * 3 * D]
                        g.indirect_dma_start(out=o, out_offset=None, in_=row_tab[p],
                                             in_offset=bass.IndirectOffsetOnAxis(ap=src_ix[:, r, k:k + 1], axis=0))\
                         .then_inc(rows_in.of(r), 16)

                before = chains["n0"].end if p == "gcn" else chains["n_" + PASSES[PASSES.index(p) - 1]].end
                pool.wait_ge(s_steps, before)
                if weighted:
                    c2 = dst_tab.shape[1]
                    for t in range(NT):
                        g.indirect_dma_start(out=starts[p], in_=dst_all[:, t, :], in_offset=None,
                                             out_offset=bass.IndirectOffsetOnAxis(ap=start_i[:, t:t + 1], axis=0))\
                         .then_inc(s_gather, 16)
                    for a in range(QA):
                        g.indirect_dma_start(out=first_rows[:, a, 0:c2], out_offset=None, in_=dst_tab,
                                             in_offset=bass.IndirectOffsetOnAxis(ap=first_i[:, a:a + 1], axis=0))\
                         .then_inc(s_gather, 16)
                    gathered[0] += 16 * (NT + QA)
                    pool.wait_ge(s_gather, gathered[0])
                    pool.sem_inc(s_steps, 1)
                    pool.wait_ge(s_steps, chains["s_" + p].at("firsts") + 1)
                over_groups(pool, [(0, indices), (1, gather)])
                c = chains["x_" + p]
                pool.wait_ge(s_steps, c.base + 1)
                av = agg_of(p)
                for t in range(NT):
                    g.indirect_dma_start(out=av[:, t, :], out_offset=None, in_=ends[p],
                                         in_offset=bass.IndirectOffsetOnAxis(ap=end_i[:, t:t + 1], axis=0))\
                     .then_inc(s_gather, 16)
                gathered[0] += 16 * NT
                pool.wait_ge(s_steps, c.at("agg_ok"))
                pool.wait_ge(s_gather, gathered[0])
                for t in range(NT):
                    g.indirect_dma_start(out=av[:, t, :], out_offset=None, in_=carry[p],
                                         in_offset=bass.IndirectOffsetOnAxis(ap=carry_i[:, t:t + 1], axis=0),
                                         compute_op=ALU.add).then_inc(s_gather, 16)
                gathered[0] += 16 * NT
                pool.wait_ge(s_gather, gathered[0])
                pool.sem_inc(s_steps, 1)

            for p in PASSES:
                edge_pass(p)

        @block.scalar
        def _(act):
            a = nc.scalar

            def copy(o, i):
                return a.activation(o, i, ACT.Copy)

            act.wait_ge(s_setup, 2)
            act.wait_ge(s_steps, chains["prep"].at("sort_in"))
            for t, parts in ((starts["attn"], 7), (starts["gat1"], 1), (starts["gat2"], 1)):
                n = EP * t.shape[1] // P // parts
                flat = t[0:EP, :].rearrange("(b p e) c -> b p (e c)", b=parts, p=P)
                for b in range(parts):
                    act.dma_start(flat[b], scratch[:, 0:n]).then_inc(s_fill, 16)
            full = E // P * P
            tail = E - full
            act.dma_start(eattr[0:full, :].rearrange("(t p) c -> t p c", p=P),
                          edge_attr_64[0:full, :].rearrange("(t p) c -> t p c", p=P)[:, ::-1, :]).then_inc(s_fill, 16)
            act.dma_start(eattr[full + P - tail:full + P, :].rearrange("t (s c) -> s t c", s=2),
                          edge_attr_64[full:E, :].rearrange("t (s c) -> s t c", s=2)[:, ::-1, :]).then_inc(s_fill, 16)
            c = chains["hist"]
            act.wait_ge(s_steps, c.at("deg_sqrt"))
            a.activation(norm[:, :, :], norm[:, :, :], ACT.Sqrt).then_inc(s_steps, 1)
            def wt_copy():
                copy(fc1_t[:, :, :], ps[:, 0:384].rearrange("p (h n) -> p h n", h=3))
                copy(res1_t[:, :, :], bank(1)[:, 0:384].rearrange("p (h n) -> p h n", h=3))
                copy(w2[:, :, 0:D], bank(2)[:, 0:384].rearrange("p (h n) -> p h n", h=3))
                copy(w2[:, :, D + 2:2 * D + 2], bank(3)[:, 0:384].rearrange("p (h n) -> p h n", h=3))
                copy(sage_t[:, :, :], bank(4)[:, :].rearrange("p (h n) -> p h n", h=4))
                copy(u1[:, :, :], bank(5)[:, 0:6].rearrange("p (l h) -> p l h", l=2))
                return copy(w2[:, :, D:D + 2], bank(6)[:, 0:6].rearrange("p (h l) -> p h l", l=2))

            act.wait_ge(s_steps, c.at("wt_sb"))
            wt_copy().then_inc(s_steps, 1)
            act.wait_ge(s_steps, c.at("bn_sd"))
            a.activation(bn_a[:, :, :], bn_a[:, :, :], ACT.Sqrt).then_inc(s_steps, 1)

            def ln_act(c, j, pre):
                act.wait_ge(s_steps, c.at(pre + "sq", j))
                a.activation(sq[:, :, :], y[:, :, :], ACT.Square).then_inc(s_steps, 1)
                act.wait_ge(s_steps, c.at(pre + "sd", j))
                a.activation(st[:, 2, :], st[:, 1, :], ACT.Sqrt).then_inc(s_steps, 1)

            def keep_h(c, j):
                act.wait_ge(s_steps, c.at("hkeep", j))
                apart(act, s_apart_act)
                copy(tiles(h_sb, j), hs[:, :, :]).then_inc(s_steps, 1)

            def load_h(c, j):
                act.wait_ge(s_steps, c.at("hl", j))
                apart(act, s_apart_act)
                copy(hs[:, :, :], tiles(h_sb, j)).then_inc(s_steps, 1)

            def split_act(c, j):
                act.wait_ge(s_steps, c.at("hi", j))
                copy(tab_b[:, :, 0, :], hs[:, :, :]).then_inc(s_steps, 1)
                act.wait_ge(s_steps, c.at("mid", j))
                copy(tab_b[:, :, 1, :], sq[:, :, :]).then_inc(s_steps, 1)

            c = chains["n0"]
            with act.Fori(0, NJ) as j:
                ln_act(c, j, "a")
                keep_h(c, j)
                split_act(c, j)
            act.wait_ge(s_fill, FILLS)

            def edge_pass(p):
                W = width(p)
                weighted = p in WEIGHTED

                def attr_sb(q, r):
                    act.wait_ge(attr_t_done.sem, attr_t_done.at(p, q, r))
                    if past(q, r, 2):
                        act.wait_ge(e_done.sem, e_done.at(p, q, r, 2))
                    copy(at_t[:, r % 2, :], bank(0)[0:ED, :]).then_inc(attr_sb_done.sem, 1)

                def keep_max(q, r):
                    heads = WEIGHTED[p][0]
                    act.wait_ge(max_done.sem, max_done.at(p, q, r))
                    apart(act, s_apart_act)
                    g0 = q * (UNROLL * GC) + r * GC
                    v = mx[0:heads, r % 2, :].rearrange("h (k e) -> h k e", k=GC)[:, ::-1, :]
                    copy(first_m[0:heads, bass.ds(g0, GC)], v[:, :, P - 1])
                    copy(last_m[0:heads, bass.ds(g0, GC)], v[:, :, 0]).then_inc(kept_done.sem, 1)

                def exps(q, r):
                    heads, _, scale = WEIGHTED[p]
                    act.wait_ge(dif_done.sem, dif_done.at(p, q, r))
                    if past(q, r, 2):
                        act.wait_ge(msg_done.sem, msg_done.at(p, q, r, 2))
                    a.activation(wgt[:, r % 2, 0:GC * heads], dif[:, r % 2, 0:GC * heads], ACT.Exp, scale=scale)\
                     .then_inc(exp_done.sem, 1)

                def same_f32(q, r):
                    act.wait_ge(same_in.of(r), same_in.at(p, q, r))
                    if past(q, r, 4):
                        act.wait_ge(sum_done.sem, sum_done.at(p, q, r, 4))
                    copy(same_f[:, r, :, :], same_b[:, r, :, :]).then_inc(same_f_done.sem, 1)

                def evac(q, r):
                    act.wait_ge(sum_done.sem, sum_done.at(p, q, r))
                    if past(q, r, 2):
                        act.wait_ge(ends_out.of(r), ends_out.at(p, q, r, 1))
                    o = o_b[:, r % 2, 0:GC * W].rearrange("p (k c) -> p k c", k=GC)
                    if p == "gat1":
                        s = bank(4, 4).rearrange("p (k c) -> p k c", k=GC)[:, :, 0:W]
                    elif weighted:
                        s = bank(4, 2).rearrange("p (k c) -> p k c", k=GC)[:, :, 0:W]
                    else:
                        s = bank(4 + r % 2).rearrange("p (k c) -> p k c", k=GC)
                    copy(o, s).then_inc(evac_done.sem, 1)

                if p in er_all:
                    cs = chains["s_" + p]
                    n = starts[p].shape[1]
                    act.wait_ge(s_steps, cs.at("er_sb"))
                    copy(er_c[:, :, 0:n].rearrange("p t c -> p c t"),
                         ps[:, 0:n * BANK].rearrange("p (c t) -> p c t", c=n)[:, :, 0:CH]).then_inc(s_steps, 1)
                if p == "attn":
                    over_groups(act, [(3, exps), (3, keep_max), (0, same_f32), (3, evac), (0, attr_sb)])
                elif weighted:
                    over_groups(act, [(1, same_f32), (3, keep_max), (3, exps), (4, evac)])
                else:
                    over_groups(act, [(2, evac)])

                c = chains["x_" + p]
                r_v = ps[0:CQ, 4 * BANK:8 * BANK].rearrange("p (a c) -> p a c", a=QA)[:, :, 0:W]
                if weighted:
                    heads, _, scale = WEIGHTED[p]
                    act.wait_ge(s_steps, c.at("lc_sb"))
                    copy(last_c[:, :, 0:heads],
                                                        ps[0:CQ, 0:QA * heads].rearrange("p (a h) -> p a h", a=QA)).then_inc(s_steps, 1)
                    for h in range(heads):
                        act.wait_ge(s_steps, c.at(f"e{h}"))
                        for t in range(QA):
                            i = a.activation(gw[:, t, t * CQ:], gw[:, t, t * CQ:], ACT.Exp, scale=-scale)
                        i.then_inc(s_steps, 1)
                act.wait_ge(s_steps, c.at("r_sb"))
                copy(r_rows[:, :, 0:W], r_v).then_inc(s_steps, 1)

            def t_copy(c, j, name, o, s):
                act.wait_ge(s_steps, c.at(name, j))
                copy(o, s).then_inc(s_steps, 1)

            edge_pass("gcn")
            c = chains["n_gcn"]
            with act.Fori(0, NJ) as j:
                t_copy(c, j, "Ts", a_t[:, 0:JT * P], ps[:, 0:JT * P])
                ln_act(c, j, "a")
                ln_act(c, j, "b")
                keep_h(c, j)
                t_copy(c, j, "T2s", h_t[:, :], ps[:, 0:JT * P])
                act.wait_ge(s_steps, c.at("qk", j))
                apart(act, s_apart_act)
                copy(tiles(q_all, j), tab[:, :, 0:D]).then_inc(s_steps, 1)
            edge_pass("attn")
            c = chains["n_attn"]
            with act.Fori(0, NJ) as j:
                load_h(c, j)
                t_copy(c, j, "Ts", h_t[:, :], ps[:, 0:JT * P])
                ln_act(c, j, "a")
                t_copy(c, j, "T2s", a_t[:, 0:JT * P], ps[:, 0:JT * P])
                for o in range(4):
                    act.wait_ge(s_steps, c.at(f"gelu{o}", j))
                    a.activation(
                        hid[:, o, :].rearrange("p (s n) -> p s n", s=2),
                        bank(2 * o, 2).rearrange("p (s n) -> p s n", s=2)[:, :, 0:JT * P // 2],
                        ACT.Gelu, bias=b_f1[:, o:o + 1]).then_inc(s_steps, 1)
                ln_act(c, j, "b")
                ln_act(c, j, "c")
                keep_h(c, j)
                t_copy(c, j, "T3s", h_t[:, :], ps[:, 0:JT * P])
                t_copy(c, j, "tab", tab[:, :, 0:D], hs[:, :, :])
            edge_pass("gat1")
            c = chains["n_gat1"]
            with act.Fori(0, NJ) as j:
                load_h(c, j)
                t_copy(c, j, "Ts", a_t[:, :], ps[:, 0:JT * H2 * P])
                t_copy(c, j, "T1s", h_t[:, :], ps[:, 4 * BANK:4 * BANK + JT * P])
                act.wait_ge(s_steps, c.at("exp", j))
                a.activation(a_n[:, :, :], a_n[:, :, :], ACT.Exp).then_inc(s_steps, 1)
                t_copy(c, j, "T2s", a_t[:, :], ps[:, 0:JT * H2 * P])
                f_v = ps[:, 0:JT * BANK].rearrange("p (k c) -> p k c", k=JT)
                act.wait_ge(s_steps, c.at("er_s", j))
                apart(act, s_apart_act)
                copy(tiles(er_all["gat2"], j), f_v[:, :, D:D + 2]).then_inc(s_steps, 1)
                act.wait_ge(s_steps, c.at("res", j))
                apart(act, s_apart_act)
                copy(tiles(h_sb, j), f_v[:, :, D + 2:2 * D + 2]).then_inc(s_steps, 1)
            edge_pass("gat2")
            c = chains["n_gat2"]
            with act.Fori(0, NJ) as j:
                ln_act(c, j, "a")
                keep_h(c, j)
                split_act(c, j)
            for p in ("sage1", "sage2"):
                edge_pass(p)
                c = chains["n_" + p]
                with act.Fori(0, NJ) as j:
                    load_h(c, j)
                    t_copy(c, j, "Ts", a_t[:, 0:JT * P], ps[:, 0:JT * P])
                    t_copy(c, j, "T1s", h_t[:, :], ps[:, 2 * BANK:2 * BANK + JT * P])
                    if p == "sage1":
                        keep_h(c, j)
                        split_act(c, j)

        @block.tensor
        def _(pe):
            mm = nc.tensor.matmul

            c = chains["prep"]
            pe.wait_ge(s_steps, c.at("look_ps"))
            mm(ps[0:1, 0:1], falls[:, :], ones[0:CQ, 0:1], start=True, stop=True).then_inc(s_steps, 1)
            pe.wait_ge(s_steps, c.at("sort_pre"))
            unsorted_pe = pe.value_load(unsorted_i[0:1, 0:1], min_val=0, max_val=EP)
            for step, mat in (("sort_pre", upper), ("sort_tot", ones)):
                pe.wait_ge(s_steps, c.at(step))
                with pe.If(unsorted_pe > 0):
                    for n0 in range(0, NP, BANK):
                        n1 = min(n0 + BANK, NP)
                        mm(ps[:, n0:n1], mat[:, :], held[:, n0:n1], start=True, stop=True)
                pe.drain()
                pe.sem_inc(s_steps, 1)
            pe.wait_ge(s_steps, c.at("cols"))
            for a in range(QA):
                mm(ps[:, a * CQ:(a + 1) * CQ], src_rf[:, a, :], ident[0:CQ, 0:CQ], start=True, stop=True)
                i = mm(ps[:, BANK + a * CQ:BANK + (a + 1) * CQ], dst_rf[:, a, :], ident[0:CQ, 0:CQ], start=True, stop=True)
            i.then_inc(s_steps, 1)

            def hist(first, last, turn, slot):
                pe.wait_ge(s_hot, turn * 2 + 2)
                for s in range(2):
                    for k in range(UNROLL):
                        i = mm(ps[:, s * BANK:s * BANK + NT], hot_lo[:, 2 * slot + s, k, :], hot_hi[:, 2 * slot + s, k, :],
                               start=first and k == 0, stop=last and k == UNROLL - 1, skip_group_check=True)
                i.then_inc(s_hist, 1)

            hist(True, False, 0, 0)
            hist(False, False, 1, 1)
            with pe.Fori(1, NG // 2 - 1) as t:
                hist(False, False, t * 2, 0)
                hist(False, False, t * 2 + 1, 1)
            hist(False, False, NG - 2, 0)
            hist(False, True, NG - 1, 1)
            c = chains["hist"]
            pe.wait_ge(s_hist, NG)
            pe.wait_ge(s_steps, c.at("hist_start"))
            pe.sem_inc(s_steps, 1)
            pe.wait_ge(s_steps, c.at("cum_ps"))
            mm(ps[:, 0:NT], upper[:, :], deg[:, 1, :], start=True, stop=True)
            mm(ps[:, BANK:BANK + NT], ones[:, :], deg[:, 1, :], start=True, stop=True).then_inc(s_steps, 1)
            pe.wait_ge(s_steps, c.at("bnd_ps"))
            for a in range(QA):
                mm(ps[0:CQ, a:a + 1], dst_f[:, a * CQ:(a + 1) * CQ], ident[:, 0:1], start=True, stop=True)
                mm(ps[0:CQ, QA + a:QA + a + 1], dst_f[:, a * CQ:(a + 1) * CQ], ident[:, P - 1:P], start=True, stop=True)
            mm(ps[0:CQ, BANK:BANK + CH], bc(ident[:, P - 1:P], [P, CQ]), dst_f[:, :], start=True, stop=True)\
                .then_inc(s_steps, 1)
            pe.wait_ge(s_steps, c.at("wt_ps"))
            for i in range(16):
                mm(ps[:, (i // 3) * BANK + (i % 3) * D if i < 12 else 4 * BANK + (i - 12) * D:][:, 0:D],
                   raw[:, i, :], ident[:, :], start=True, stop=True)
            for h in range(H2):
                for l in range(2):
                    mm(ps[:, 5 * BANK + l * H2 + h:5 * BANK + l * H2 + h + 1], raw[:, h, :], a1[:, l, h:h + 1],
                       start=True, stop=True)
                i = mm(ps[:, 6 * BANK + 2 * h:6 * BANK + 2 * h + 2], raw[:, 6 + h, :], a2[:, :], start=True, stop=True)
            i.then_inc(s_steps, 1)

            def edge_pass(p):
                W = width(p)
                weighted = p in WEIGHTED
                if weighted:
                    heads, cols, _ = WEIGHTED[p]

                if p in er_all:
                    cs = chains["s_" + p]
                    n = starts[p].shape[1]
                    pe.wait_ge(s_steps, cs.at("er_ps"))
                    for a in range(QA):
                        for h in range(n):
                            i = nc.tensor.transpose(ps[:, h * BANK + a * CQ:h * BANK + (a + 1) * CQ],
                                                    er_r[:, a, h:P * n:n], ident[0:CQ, 0:CQ])
                    i.then_inc(s_steps, 1)
                    pe.wait_ge(s_steps, cs.end)

                def bcast_dst(q, r):
                    pe.wait_ge(diag_done.sem, diag_done.at(p, q, r))
                    if past(q, r, 1):
                        pe.wait_ge(same_done.sem, same_done.at(p, q, r, 1))
                    mm(bank(0), ones[:, :], diag[:, r % 2, :, :].rearrange("p k c -> p (k c)"), start=True, stop=True)\
                        .then_inc(bcast_done.sem, 1)

                def attr_t(q, r):
                    pe.wait_ge(attr_in.of(r), attr_in.at(p, q, r))
                    if past(q, r, 1):
                        pe.wait_ge(attr_sb_done.sem, attr_sb_done.at(p, q, r, 1))
                    apart(pe, s_apart_pe)
                    for k in range(GC):
                        i = nc.tensor.transpose(bank(0)[0:ED, k * P:(k + 1) * P], at_b[:, r, k, :], ident[:, :])
                    i.then_inc(attr_t_done.sem, 1)

                def edge_terms(q, r):
                    pe.wait_ge(attr_sb_done.sem, attr_sb_done.at(p, q, r))
                    if past(q, r, 1):
                        pe.wait_ge(kve_done.sem, kve_done.at(p, q, r, 1))
                    for k in range(GC):
                        i = mm(bank(1)[:, k * D:(k + 1) * D], at_t[:, r % 2, k * P:(k + 1) * P], w_e[:, :],
                               start=True, stop=True)
                    i.then_inc(e_done.sem, 1)

                def logit_t(q, r):
                    pe.wait_ge(logit_done.sem, logit_done.at(p, q, r))
                    if past(q, r, 1):
                        pe.wait_ge(fwd_done.sem, fwd_done.at(p, q, r, 1))
                    apart(pe, s_apart_pe)
                    for k in range(GC):
                        i = nc.tensor.transpose(bank(2)[0:heads, (GC - 1 - k) * P:(GC - k) * P],
                                                logit[:, r % 2, k * heads:(k + 1) * heads], ident[:, :])
                    i.then_inc(logit_t_done.sem, 1)

                def dst_rows(q, r):
                    pe.wait_ge(same_f_done.sem, same_f_done.at(p, q, r))
                    if past(q, r, 1):
                        pe.wait_ge(prod_done.sem, prod_done.at(p, q, r, 1))
                    if p == "attn":
                        pe.wait_ge(starts_in.of(r), starts_in.at(p, q, r))
                        for k in range(GC):
                            i = mm(bank(3)[:, k * D:(k + 1) * D], same_f[:, r, k, :], q_b[:, r, k, :],
                                   start=True, stop=True)
                    else:
                        n = starts[p].shape[1]
                        for k in range(GC):
                            g = q * (UNROLL * GC) + (r * GC + k)
                            i = mm(bank(3)[:, k * n:(k + 1) * n], same_f[:, r, k, :],
                                   er_c[:, bass.ds(g, 1), 0:n].rearrange("p t c -> p (t c)"), start=True, stop=True)
                    i.then_inc(dst_done.sem, 1)

                def max_t(q, r):
                    pe.wait_ge(max_done.sem, max_done.at(p, q, r))
                    if past(q, r, 1):
                        pe.wait_ge(dif_done.sem, dif_done.at(p, q, r, 1))
                    apart(pe, s_apart_pe)
                    for k in range(GC):
                        i = nc.tensor.transpose(max_ps(p)[:, k * heads:(k + 1) * heads],
                                                mx[0:heads, r % 2, (GC - 1 - k) * P:(GC - k) * P],
                                                ident[0:heads, 0:heads])
                    i.then_inc(max_t_done.sem, 1)

                def sums(q, r):
                    if weighted:
                        pe.wait_ge(msg_done.sem, msg_done.at(p, q, r))
                        pe.wait_ge(same_f_done.sem, same_f_done.at(p, q, r))
                        if past(q, r, 1):
                            pe.wait_ge(evac_done.sem, evac_done.at(p, q, r, 1))
                        for k in range(GC):
                            if p == "gat1":
                                o = bank(4 + k)[:, 0:W]
                            else:
                                o = bank(4 + k // 2)[:, (k % 2) * 256:(k % 2) * 256 + W]
                            i = mm(o, same_f[:, r, k, :], msg[:, r % 2, k * W:(k + 1) * W], start=True, stop=True)
                    else:
                        pe.wait_ge(rows_in.of(r), rows_in.at(p, q, r))
                        if p == "gcn":
                            pe.wait_ge(same_done.sem, same_done.at(p, q, r))
                        else:
                            pe.wait_ge(same_in.of(r), same_in.at(p, q, r))
                        if past(q, r, 2):
                            pe.wait_ge(evac_done.sem, evac_done.at(p, q, r, 2))
                        for k in range(GC):
                            for s in range(3):
                                o = (k * 3 + s) * D
                                i = mm(bank(4 + r % 2)[:, k * D:(k + 1) * D], same_b[:, r, k, :],
                                       row_s[:, r, o:o + D], start=s == 0, stop=s == 2)
                    i.then_inc(sum_done.sem, 1)

                if p == "gcn":
                    over_groups(pe, [(1, bcast_dst), (2, sums)])
                elif p == "attn":
                    over_groups(pe, [(3, max_t), (1, edge_terms), (1, dst_rows), (2, logit_t), (3, sums), (0, attr_t)])
                elif weighted:
                    over_groups(pe, [(2, dst_rows), (3, max_t), (2, logit_t), (4, sums)])
                else:
                    over_groups(pe, [(2, sums)])

                c = chains["x_" + p]

                def carried(h, c0, c1, mat):
                    for b in range(QA):
                        for t in range(b + 1):
                            i = mm(ps[0:CQ, (4 + b) * BANK + c0:(4 + b) * BANK + c1], mat[:, t, b * CQ:(b + 1) * CQ],
                                   z_rows[:, t, c0:c1], start=t == 0, stop=t == b)
                    return i

                if weighted:
                    pe.wait_ge(s_steps, c.at("lc_ps"))
                    for a in range(QA):
                        i = mm(ps[0:CQ, a * heads:(a + 1) * heads], last_m[0:heads, a * CQ:(a + 1) * CQ],
                               ident[0:heads, 0:heads], start=True, stop=True)
                    i.then_inc(s_steps, 1)
                    for h in range(heads):
                        pe.wait_ge(s_steps, c.at(f"fb{h}"))
                        mm(ps[0:CQ, BANK:BANK + CH], spread[0:heads, h, :],
                                                          first_m[0:heads, :], start=True, stop=True).then_inc(s_steps, 1)
                        pe.wait_ge(s_steps, c.at(f"r{h}"))
                        carried(h, h * (cols + 1), (h + 1) * (cols + 1), gw).then_inc(s_steps, 1)
                else:
                    pe.wait_ge(s_steps, c.at("r"))
                    carried(0, 0, D, carries).then_inc(s_steps, 1)

            def transposes(c, j, name, srcs, b0=0):
                pe.wait_ge(s_steps, c.at(name, j))
                for i, s in enumerate(srcs):
                    last = nc.tensor.transpose(ps[:, b0 * BANK + i * P:b0 * BANK + (i + 1) * P], s, ident[:, :])
                last.then_inc(s_steps, 1)

            def linear(c, j, name, out_of, terms):
                pe.wait_ge(s_steps, c.at(name, j))
                for k in range(JT):
                    for i, (lhs, rhs) in enumerate(terms):
                        last = mm(out_of(k), lhs(k), rhs, start=i == 0, stop=i == len(terms) - 1)
                last.then_inc(s_steps, 1)

            def part(t, k, n=P):
                return t[:, k * n:(k + 1) * n]

            edge_pass("gcn")
            c = chains["n_gcn"]
            with pe.Fori(0, NJ) as j:
                transposes(c, j, "T", [a_n[:, k, 0:D] for k in range(JT)])
                linear(c, j, "lin", lambda k: part(ps, 8 + k), [(lambda k: part(a_t, k), w0[:, :])])
                transposes(c, j, "T2", [hs[:, k, :] for k in range(JT)])
                linear(c, j, "qkv", lambda k: bank(2 + k)[:, 0:3 * D], [(lambda k: part(h_t, k), w_qkv[:, :])])
            edge_pass("attn")
            c = chains["n_attn"]
            with pe.Fori(0, NJ) as j:
                transposes(c, j, "T", [hs[:, k, :] for k in range(JT)])
                linear(c, j, "lin", lambda k: part(ps, 8 + k), [(lambda k: part(h_t, k), w_skip[:, :])])
                transposes(c, j, "T2", [y[:, k, :] for k in range(JT)])
                pe.wait_ge(s_steps, c.at("ffn1", j))
                half = JT * P // 2
                for o in range(4):
                    for s in range(2):
                        i = mm(bank(2 * o + s)[:, 0:half], w_f1[:, o * P:(o + 1) * P], a_t[:, s * half:(s + 1) * half],
                               start=True, stop=True)
                i.then_inc(s_steps, 1)
                linear(c, j, "ffn2", lambda k: part(ps, k),
                       [((lambda k, o=o: hid[:, o, k * P:(k + 1) * P]), w_f2[:, o, :]) for o in range(4)])
                transposes(c, j, "T3", [hs[:, k, :] for k in range(JT)])
                linear(c, j, "el", lambda k: bank(2)[:, k * 6:(k + 1) * 6],
                       [(lambda k: part(h_t, k), u1[:, :, :].rearrange("p l h -> p (l h)"))])
            edge_pass("gat1")
            c = chains["n_gat1"]
            with pe.Fori(0, NJ) as j:
                pe.wait_ge(s_steps, c.at("T", j))
                for k in range(JT):
                    for h in range(H2):
                        nc.tensor.transpose(part(ps, k * H2 + h), a_n[:, k, h * D:(h + 1) * D], ident[:, :])
                    last = nc.tensor.transpose(ps[:, 4 * BANK + k * P:4 * BANK + (k + 1) * P], hs[:, k, :], ident[:, :])
                last.then_inc(s_steps, 1)
                pe.wait_ge(s_steps, c.at("lin", j))
                for k in range(JT):
                    for h in range(H2):
                        o = bank(k)[:, h * D:(h + 1) * D]
                        mm(o, part(a_t, k * H2 + h), fc1_t[:, h, :], start=True, stop=False)
                        i = mm(o, part(h_t, k), res1_t[:, h, :], start=False, stop=True)
                i.then_inc(s_steps, 1)
                transposes(c, j, "T2", [a_n[:, k, h * D:(h + 1) * D] for k in range(JT) for h in range(H2)])
                linear(c, j, "feat", lambda k: bank(k)[:, 0:2 * D + 2],
                       [((lambda k, h=h: part(a_t, k * H2 + h)), w2[:, h, :]) for h in range(H2)])
            edge_pass("gat2")
            for i, p in enumerate(("sage1", "sage2")):
                edge_pass(p)
                c = chains["n_" + p]
                with pe.Fori(0, NJ) as j:
                    pe.wait_ge(s_steps, c.at("T", j))
                    for k in range(JT):
                        nc.tensor.transpose(part(ps, k), a_n[:, k, 0:D], ident[:, :])
                        last = nc.tensor.transpose(part(ps, 8 + k), hs[:, k, :], ident[:, :])
                    last.then_inc(s_steps, 1)
                    linear(c, j, "lin", lambda k: bank(4 + k // 4)[:, (k % 4) * P:(k % 4 + 1) * P],
                           [(lambda k: part(a_t, k), sage_t[:, 2 * i, :]), (lambda k: part(h_t, k), sage_t[:, 2 * i + 1, :])])

        @block.vector
        def _(dve):
            v = nc.vector
            tt, ts, stt = v.tensor_tensor, v.tensor_scalar, v.scalar_tensor_tensor

            c = chains["prep"]
            dve.wait_ge(s_steps, c.at("look_lt"))
            tt(brk_r[:, :, :], dst_r[:, :, :], prev_r[:, :, :], ALU.is_lt).then_inc(s_steps, 1)
            dve.wait_ge(s_steps, c.at("look_sum"))
            v.reduce_sum(falls[:, :], brk_r[:, :, :].rearrange("t a e -> t (a e)"), axis=AX_X).then_inc(s_steps, 1)
            dve.wait_ge(s_steps, c.at("look_i"))
            v.tensor_copy(unsorted_i[:, :], ps[0:1, 0:1]).then_inc(s_steps, 1)
            dve.wait_ge(s_steps, c.at("sort_in"))
            unsorted_dve = dve.value_load(unsorted_i[0:1, 0:1], min_val=0, max_val=EP)
            dve.wait_ge(s_steps, c.at("sort_hist"))
            with dve.If(unsorted_dve > 0):
                v.memset(held[:, :], 0.0)
                v.tensor_copy(nodes[:, :], run[:, :].bitcast(I32))
                v.tensor_copy(dst_kf[:, :], dst_k[:, :]).then_inc(s_sort_dve, 1)
                dve.wait_ge(s_sort_dve, 1)
                with dve.Fori(0, CH) as i:
                    stt(held[:, :], nodes[:, :], dst_kf[:, bass.ds(i, 1)], held[:, :], ALU.is_equal, ALU.add)\
                        .then_inc(s_sort_dve, 1)
                    dve.wait_ge(s_sort_dve, i + 2)
                    apart(dve, s_apart_dve)
            dve.sem_inc(s_steps, 1)
            dve.wait_ge(s_steps, c.at("sort_pre_sb"))
            with dve.If(unsorted_dve > 0):
                tt(run[:, :], ps[:, 0:NP], held[:, :], ALU.subtract).then_inc(s_sort_dve, 1)
                dve.wait_ge(s_sort_dve, CH + 2)
            dve.sem_inc(s_steps, 1)
            dve.wait_ge(s_steps, c.at("sort_rank"))
            with dve.If(unsorted_dve > 0):
                v.tensor_tensor_scan(held[:, :], bc(ones[:, 0:1], [P, NP]), ps[:, 0:NP], 0.0, ALU.mult, ALU.add)\
                    .then_inc(s_sort_dve, 1)
                dve.wait_ge(s_sort_dve, CH + 3)
                tt(held[:, :], held[:, :], ps[:, 0:NP], ALU.subtract).then_inc(s_sort_dve, 1)
                dve.wait_ge(s_sort_dve, CH + 4)
                tt(run[:, :], run[:, :], held[:, :], ALU.add).then_inc(s_sort_dve, 1)
                dve.wait_ge(s_sort_dve, CH + 5)
                with dve.Fori(0, CH) as i:
                    stt(held[:, :], nodes[:, :], dst_kf[:, bass.ds(i, 1)], run[:, :], ALU.is_equal, ALU.mult)\
                        .then_inc(s_sort_dve, 1)
                    dve.wait_ge(s_sort_dve, i * 2 + (CH + 6))
                    apart(dve, s_apart_dve)
                    v.reduce_sum(rank[:, bass.ds(i, 1)], held[:, :], axis=AX_X)
                    stt(run[:, :], nodes[:, :], dst_kf[:, bass.ds(i, 1)], run[:, :], ALU.is_equal, ALU.add)\
                        .then_inc(s_sort_dve, 1)
                    dve.wait_ge(s_sort_dve, i * 2 + (CH + 7))
                    apart(dve, s_apart_dve)
                v.tensor_copy(rank_i[:, 0, :], rank[:, :])
                ts(rank_i[:, 1, :], rank[:, :], float(P), None, ALU.add).then_inc(s_sort_dve, 1)
                dve.wait_ge(s_sort_dve, 3 * CH + 6)
                ts(rank_i[:, 2, :], rank_i[:, 0, :], P - 1, None, ALU.bitwise_xor).then_inc(s_sort_dve, 1)
                dve.wait_ge(s_sort_dve, 3 * CH + 7)
            dve.sem_inc(s_steps, 1)
            dve.wait_ge(s_steps, c.at("iota_f"))
            v.tensor_copy(iota_row[:, :], iota_i[:, :]).then_inc(s_steps, 1)
            dve.wait_ge(s_steps, c.at("cast"))
            v.tensor_copy(src_rf[:, :, ::-1], src_r[:, :, :])
            v.tensor_copy(dst_rf[:, :, ::-1], dst_r[:, :, :]).then_inc(s_steps, 1)
            dve.wait_ge(s_steps, c.at("brk"))
            tt(brk_r[:, :, :], dst_r[:, :, :], prev_r[:, :, :], ALU.not_equal).then_inc(s_steps, 1)
            dve.wait_ge(s_steps, c.at("brk2"))
            ts(brk_r[:, :, :], brk_r[:, :, :], -BIG, None, ALU.mult).then_inc(s_steps, 1)
            dve.wait_ge(s_steps, c.at("cols_i"))
            v.tensor_copy(src_i[:, :], ps[:, 0:CH])
            v.tensor_copy(dst_f[:, :], ps[:, BANK:BANK + CH])
            v.tensor_copy(dst_i[:, :], ps[:, BANK:BANK + CH]).then_inc(s_steps, 1)
            dve.wait_ge(s_steps, c.at("bits"))
            for i, t in enumerate((src_i, dst_i)):
                ts(part_i[:, :], t[:, :], P - 1, None, ALU.bitwise_and).then_inc(s_seed, 1)
                dve.wait_ge(s_seed, 4 * i + 1)
                v.tensor_copy(lo_f[:, i, :], part_i[:, :]).then_inc(s_seed, 1)
                dve.wait_ge(s_seed, 4 * i + 2)
                ts(part_i[:, :], t[:, :], 7, None, ALU.logical_shift_right).then_inc(s_seed, 1)
                dve.wait_ge(s_seed, 4 * i + 3)
                v.tensor_copy(hi_f[:, i, :], part_i[:, :]).then_inc(s_seed, 1)
                dve.wait_ge(s_seed, 4 * i + 4)
            dve.sem_inc(s_steps, 1)
            dve.wait_ge(s_steps, c.at("bits_f"))
            dve.sem_inc(s_steps, 1)

            def hot(turn, slot, wait):
                for s in range(2):
                    if wait:
                        dve.wait_ge(s_hist, turn - 1)
                    cols = bass.ds(turn * UNROLL, UNROLL)
                    tt(hot_lo[:, 2 * slot + s, :, :], bc(iota_row[:, :].rearrange("p (a c) -> p a c", a=1), [P, UNROLL, P]),
                       bc(lo_f[:, s, cols].rearrange("p (a c) -> p a c", c=1), [P, UNROLL, P]), ALU.is_equal)
                    tt(hot_hi[:, 2 * slot + s, :, :], bc(iota_row[:, 0:NT].rearrange("p (a c) -> p a c", a=1), [P, UNROLL, NT]),
                       bc(hi_f[:, s, cols].rearrange("p (a c) -> p a c", c=1), [P, UNROLL, NT]), ALU.is_equal)\
                        .then_inc(s_hot, 1)

            dve.wait_ge(s_steps, chains["prep"].end)
            hot(0, 0, False)
            hot(1, 1, False)
            with dve.Fori(1, NG // 2) as t:
                hot(t * 2, 0, True)
                hot(t * 2 + 1, 1, True)

            c = chains["hist"]
            dve.wait_ge(s_steps, c.at("hist_read"))
            v.tensor_copy(deg[:, 0, :], ps[:, 0:NT])
            v.tensor_copy(deg[:, 1, :], ps[:, BANK:BANK + NT]).then_inc(s_steps, 1)
            n = lambda i: ntmp[:, i, :]
            ni = lambda i: ntmp_i[:, i, :]
            dve.wait_ge(s_steps, c.at("deg_max"))
            ts(norm[:, :, :], deg[:, :, :], 1.0, None, ALU.max).then_inc(s_steps, 1)
            dve.wait_ge(s_steps, c.at("deg_norm"))
            v.reciprocal(norm[:, :, :], norm[:, :, :]).then_inc(s_steps, 1)
            dve.wait_ge(s_steps, c.at("cnt_r"))
            ts(n(0), deg[:, 1, :], 1.0, None, ALU.max).then_inc(s_seed, 1)
            dve.wait_ge(s_seed, 9)
            v.reciprocal(cnt_r[:, :], n(0)).then_inc(s_steps, 1)
            dve.wait_ge(s_steps, c.at("tot_sb"))
            v.tensor_copy(tot[:, :], ps[:, BANK:BANK + NT]).then_inc(s_steps, 1)
            dve.wait_ge(s_steps, c.at("tot_scan"))
            v.tensor_tensor_scan(tot_x[:, :], ones[:, 0:NT], tot[:, :], 0.0, ALU.mult, ALU.add).then_inc(s_steps, 1)
            dve.wait_ge(s_steps, c.at("tot_ex"))
            tt(tot_x[:, :], tot_x[:, :], tot[:, :], ALU.subtract).then_inc(s_steps, 1)
            dve.wait_ge(s_steps, c.at("cum"))
            tt(cum[:, :], tot_x[:, :], ps[:, 0:NT], ALU.add).then_inc(s_steps, 1)
            dve.wait_ge(s_steps, c.at("nz"))
            ts(n(0), deg[:, 1, :], 0.0, None, ALU.is_gt).then_inc(s_steps, 1)
            dve.wait_ge(s_steps, c.at("end"))
            stt(n(1), cum[:, :], -1.0, n(0), ALU.add, ALU.mult).then_inc(s_steps, 1)
            dve.wait_ge(s_steps, c.at("end_ii"))
            v.tensor_copy(ni(0), n(1)).then_inc(s_steps, 1)
            dve.wait_ge(s_steps, c.at("end_xor"))
            ts(ni(1), ni(0), P - 1, None, ALU.bitwise_xor).then_inc(s_steps, 1)
            dve.wait_ge(s_steps, c.at("end_f"))
            v.tensor_copy(n(2), ni(1)).then_inc(s_steps, 1)
            dve.wait_ge(s_steps, c.at("end_m"))
            stt(n(2), n(2), float(-EP), n(0), ALU.add, ALU.mult).then_inc(s_steps, 1)
            dve.wait_ge(s_steps, c.at("end_i"))
            ts(end_i[:, :], n(2), float(EP), None, ALU.add).then_inc(s_steps, 1)
            dve.wait_ge(s_steps, c.at("blk_i"))
            ts(ni(2), ni(0), 7, None, ALU.logical_shift_right).then_inc(s_steps, 1)
            dve.wait_ge(s_steps, c.at("blk_f"))
            v.tensor_copy(n(3), ni(2)).then_inc(s_steps, 1)
            dve.wait_ge(s_steps, c.at("start"))
            tt(n(4), cum[:, :], deg[:, 1, :], ALU.subtract).then_inc(s_steps, 1)
            dve.wait_ge(s_steps, c.at("inner"))
            stt(n(4), n(3), float(P), n(4), ALU.mult, ALU.is_ge).then_inc(s_steps, 1)
            dve.wait_ge(s_steps, c.at("blk_m"))
            tt(n(4), n(4), n(0), ALU.mult).then_inc(s_steps, 1)
            dve.wait_ge(s_steps, c.at("blk_n"))
            stt(n(3), n(3), float(-CH), n(4), ALU.add, ALU.mult).then_inc(s_steps, 1)
            dve.wait_ge(s_steps, c.at("carry_i"))
            ts(carry_i[:, :], n(3), float(CH), None, ALU.add).then_inc(s_steps, 1)
            dve.wait_ge(s_steps, c.at("st_i"))
            tt(n(5), cum[:, :], deg[:, 1, :], ALU.subtract).then_inc(s_steps, 1)
            dve.wait_ge(s_steps, c.at("st_x"))
            v.tensor_copy(ni(3), n(5)).then_inc(s_steps, 1)
            dve.wait_ge(s_steps, c.at("st_f"))
            ts(ni(4), ni(3), P - 1, None, ALU.bitwise_xor).then_inc(s_steps, 1)
            dve.wait_ge(s_steps, c.at("id_f"))
            v.tensor_copy(n(6), node_i[:, :])
            v.tensor_copy(n(7), ni(4)).then_inc(s_steps, 1)
            dve.wait_ge(s_steps, c.at("st_d"))
            ts(n(6), n(6), float(EP), None, ALU.add).then_inc(s_steps, 1)
            dve.wait_ge(s_steps, c.at("st_m"))
            tt(n(7), n(7), n(6), ALU.subtract).then_inc(s_steps, 1)
            dve.wait_ge(s_steps, c.at("st_n"))
            tt(n(7), n(7), n(0), ALU.mult).then_inc(s_steps, 1)
            dve.wait_ge(s_steps, c.at("start_i"))
            tt(start_i[:, :], n(7), n(6), ALU.add).then_inc(s_steps, 1)
            dve.wait_ge(s_steps, c.at("last_sb"))
            v.tensor_copy(first_i[:, :], ps[0:CQ, QA:2 * QA])
            v.tensor_copy(last_dst[:, :], ps[0:CQ, 0:QA]).then_inc(s_steps, 1)
            dve.wait_ge(s_steps, c.at("after_f"))
            v.tensor_copy(after[:, :], after_i[0:CQ, :]).then_inc(s_steps, 1)
            dve.wait_ge(s_steps, c.at("carries"))
            for a in range(QA):
                i = ts(carries[:, a, :], after[:, :], float(a * CQ), None, ALU.is_gt)
            i.then_inc(s_steps, 1)
            dve.wait_ge(s_steps, c.at("carries2"))
            for a in range(QA):
                i = stt(carries[:, a, :], ps[0:CQ, BANK:BANK + CH], last_dst[:, a:a + 1], carries[:, a, :],
                        ALU.is_equal, ALU.mult)
            i.then_inc(s_steps, 1)
            dve.wait_ge(s_steps, c.at("spread"))
            v.tensor_copy(
                spread[:, :, :], bc(ident[0:H1, 0:H1].rearrange("h (g c) -> h g c", c=1), [H1, H1, CQ])).then_inc(s_steps, 1)
            dve.wait_ge(s_steps, c.at("bn_var"))
            for i in range(2):
                last = ts(bn_a[:, i, :], rows[f"L3_gnn_rv{i}"][:, :], EPS, None, ALU.add)
            last.then_inc(s_steps, 1)
            dve.wait_ge(s_steps, c.at("bn_rs"))
            v.reciprocal(bn_a[:, :, :], bn_a[:, :, :]).then_inc(s_steps, 1)
            for name, o, x0, y0, op in (("bn_a", bn_a, bn_a, "g", ALU.mult), ("bn_b1", bn_b, "b", "rm", ALU.subtract),
                                        ("bn_b2", bn_b, bn_b, bn_a, ALU.mult), ("bn_b3", bn_b, bn_b, "be", ALU.add)):
                dve.wait_ge(s_steps, c.at(name))
                pick = lambda s, i: rows[f"L3_gnn_{s}{i}"][:, :] if isinstance(s, str) else s[:, i, :]
                for i in range(2):
                    last = tt(o[:, i, :], pick(x0, i), pick(y0, i), op)
                last.then_inc(s_steps, 1)

            def nb(ap, n=D):
                return bc(ap.rearrange("p (k a) -> p k a", a=1), [P, JT, n])

            def fb(ap, n=D):
                return bc(ap.rearrange("p (a c) -> p a c", a=1), [P, JT, n])

            Y = y[:, :, :]

            def norm_steps(c, j, pre):
                dve.wait_ge(s_steps, c.at(pre + "mean", j))
                v.reduce_sum(st[:, 0, :], Y, axis=AX_X).then_inc(s_steps, 1)
                dve.wait_ge(s_steps, c.at(pre + "neg", j))
                ts(st[:, 4, :], st[:, 0, :], 1.0 / D, None, ALU.mult).then_inc(s_steps, 1)
                dve.wait_ge(s_steps, c.at(pre + "cent", j))
                tt(Y, Y, nb(st[:, 4, :]), ALU.subtract).then_inc(s_steps, 1)
                dve.wait_ge(s_steps, c.at(pre + "var", j))
                v.reduce_sum(st[:, 0, :], sq[:, :, :], axis=AX_X).then_inc(s_steps, 1)
                dve.wait_ge(s_steps, c.at(pre + "vare", j))
                ts(st[:, 1, :], st[:, 0, :], 1.0 / D, EPS, ALU.mult, ALU.add).then_inc(s_steps, 1)
                dve.wait_ge(s_steps, c.at(pre + "rs", j))
                v.reciprocal(st[:, 3, :], st[:, 2, :]).then_inc(s_steps, 1)

            def add_to_x(c, j, name):
                dve.wait_ge(s_steps, c.at(name, j))
                tt(Y, Y, tiles(x_sb, j), ALU.add).then_inc(s_steps, 1)
                dve.wait_ge(s_steps, c.at("xk", j))
                apart(dve, s_apart_dve)
                v.tensor_copy(tiles(x_sb, j), Y).then_inc(s_steps, 1)

            def relu_norm(c, j):
                dve.wait_ge(s_steps, c.at("hs", j))
                stt(hs[:, :, :], Y, 0.0, nb(st[:, 3, :]), ALU.max, ALU.mult).then_inc(s_steps, 1)

            def split_dve(c, j):
                dve.wait_ge(s_steps, c.at("r1", j))
                tt(sq[:, :, :], hs[:, :, :], tab_b[:, :, 0, :], ALU.subtract).then_inc(s_steps, 1)
                dve.wait_ge(s_steps, c.at("r2", j))
                tt(sq[:, :, :], sq[:, :, :], tab_b[:, :, 1, :], ALU.subtract).then_inc(s_steps, 1)
                dve.wait_ge(s_steps, c.at("lo", j))
                v.tensor_copy(tab_b[:, :, 2, :], sq[:, :, :]).then_inc(s_steps, 1)

            def cols(ap, j):
                return ap[:, bass.ds(j * JT, JT)]

            c = chains["n0"]
            with dve.Fori(0, NJ) as j:
                dve.wait_ge(s_steps, c.at("xl", j))
                v.tensor_copy(Y, tiles(x_sb, j)).then_inc(s_steps, 1)
                norm_steps(c, j, "a")
                relu_norm(c, j)
                dve.wait_ge(s_steps, c.at("hn", j))
                tt(hs[:, :, :], hs[:, :, :], nb(cols(norm[:, 0, :], j)), ALU.mult).then_inc(s_steps, 1)
                split_dve(c, j)

            def edge_pass(p):
                W = width(p)
                weighted = p in WEIGHTED
                if weighted:
                    heads, nc_, _ = WEIGHTED[p]

                def diags(q, r):
                    if past(q, r, 2):
                        dve.wait_ge(bcast_done.sem, bcast_done.at(p, q, r, 2))
                    g0 = bass.ds(q * (UNROLL * GC) + r * GC, GC)
                    tt(diag[:, r % 2, :, :], bc(ident[:, :].rearrange("p (a c) -> p a c", a=1), [P, GC, P]),
                       bc(dst_f[:, g0].rearrange("p (k c) -> p k c", c=1), [P, GC, P]), ALU.mult)\
                        .then_inc(diag_done.sem, 1)

                def same(q, r):
                    dve.wait_ge(bcast_done.sem, bcast_done.at(p, q, r))
                    if past(q, r, 4):
                        dve.wait_ge(sum_done.sem, sum_done.at(p, q, r, 4))
                    if past(q, r, 4):
                        dve.wait_ge(same_out.of(r), same_out.at(p, q, r, 1))
                    g0 = bass.ds(q * (UNROLL * GC) + r * GC, GC)
                    tt(same_b[:, r, :, :], bank(0).rearrange("p (k c) -> p k c", k=GC),
                       bc(dst_f[:, g0].rearrange("p (k c) -> p k c", c=1), [P, GC, P]), ALU.is_equal)\
                        .then_inc(same_done.sem, 1)

                def terms(q, r):
                    dve.wait_ge(rows_in.of(r), rows_in.at(p, q, r))
                    dve.wait_ge(dst_done.sem, dst_done.at(p, q, r))
                    if p == "attn":
                        dve.wait_ge(e_done.sem, e_done.at(p, q, r))
                        kv = row_b[:, r, :, :].rearrange("p k (s c) -> p k s c", s=2)
                        tt(kv, kv, bc(bank(1).rearrange("p (k s c) -> p k s c", k=GC, s=1), [P, GC, 2, D]), ALU.add)\
                            .then_inc(kve_done.sem, 1)
                        dve.wait_ge(kve_done.sem, kve_done.at(p, q, r))
                        if past(q, r, 1):
                            dve.wait_ge(logit_done.sem, logit_done.at(p, q, r, 1))
                        tt(prod[:, :, :], row_b[:, r, :, 0:D], bank(3).rearrange("p (k c) -> p k c", k=GC), ALU.mult)\
                            .then_inc(prod_done.sem, 1)
                    else:
                        z = z_b[:, :, 0:heads]
                        if past(q, r, 1):
                            dve.wait_ge(logit_done.sem, logit_done.at(p, q, r, 1))
                        er0 = 0 if p == "gat1" else 1
                        er_v = bank(3)[:, 0:GC * starts[p].shape[1]].rearrange("p (k c) -> p k c", k=GC)
                        tt(z, row_b[:, r, :, D:D + heads], er_v[:, :, er0:er0 + heads], ALU.add).then_inc(prod_done.sem, 1)

                def logits(q, r):
                    dve.wait_ge(prod_done.sem, prod_done.at(p, q, r))
                    if past(q, r, 2):
                        dve.wait_ge(logit_t_done.sem, logit_t_done.at(p, q, r, 2))
                    if past(q, r, 2):
                        dve.wait_ge(dif_done.sem, dif_done.at(p, q, r, 2))
                    l = logit[:, r % 2, 0:GC * heads]
                    if p == "attn":
                        v.reduce_sum(l, prod[:, :, :].rearrange("p k (h c) -> p (k h) c", h=heads), axis=AX_X)\
                            .then_inc(logit_done.sem, 1)
                    else:
                        z = z_b[:, :, 0:heads]
                        stt(l.rearrange("p (k h) -> p k h", k=GC), z, 0.2, z, ALU.mult, ALU.max)\
                            .then_inc(logit_done.sem, 1)

                def maxima(q, r):
                    s = r % 2
                    dve.wait_ge(logit_t_done.sem, logit_t_done.at(p, q, r))
                    dve.wait_ge(brk_in.of(r), brk_in.at(p, q, r))
                    if past(q, r, 1):
                        dve.wait_ge(fwd_done.sem, fwd_done.at(p, q, r, 1))
                    if past(q, r, 1):
                        dve.wait_ge(max_done.sem, max_done.at(p, q, r, 1))
                    b = brk_b[0:heads, r, :]
                    v.tensor_tensor_scan(fwd[0:heads, s, :], b[:, 0:GC * P], bank(2)[0:heads, ::-1],
                                         fwd[0:heads, 1 - s, GC * P - 1:GC * P], ALU.add, ALU.max)\
                        .then_inc(fwd_done.sem, 1)
                    dve.wait_ge(fwd_done.sem, fwd_done.at(p, q, r))
                    if past(q, r, 2):
                        dve.wait_ge(max_t_done.sem, max_t_done.at(p, q, r, 2))
                    if past(q, r, 2):
                        dve.wait_ge(kept_done.sem, kept_done.at(p, q, r, 2))
                    v.tensor_tensor_scan(mx[0:heads, s, :], b[:, GC * P:0:-1], fwd[0:heads, s, ::-1],
                                         -BIG, ALU.add, ALU.max).then_inc(max_done.sem, 1)

                def difs(q, r):
                    dve.wait_ge(max_t_done.sem, max_t_done.at(p, q, r))
                    if past(q, r, 2):
                        dve.wait_ge(exp_done.sem, exp_done.at(p, q, r, 2))
                    n = GC * heads
                    tt(dif[:, r % 2, 0:n], logit[:, r % 2, 0:n], max_ps(p)[:, 0:n], ALU.subtract).then_inc(dif_done.sem, 1)

                def messages(q, r):
                    dve.wait_ge(exp_done.sem, exp_done.at(p, q, r))
                    if past(q, r, 2):
                        dve.wait_ge(sum_done.sem, sum_done.at(p, q, r, 2))
                    s = r % 2
                    m = msg[:, s, 0:GC * W].rearrange("p (k h c) -> p k h c", k=GC, h=heads)
                    e = wgt[:, s, 0:GC * heads].rearrange("p (k h c) -> p k h c", k=GC, h=heads)
                    v.tensor_copy(m[:, :, :, nc_:nc_ + 1], e)
                    if p == "attn":
                        i = tt(m[:, :, :, 0:nc_], row_b[:, r, :, D:2 * D].rearrange("p k (h c) -> p k h c", h=heads),
                               bc(e, [P, GC, heads, nc_]), ALU.mult)
                    else:
                        i = tt(m[:, :, :, 0:nc_],
                               bc(row_b[:, r, :, 0:D].rearrange("p k (h c) -> p k h c", h=1), [P, GC, heads, D]),
                               bc(e, [P, GC, heads, nc_]), ALU.mult)
                    i.then_inc(msg_done.sem, 1)

                if p == "gcn":
                    over_groups(dve, [(0, diags), (1, same)])
                elif weighted:
                    if p == "attn":
                        over_groups(dve, [(3, maxima), (2, terms), (3, difs), (2, logits), (3, messages)])
                    else:
                        over_groups(dve, [(4, messages), (3, maxima), (2, terms), (2, logits), (3, difs)])

                c = chains["x_" + p]
                if weighted:
                    for h in range(heads):
                        dve.wait_ge(s_steps, c.at(f"d{h}"))
                        for t in range(QA):
                            i = ts(gw[:, t, t * CQ:], ps[0:CQ, BANK + t * CQ:BANK + CH], last_c[:, t, h:h + 1], 0.0,
                                   ALU.subtract, ALU.max)
                        i.then_inc(s_steps, 1)
                        dve.wait_ge(s_steps, c.at(f"g{h}"))
                        for t in range(QA):
                            i = tt(gw[:, t, t * CQ:], gw[:, t, t * CQ:], carries[:, t, t * CQ:], ALU.mult)
                        i.then_inc(s_steps, 1)

            edge_pass("gcn")
            c = chains["n_gcn"]
            av = agg_of("gcn")
            with dve.Fori(0, NJ) as j:
                dve.wait_ge(s_steps, c.at("an", j))
                tt(a_n[:, :, 0:D], tiles(av, j), nb(cols(norm[:, 1, :], j)), ALU.mult).then_inc(s_steps, 1)
                lin = ps[:, 8 * P:13 * P].rearrange("p (k c) -> p k c", k=JT)
                dve.wait_ge(s_steps, c.at("y", j))
                tt(Y, lin, fb(rows["L0_gnn_b"][:, :]), ALU.add).then_inc(s_steps, 1)
                norm_steps(c, j, "a")
                dve.wait_ge(s_steps, c.at("an2", j))
                tt(Y, Y, nb(st[:, 3, :]), ALU.mult).then_inc(s_steps, 1)
                dve.wait_ge(s_steps, c.at("ag", j))
                tt(Y, Y, fb(rows["L0_gnn_gamma"][:, :]), ALU.mult).then_inc(s_steps, 1)
                dve.wait_ge(s_steps, c.at("ab", j))
                tt(Y, Y, fb(rows["L0_gnn_beta"][:, :]), ALU.add).then_inc(s_steps, 1)
                dve.wait_ge(s_steps, c.at("ar", j))
                stt(Y, Y, 0.0, tiles(h_sb, j), ALU.max, ALU.add).then_inc(s_steps, 1)
                add_to_x(c, j, "ax")
                norm_steps(c, j, "b")
                relu_norm(c, j)
                q_v = ps[:, 2 * BANK:(2 + JT) * BANK].rearrange("p (k c) -> p k c", k=JT)[:, :, 0:3 * D]
                dve.wait_ge(s_steps, c.at("tab", j))
                tt(tab[:, :, :], q_v, fb(b_qkv[:, :], 3 * D), ALU.add).then_inc(s_steps, 1)

            def weights_of(c, j, p):
                heads, nc_, _ = WEIGHTED[p]
                av = agg_of(p).rearrange("p t (h c) -> p t h c", h=heads)
                a = av[:, bass.ds(j * JT, JT), :, :]
                r0 = rec[:, 0, 0:JT * heads].rearrange("p (k h c) -> p k h c", k=JT, h=heads)
                r1 = rec[:, 1, 0:JT * heads].rearrange("p (k h c) -> p k h c", k=JT, h=heads)
                dve.wait_ge(s_steps, c.at("den", j))
                ts(r0, a[:, :, :, nc_:nc_ + 1], 0.5, None, ALU.max).then_inc(s_steps, 1)
                dve.wait_ge(s_steps, c.at("rec", j))
                v.reciprocal(rec[:, 1, 0:JT * heads], rec[:, 0, 0:JT * heads]).then_inc(s_steps, 1)
                o = a_n[:, :, 0:heads * nc_].rearrange("p k (h c) -> p k h c", h=heads)
                dve.wait_ge(s_steps, c.at("an", j))
                tt(o, a[:, :, :, 0:nc_], bc(r1, [P, JT, heads, nc_]), ALU.mult).then_inc(s_steps, 1)

            def affine(c, j, pre, gamma, beta):
                dve.wait_ge(s_steps, c.at(pre + "n2", j))
                tt(Y, Y, nb(st[:, 3, :]), ALU.mult).then_inc(s_steps, 1)
                dve.wait_ge(s_steps, c.at(pre + "g", j))
                tt(Y, Y, fb(rows[gamma][:, :]), ALU.mult).then_inc(s_steps, 1)
                dve.wait_ge(s_steps, c.at(pre + "b", j))
                tt(Y, Y, fb(rows[beta][:, :]), ALU.add).then_inc(s_steps, 1)

            edge_pass("attn")
            c = chains["n_attn"]
            with dve.Fori(0, NJ) as j:
                weights_of(c, j, "attn")
                dve.wait_ge(s_steps, c.at("y", j))
                tt(Y, lin, a_n[:, :, 0:D], ALU.add).then_inc(s_steps, 1)
                dve.wait_ge(s_steps, c.at("y2", j))
                tt(Y, Y, fb(rows["L1_gnn_bskip"][:, :]), ALU.add).then_inc(s_steps, 1)
                dve.wait_ge(s_steps, c.at("y3", j))
                tt(Y, Y, hs[:, :, :], ALU.add).then_inc(s_steps, 1)
                norm_steps(c, j, "a")
                affine(c, j, "a", "L1_gnn_g1", "L1_gnn_b1")
                ffn = ps[:, 0:JT * P].rearrange("p (k c) -> p k c", k=JT)
                dve.wait_ge(s_steps, c.at("z", j))
                tt(Y, Y, ffn, ALU.add).then_inc(s_steps, 1)
                dve.wait_ge(s_steps, c.at("z2", j))
                tt(Y, Y, fb(rows["L1_gnn_bf2"][:, :]), ALU.add).then_inc(s_steps, 1)
                norm_steps(c, j, "b")
                affine(c, j, "b", "L1_gnn_g2", "L1_gnn_b2")
                add_to_x(c, j, "bx")
                norm_steps(c, j, "c")
                relu_norm(c, j)
                el_v = bank(2)[:, 0:JT * 2 * H2].rearrange("p (k l h) -> p k l h", k=JT, l=2)
                dve.wait_ge(s_steps, c.at("el_s", j))
                v.tensor_copy(tab[:, :, D:D + H2], el_v[:, :, 0, :]).then_inc(s_steps, 1)
                dve.wait_ge(s_steps, c.at("er_s", j))
                apart(dve, s_apart_dve)
                v.tensor_copy(tiles(er_all["gat1"], j), el_v[:, :, 1, :]).then_inc(s_steps, 1)

            edge_pass("gat1")
            c = chains["n_gat1"]
            wide = ps[:, 0:JT * BANK].rearrange("p (k c) -> p k c", k=JT)
            with dve.Fori(0, NJ) as j:
                weights_of(c, j, "gat1")
                W3 = H2 * D
                dve.wait_ge(s_steps, c.at("z", j))
                tt(tab[:, :, 0:W3], wide[:, :, 0:W3], fb(bias1[:, :], W3), ALU.add).then_inc(s_steps, 1)
                dve.wait_ge(s_steps, c.at("min", j))
                ts(a_n[:, :, :], tab[:, :, 0:W3], 0.0, None, ALU.min).then_inc(s_steps, 1)
                dve.wait_ge(s_steps, c.at("elu", j))
                stt(a_n[:, :, :], tab[:, :, 0:W3], 0.0, a_n[:, :, :], ALU.max, ALU.add).then_inc(s_steps, 1)
                dve.wait_ge(s_steps, c.at("elu2", j))
                ts(a_n[:, :, :], a_n[:, :, :], -1.0, None, ALU.add).then_inc(s_steps, 1)
                dve.wait_ge(s_steps, c.at("tab", j))
                v.tensor_copy(tab[:, :, 0:D + 1], wide[:, :, 0:D + 1]).then_inc(s_steps, 1)

            edge_pass("gat2")
            c = chains["n_gat2"]
            with dve.Fori(0, NJ) as j:
                weights_of(c, j, "gat2")
                dve.wait_ge(s_steps, c.at("y", j))
                tt(Y, a_n[:, :, 0:D], tiles(h_sb, j), ALU.add).then_inc(s_steps, 1)
                dve.wait_ge(s_steps, c.at("y2", j))
                tt(Y, Y, fb(rows["L2_gnn_bias2"][:, :]), ALU.add).then_inc(s_steps, 1)
                add_to_x(c, j, "yx")
                norm_steps(c, j, "a")
                relu_norm(c, j)
                split_dve(c, j)

            for i, p in enumerate(("sage1", "sage2")):
                edge_pass(p)
                c = chains["n_" + p]
                av = agg_of(p)
                sage = ps[:, 4 * BANK:4 * BANK + JT * P].rearrange("p (k c) -> p k c", k=JT)
                with dve.Fori(0, NJ) as j:
                    dve.wait_ge(s_steps, c.at("an", j))
                    tt(a_n[:, :, 0:D], tiles(av, j), nb(cols(cnt_r[:, :], j)), ALU.mult).then_inc(s_steps, 1)
                    dve.wait_ge(s_steps, c.at("ya", j))
                    tt(Y, sage, fb(bn_a[:, i, :]), ALU.mult).then_inc(s_steps, 1)
                    dve.wait_ge(s_steps, c.at("yb", j))
                    tt(Y, Y, fb(bn_b[:, i, :]), ALU.add).then_inc(s_steps, 1)
                    if p == "sage1":
                        dve.wait_ge(s_steps, c.at("hs", j))
                        ts(hs[:, :, :], Y, 0.0, None, ALU.max).then_inc(s_steps, 1)
                        split_dve(c, j)
                    else:
                        dve.wait_ge(s_steps, c.at("yx", j))
                        tt(tiles(x_sb, j), Y, tiles(x_sb, j), ALU.add).then_inc(s_steps, 1)


_INS = ["x", "src", "dst", "edge_attr_64", "L0_gnn_W", "L0_gnn_b", "L0_gnn_gamma", "L0_gnn_beta", "L1_gnn_Wq",
        "L1_gnn_bq", "L1_gnn_Wk", "L1_gnn_bk", "L1_gnn_Wv", "L1_gnn_bv", "L1_gnn_We", "L1_gnn_Wskip",
        "L1_gnn_bskip", "L1_gnn_g1", "L1_gnn_b1", "L1_gnn_g2", "L1_gnn_b2", "L1_gnn_Wf1", "L1_gnn_bf1",
        "L1_gnn_Wf2", "L1_gnn_bf2", "L2_gnn_fc1_w", "L2_gnn_attn_l1", "L2_gnn_attn_r1", "L2_gnn_res1_w",
        "L2_gnn_bias1", "L2_gnn_fc2_w", "L2_gnn_attn_l2", "L2_gnn_attn_r2", "L2_gnn_res2_w", "L2_gnn_bias2",
        "L3_gnn_Wl0", "L3_gnn_Wr0", "L3_gnn_b0", "L3_gnn_g0", "L3_gnn_be0", "L3_gnn_rm0", "L3_gnn_rv0",
        "L3_gnn_Wl1", "L3_gnn_Wr1", "L3_gnn_b1", "L3_gnn_g1", "L3_gnn_be1", "L3_gnn_rm1", "L3_gnn_rv1"]


def kernel(**inputs):
    import numpy as _np
    import concourse.bacc as _bacc
    from concourse.bass_utils import run_bass_kernel_spmd as _run

    nc = _bacc.Bacc("TRN2", target_bir_lowering=False, num_devices=1)
    arrays, args = {}, {}
    for name in _INS:
        a = _np.ascontiguousarray(inputs[name])
        arrays[f"in_{name}"] = a
        args[name] = nc.dram_tensor(f"in_{name}", a.shape, mybir.dt.from_np(a.dtype), kind="ExternalInput").ap()
    out = nc.dram_tensor("out_x", (N, D), F32, kind="ExternalOutput").ap()
    gnn_stack_kernel(nc, out, **args)
    return _run(nc, [arrays], core_ids=[0]).results[0]["out_x"]
```
